# Optimizing a Trainium2 kernel written in Bass

```python
import numpy as np
import jax
import jax.numpy as jnp

def _softmax(x, axis=-1):
    return jax.nn.softmax(x, axis=axis)

def _gelu(x):
    return jax.nn.gelu(x, approximate=True)

def _silu(x):
    return jax.nn.silu(x)

def _sigmoid(x):
    return jax.nn.sigmoid(x)

def _layernorm(x, axis=-1, eps=1e-05):
    m = jnp.mean(x, axis=axis, keepdims=True)
    v = jnp.var(x, axis=axis, keepdims=True)
    return (x - m) / jnp.sqrt(v + eps)

def _scatter_add(tgt, idx, src, axis=0):
    return tgt.at[idx].add(src)

def _segment_sum(src, seg, n):
    return jax.ops.segment_sum(src, seg, n)
kernel_name = 'mk_lm_tower_d1_tok_ids768_r4_4f48ef'

def setup_inputs(seed: int=0):
    np.random.seed(seed)
    _w = jnp.asarray

    def _rec_inputs():
        import jax
        import jax.numpy as jnp
        _rk = jax.random.key(seed)
        x = jax.random.randint(jax.random.fold_in(_rk, 1), (8, 512), 0, 25426, jnp.int32)
        fside_BS_values = jax.random.uniform(jax.random.fold_in(_rk, 21), (8, 512), jnp.float32, 0.0, 0.999927)
        return (x, fside_BS_values)
    x, fside_BS_values = _rec_inputs()

    def _L0_tok_setup():
        import jax, jax.numpy as jnp
        import numpy as np
        V, H, S, B = (25426, 192, 512, 8)
        DK = 64
        NUM_K = 4

        def _ln(x, g, b, eps):
            m = jnp.mean(x, axis=-1, keepdims=True)
            v = jnp.mean(jnp.square(x - m), axis=-1, keepdims=True)
            return (x - m) * jax.lax.rsqrt(v + eps) * g + b

        def _qgelu(x):
            return x * jax.nn.sigmoid(1.702 * x)
        key = jax.random.key(seed)
        ks = list(jax.random.split(key, 32))

        def nrm(k, shape, scale=0.02):
            return jax.random.normal(k, shape, dtype=jnp.float32) * scale
        inp = {}
        inp['input_ids'] = jax.random.randint(ks[0], (B, S), 0, V, dtype=jnp.int32)
        inp['values'] = jax.random.uniform(ks[1], (B, S), dtype=jnp.float32)
        inp['word_emb'] = nrm(ks[2], (V, H))
        inp['tok_type_emb'] = nrm(ks[3], (2, H))
        inp['pos_emb'] = nrm(ks[4], (S, H))
        names = ['promoter', 'co_exp', 'gene_family', 'peca_grn']
        for i, n in enumerate(names):
            inp[n + '_k'] = nrm(ks[5 + 3 * i], (V, DK), 1.0)
            inp[n + '_W'] = nrm(ks[6 + 3 * i], (DK, H))
            inp[n + '_b'] = jnp.zeros((H,), jnp.float32)
        cat_in = H * (1 + NUM_K) + 1
        inp['cat_fc_W'] = nrm(ks[20], (cat_in, H))
        inp['cat_fc_b'] = jnp.zeros((H,), jnp.float32)
        inp['cat_ln_g'] = jnp.ones((H,), jnp.float32)
        inp['cat_ln_b'] = jnp.zeros((H,), jnp.float32)
        inp['cat_proj_W'] = nrm(ks[21], (H, H))
        inp['cat_proj_b'] = jnp.zeros((H,), jnp.float32)
        inp['ln_g'] = jnp.ones((H,), jnp.float32)
        inp['ln_b'] = jnp.zeros((H,), jnp.float32)
        inp['homologous_index'] = jax.random.permutation(ks[22], jnp.arange(V, dtype=jnp.int32))
        return inp
    _L0_tok_all = _L0_tok_setup()
    _L0_tok_in = {k: v for k, v in _L0_tok_all.items() if k in ('word_emb', 'tok_type_emb', 'pos_emb', 'promoter_k', 'promoter_W', 'promoter_b', 'co_exp_k', 'co_exp_W', 'co_exp_b', 'gene_family_k', 'gene_family_W', 'gene_family_b', 'peca_grn_k', 'peca_grn_W', 'peca_grn_b', 'cat_fc_W', 'cat_fc_b', 'cat_ln_g', 'cat_ln_b', 'cat_proj_W', 'cat_proj_b', 'ln_g', 'ln_b', 'homologous_index')}
    del _L0_tok_all

    def _L0_attn_setup():
        import jax, jax.numpy as jnp
        import numpy as np
        ALPHA = 0.35

        def _round_ln_pow2(x):
            y = jnp.floor(jnp.log2(x))
            up = x - 2.0 ** y > 2.0 ** (y + 1.0) - x
            return 2.0 ** (y + up.astype(x.dtype))
        key = jax.random.key(seed)
        k1, k2, k3, k4, k5 = jax.random.split(key, 5)
        B, N, C = (64, 197, 192)
        return {'x': jax.random.normal(k1, (B, N, C), dtype=jnp.float32), 'qkv_weight': jax.random.normal(k2, (3 * C, C), dtype=jnp.float32) * 0.02, 'qkv_bias': jax.random.normal(k3, (3 * C,), dtype=jnp.float32) * 0.02, 'proj_weight': jax.random.normal(k4, (C, C), dtype=jnp.float32) * 0.02, 'proj_bias': jax.random.normal(k5, (C,), dtype=jnp.float32) * 0.02}
    _L0_attn_all = _L0_attn_setup()
    _L0_attn_in = {k: v for k, v in _L0_attn_all.items() if k in ('qkv_weight', 'qkv_bias', 'proj_weight', 'proj_bias')}
    del _L0_attn_all

    def _L0_ffn_setup():
        import jax, jax.numpy as jnp
        import numpy as np
        D_MODEL, D_FF, N_EXPERTS, TOP_K = (192, 768, 8, 2)
        B, S = (2, 256)
        LN_EPS = 1e-05

        def _layernorm(x, gamma, beta):
            mu = jnp.mean(x, axis=-1, keepdims=True)
            var = jnp.mean(jnp.square(x - mu), axis=-1, keepdims=True)
            return (x - mu) * jax.lax.rsqrt(var + LN_EPS) * gamma + beta
        key = jax.random.key(seed)
        k1, k2, k3, k4 = jax.random.split(key, 4)
        return {'hidden_states': jax.random.normal(k1, (B, S, D_MODEL), dtype=jnp.float32), 'ln_gamma': jnp.ones((D_MODEL,), dtype=jnp.float32), 'ln_beta': jnp.zeros((D_MODEL,), dtype=jnp.float32), 'router_w': jax.random.normal(k2, (D_MODEL, N_EXPERTS), dtype=jnp.float32) * 0.02, 'w1': jax.random.normal(k3, (N_EXPERTS, D_MODEL, D_FF), dtype=jnp.float32) * 0.02, 'w2': jax.random.normal(k4, (N_EXPERTS, D_FF, D_MODEL), dtype=jnp.float32) * 0.02}
    _L0_ffn_all = _L0_ffn_setup()
    _L0_ffn_in = {k: v for k, v in _L0_ffn_all.items() if k in ('ln_gamma', 'ln_beta', 'router_w', 'w1', 'w2')}
    del _L0_ffn_all
    return {'x': x, 'fside_BS_values': fside_BS_values, 'L0_tok_word_emb': _L0_tok_in['word_emb'], 'L0_tok_tok_type_emb': _L0_tok_in['tok_type_emb'], 'L0_tok_pos_emb': _L0_tok_in['pos_emb'], 'L0_tok_promoter_k': _L0_tok_in['promoter_k'], 'L0_tok_promoter_W': _L0_tok_in['promoter_W'], 'L0_tok_promoter_b': _L0_tok_in['promoter_b'], 'L0_tok_co_exp_k': _L0_tok_in['co_exp_k'], 'L0_tok_co_exp_W': _L0_tok_in['co_exp_W'], 'L0_tok_co_exp_b': _L0_tok_in['co_exp_b'], 'L0_tok_gene_family_k': _L0_tok_in['gene_family_k'], 'L0_tok_gene_family_W': _L0_tok_in['gene_family_W'], 'L0_tok_gene_family_b': _L0_tok_in['gene_family_b'], 'L0_tok_peca_grn_k': _L0_tok_in['peca_grn_k'], 'L0_tok_peca_grn_W': _L0_tok_in['peca_grn_W'], 'L0_tok_peca_grn_b': _L0_tok_in['peca_grn_b'], 'L0_tok_cat_fc_W': _L0_tok_in['cat_fc_W'], 'L0_tok_cat_fc_b': _L0_tok_in['cat_fc_b'], 'L0_tok_cat_ln_g': _L0_tok_in['cat_ln_g'], 'L0_tok_cat_ln_b': _L0_tok_in['cat_ln_b'], 'L0_tok_cat_proj_W': _L0_tok_in['cat_proj_W'], 'L0_tok_cat_proj_b': _L0_tok_in['cat_proj_b'], 'L0_tok_ln_g': _L0_tok_in['ln_g'], 'L0_tok_ln_b': _L0_tok_in['ln_b'], 'L0_tok_homologous_index': _L0_tok_in['homologous_index'], 'L0_attn_qkv_weight': _L0_attn_in['qkv_weight'], 'L0_attn_qkv_bias': _L0_attn_in['qkv_bias'], 'L0_attn_proj_weight': _L0_attn_in['proj_weight'], 'L0_attn_proj_bias': _L0_attn_in['proj_bias'], 'L0_ffn_ln_gamma': _L0_ffn_in['ln_gamma'], 'L0_ffn_ln_beta': _L0_ffn_in['ln_beta'], 'L0_ffn_router_w': _L0_ffn_in['router_w'], 'L0_ffn_w1': _L0_ffn_in['w1'], 'L0_ffn_w2': _L0_ffn_in['w2']}

def reference(x, fside_BS_values, L0_tok_word_emb, L0_tok_tok_type_emb, L0_tok_pos_emb, L0_tok_promoter_k, L0_tok_promoter_W, L0_tok_promoter_b, L0_tok_co_exp_k, L0_tok_co_exp_W, L0_tok_co_exp_b, L0_tok_gene_family_k, L0_tok_gene_family_W, L0_tok_gene_family_b, L0_tok_peca_grn_k, L0_tok_peca_grn_W, L0_tok_peca_grn_b, L0_tok_cat_fc_W, L0_tok_cat_fc_b, L0_tok_cat_ln_g, L0_tok_cat_ln_b, L0_tok_cat_proj_W, L0_tok_cat_proj_b, L0_tok_ln_g, L0_tok_ln_b, L0_tok_homologous_index, L0_attn_qkv_weight, L0_attn_qkv_bias, L0_attn_proj_weight, L0_attn_proj_bias, L0_ffn_ln_gamma, L0_ffn_ln_beta, L0_ffn_router_w, L0_ffn_w1, L0_ffn_w2):
    import jax
    import jax.numpy as jnp

    def _L0_tok_ref(input_ids, values, word_emb, tok_type_emb, pos_emb, promoter_k, promoter_W, promoter_b, co_exp_k, co_exp_W, co_exp_b, gene_family_k, gene_family_W, gene_family_b, peca_grn_k, peca_grn_W, peca_grn_b, cat_fc_W, cat_fc_b, cat_ln_g, cat_ln_b, cat_proj_W, cat_proj_b, ln_g, ln_b, homologous_index):
        import jax, jax.numpy as jnp
        import numpy as np
        V, H, S, B = (25426, 192, 512, 8)
        DK = 64
        NUM_K = 4

        def _ln(x, g, b, eps):
            m = jnp.mean(x, axis=-1, keepdims=True)
            v = jnp.mean(jnp.square(x - m), axis=-1, keepdims=True)
            return (x - m) * jax.lax.rsqrt(v + eps) * g + b

        def _qgelu(x):
            return x * jax.nn.sigmoid(1.702 * x)
        emb_warmup_alpha = 1.0
        seq_len = input_ids.shape[1]
        we = word_emb[input_ids]
        v = values[..., None].astype(jnp.float32)
        ids_shifted = homologous_index[input_ids]
        parts = [we, v]
        for tab, W, b in ((promoter_k, promoter_W, promoter_b), (co_exp_k, co_exp_W, co_exp_b), (gene_family_k, gene_family_W, gene_family_b), (peca_grn_k, peca_grn_W, peca_grn_b)):
            e = jnp.einsum('bsd,dh->bsh', tab[ids_shifted], W) + b
            parts.append(emb_warmup_alpha * e)
        x = jnp.concatenate(parts, axis=-1)
        h = jnp.einsum('bsc,ch->bsh', x, cat_fc_W) + cat_fc_b
        h = _ln(h, cat_ln_g, cat_ln_b, 1e-05)
        h = _qgelu(h)
        h = jnp.einsum('bsh,hk->bsk', h, cat_proj_W) + cat_proj_b
        emb = h + tok_type_emb[0] + pos_emb[:seq_len]
        emb = _ln(emb, ln_g, ln_b, 1e-12)
        return emb

    def _L0_attn_ref(x, qkv_weight, qkv_bias, proj_weight, proj_bias):
        import jax, jax.numpy as jnp
        import numpy as np
        ALPHA = 0.35

        def _round_ln_pow2(x):
            y = jnp.floor(jnp.log2(x))
            up = x - 2.0 ** y > 2.0 ** (y + 1.0) - x
            return 2.0 ** (y + up.astype(x.dtype))
        B, N, C = x.shape
        num_heads = 12
        head_dim = C // num_heads
        scale = head_dim ** (-0.5)
        global_max_x = jnp.abs(x).max(axis=(0, 1))
        max_weight = jnp.abs(qkv_weight).max(axis=0)
        channel_scale = _round_ln_pow2(global_max_x ** ALPHA / max_weight ** (1.0 - ALPHA))
        x_smoothed = x / channel_scale[None, None, :]
        weight_smoothed = qkv_weight * channel_scale[None, :]
        h = jnp.einsum('bnc,mc->bnm', x_smoothed, weight_smoothed) + qkv_bias
        qkv = h.reshape(B, N, 3, num_heads, head_dim).transpose(2, 0, 3, 1, 4)
        q, k, v = (qkv[0], qkv[1], qkv[2])
        attn = jnp.einsum('bhnd,bhmd->bhnm', q, k) * scale
        attn = jax.nn.softmax(attn, axis=-1)
        out = jnp.einsum('bhnm,bhmd->bhnd', attn, v)
        out = out.transpose(0, 2, 1, 3).reshape(B, N, C)
        out = jnp.einsum('bnc,mc->bnm', out, proj_weight) + proj_bias
        return out

    def _L0_ffn_ref(hidden_states, ln_gamma, ln_beta, router_w, w1, w2):
        import jax, jax.numpy as jnp
        import numpy as np
        D_MODEL, D_FF, N_EXPERTS, TOP_K = (192, 768, 8, 2)
        B, S = (2, 256)
        LN_EPS = 1e-05

        def _layernorm(x, gamma, beta):
            mu = jnp.mean(x, axis=-1, keepdims=True)
            var = jnp.mean(jnp.square(x - mu), axis=-1, keepdims=True)
            return (x - mu) * jax.lax.rsqrt(var + LN_EPS) * gamma + beta
        Bz, Sz, D = hidden_states.shape
        residual = hidden_states
        x = _layernorm(hidden_states, ln_gamma, ln_beta)
        tokens = x.reshape(-1, D)
        T = tokens.shape[0]
        logits = tokens @ router_w
        probs = jax.nn.softmax(logits, axis=-1)
        topw, topi = jax.lax.top_k(probs, TOP_K)
        topw = topw / jnp.sum(topw, axis=-1, keepdims=True)
        gates = jnp.zeros((T, N_EXPERTS), dtype=tokens.dtype)
        gates = gates.at[jnp.arange(T)[:, None], topi].set(topw)
        h = jnp.einsum('td,edf->etf', tokens, w1)
        h = jax.nn.silu(h)
        y = jnp.einsum('etf,efd->etd', h, w2)
        out = jnp.einsum('te,etd->td', gates, y)
        return residual + out.reshape(Bz, Sz, D)
    h = _L0_tok_ref(x, fside_BS_values, L0_tok_word_emb, L0_tok_tok_type_emb, L0_tok_pos_emb, L0_tok_promoter_k, L0_tok_promoter_W, L0_tok_promoter_b, L0_tok_co_exp_k, L0_tok_co_exp_W, L0_tok_co_exp_b, L0_tok_gene_family_k, L0_tok_gene_family_W, L0_tok_gene_family_b, L0_tok_peca_grn_k, L0_tok_peca_grn_W, L0_tok_peca_grn_b, L0_tok_cat_fc_W, L0_tok_cat_fc_b, L0_tok_cat_ln_g, L0_tok_cat_ln_b, L0_tok_cat_proj_W, L0_tok_cat_proj_b, L0_tok_ln_g, L0_tok_ln_b, L0_tok_homologous_index)
    h = h + _L0_attn_ref(_layernorm(h, axis=-1), L0_attn_qkv_weight, L0_attn_qkv_bias, L0_attn_proj_weight, L0_attn_proj_bias)
    h = h + _L0_ffn_ref(_layernorm(h, axis=-1), L0_ffn_ln_gamma, L0_ffn_ln_beta, L0_ffn_router_w, L0_ffn_w1, L0_ffn_w2)
    return h

_drawn_inputs = setup_inputs


def setup_inputs(seed=0):
    import zlib

    import numpy as np

    out = dict(_drawn_inputs(seed))
    spreads = {'L0_tok_promoter_b': (0.0, 0.1),
     'L0_tok_co_exp_b': (0.0, 0.1),
     'L0_tok_gene_family_b': (0.0, 0.1),
     'L0_tok_peca_grn_b': (0.0, 0.1),
     'L0_tok_cat_fc_b': (0.0, 0.1),
     'L0_tok_cat_ln_g': (1.0, 0.2),
     'L0_tok_cat_ln_b': (0.0, 0.1),
     'L0_tok_cat_proj_b': (0.0, 0.1),
     'L0_tok_ln_g': (1.0, 0.2),
     'L0_tok_ln_b': (0.0, 0.1),
     'L0_ffn_ln_gamma': (1.0, 0.6),
     'L0_ffn_ln_beta': (0.0, 2.0)}
    factors = {'L0_attn_qkv_bias': 8.0, 'L0_attn_proj_bias': 3.078}
    for name, (base, spread) in spreads.items():
        noise = np.random.default_rng([zlib.crc32(name.encode()), seed]).standard_normal(out[name].shape)
        drawn = base * np.exp(spread * noise) if base else spread * noise
        out[name] = jnp.asarray(drawn.astype(out[name].dtype))
    for name, factor in factors.items():
        out[name] = (out[name] * factor).astype(out[name].dtype)
    return out
```

```python
from contextlib import ExitStack

import concourse.bass as bass
from concourse import mybir

F32 = mybir.dt.float32
BF16 = mybir.dt.bfloat16
I32 = mybir.dt.int32
ALU = mybir.AluOpType
ACT = mybir.ActivationFunctionType
AX = mybir.AxisListType
ds = bass.ds

P = 128
NB, S = 8, 512
TPB = S // P
NT = NB * TPB
H = 192
HC = H // 2
DK, NTAB = 64, 4
NH, HD = 12, 16
HG = 4
NG = NH // HG
E, FF = 8, 768
FC = FF // P
FH = FF // 2
CAP = NB * S
DU = 8
DT = 2 * NB * S // P + E
QP = 6
QPARTS = (0, 0, 1, 0, 2, 1)
KPARTS = (0, 1, 0, 2, 0, 1)
QROWS = QP * HD
NEG = 2
ALPHA = 0.35
SCALE = HD ** -0.5

FUSED = ((64, 0, 1), (0, 1, 2), (64, 2, 2), (0, 3, 3))

C_ID, C_TRI, C_ONE, C_LOW, C_CAP, C_F, C_I, C_PAD, C_TOK = 0, 128, 256, 384, 448, 456, 528, 600, 601
C_PADTOK = C_TOK + NT
C_END = C_PADTOK + 1


def after(eng, sem, n):
    if not isinstance(n, int) or n > 0:
        eng.wait_ge(sem, n)


def pipeline(eng, count, unroll, lag, step):
    for k in range(unroll):
        step(0, k)
    with eng.Fori(1, count) as i:
        for k in range(unroll):
            step(i, k)
    for k in range(lag):
        step(count, k)


def build_program(nc, a, out_ext):
    ctx = ExitStack()
    with ctx:
        def sb(name, shape, dt=F32):
            return ctx.enter_context(nc.sbuf_tensor(name, shape, dt))

        def sem(name):
            return ctx.enter_context(nc.semaphore(name))

        qkd = nc.dram_tensor("qk_parts", [2, 3, P, 3, S], BF16, kind="Internal").ap()

        lists = nc.dram_tensor("expert_lists", [E * CAP + P, 2], F32, kind="Internal").ap()
        xrows = nc.dram_tensor("expert_input_rows", [NB * S + P, H], F32, kind="Internal").ap()

        const = sb("const", [P, C_END])
        ident = const[:, C_ID:C_ID + P]
        identb = sb("identb", [P, P], BF16)
        eps = sb("eps", [P, 2])
        lnp = sb("lnp", [P, 6, H])
        pos = sb("pos", [P, TPB, H])
        wfc = sb("wfc", [P, 4, H])
        wpj = sb("wpj", [HC + 2, 2, H])
        wqkv = sb("wqkv", [HC + 1, 2, 3 * H])
        wo = sb("wo", [P, NG, H])
        wr = sb("wr", [HC, 2, E])
        hall = sb("hall", [P, NT, H])
        xT = sb("xT", [P, NB, 2, S])
        big = sb("big", [P, E * (2 * FF + FC * H)])
        smalls = sb("smalls", [P, 64])

        at = 0

        def part(n):
            nonlocal at
            at += n
            return big[:, at - n:at]
        QS = part(2 * NH * S // 2).bitcast(BF16).rearrange("p (b h s) -> p b h s", b=2, h=NH)
        KS = part(2 * NH * S // 2).bitcast(BF16).rearrange("p (b h s) -> p b h s", b=2, h=NH)
        PT = part(2 * HG * S).rearrange("p (b h s) -> p b h s", b=2, h=HG)
        VV = part(2 * TPB * NH * 32).rearrange("p (b t h d) -> p b t h d", b=2, t=TPB, h=NH)
        xs = part(2 * 2 * S).rearrange("p (b k s) -> p b k s", b=2, k=2)
        at = NH * S
        G = part(4 * 512).rearrange("p (b n) -> p b n", b=4)
        GT = part(2 * 512).rearrange("p (b n) -> p b n", b=2)
        c1 = part(2 * H).rearrange("p (b n) -> p b n", b=2)
        u = part(2 * H).rearrange("p (b n) -> p b n", b=2)
        ex = part(2 * H).rearrange("p (b n) -> p b n", b=2)
        sg = part(2 * H).rearrange("p (b n) -> p b n", b=2)
        den = part(2 * H).rearrange("p (b n) -> p b n", b=2)
        q = part(2 * H).rearrange("p (b n) -> p b n", b=2)
        qT = part(2 * 2 * P).rearrange("p (b k n) -> p b k n", b=2, k=2)
        emb = part(2 * H).rearrange("p (b n) -> p b n", b=2)
        c2 = part(2 * H).rearrange("p (b n) -> p b n", b=2)
        xn = part(2 * H).rearrange("p (b n) -> p b n", b=2)
        wc = part(NTAB * 2 * H).rearrange("p (i k n) -> p i k n", i=NTAB, k=2)
        wkT = part(2 * NTAB * DK).rearrange("p (k i n) -> p k i n", k=2, i=NTAB)
        bk = part(2 * NTAB).rearrange("p (k i) -> p k i", k=2)
        fcb = part(H)
        ids = part(4).bitcast(I32)
        hid = part(4).bitcast(I32)
        assert at <= E * (2 * FF + FC * H)

        OT = sb("OT", [P, 2, NG, S])
        qk32 = sb("qk32", [P, 2, S])
        parts = sb("parts", [P, 2, 3, S], BF16)
        rest = sb("rest", [P, S])
        pvs = sb("pvs", [P, S])
        sums = sb("sums", [P, S])
        rsum = sb("rsum", [P, S])
        nmx = sb("nmx", [P, 2, TPB, HG])
        npt = sb("npt", [P, 2, TPB, 2 * HG], BF16)
        nmT = sb("nmT", [2 * HG, 2, S], BF16)
        gmx = sb("gmx", [HC, NB, 2])
        st = sb("st", [P, 3, 2, 6])
        mv = sb("mv", [P, 3, 2, 2])
        lnv = sb("lnv", [P, 3, 2])
        rstd = sb("rstd", [P, 3, 2])
        csm = sb("csm", [HC, 12, 2])
        
        ps = ctx.enter_context(nc.psum_tensor("ps", [P, 8, 512], F32))

        s_const, s_wmm, s_wvec, s_watt = sem("constants_in"), sem("fuse_weights_in"), sem("vectors_in"), sem("attention_weights_in")
        s_zero = sem("fills_done")
        s_fused, s_wfc = sem("fused_weights_done"), sem("fused_weights_ready")
        s_identb = sem("identity_bf16_ready")
        g_id = [sem(f"ids_in{k}") for k in range(4)]
        g_val = [sem(f"values_in{k}") for k in range(4)]
        g_hid = [sem(f"shifted_ids_in{k}") for k in range(4)]
        g_we = [sem(f"word_rows_in{k}") for k in range(4)]
        g_tab = [sem(f"table_rows_in{k}") for k in range(4)]
        t1_done, gt_ready, fc_done = sem("t1_done"), sem("gt_ready"), sem("fc_done")
        bn_done = [sem(f"bn{n}_done") for n in range(3)]
        mv_ready = [sem(f"mean_var{n}_ready") for n in range(3)]
        ln_log = [sem(f"log_var{n}_done") for n in range(3)]
        rs_ready = [sem(f"rstd{n}_ready") for n in range(3)]
        den_ready, sg_log, sg_ready = sem("den_ready"), sem("sigmoid_log_done"), sem("sigmoid_ready")
        c1_done, u_ready, e_ready, q_ready = sem("c1_done"), sem("u_ready"), sem("e_ready"), sem("q_ready")
        t2_done, qt_ready, pj_done = sem("t2_done"), sem("qt_ready"), sem("pj_done")
        emb_ready, c2_done, h_ready, x_ready = sem("emb_ready"), sem("c2_done"), sem("h_ready"), sem("x_ready")
        t3_done, xt_ready, gmx_ready = sem("t3_done"), sem("xt_ready"), sem("gmx_ready")
        cs_dve, cs_act, w_scaled = sem("scale_steps_vector"), sem("scale_steps_scalar"), sem("weights_scaled")

        def gate(e):
            e.nop(nofuse=True)

        def tile_of(i, k, lag):
            k, i = (k - lag) % 4, i + (k - lag) // 4
            if isinstance(i, int) and not 0 <= i < NB:
                return None
            return i, k, 4 * i + k

        def a_sync(e):
            e.dma_start(const[:, :], a["const"]).then_inc(s_const, 16)
            for n in range(NTAB):
                lo = H + 1 + n * H
                e.dma_start(wc[0:HC, n, :, :], a["fc_w"][lo:lo + H, :].rearrange("(k p) c -> p k c", k=2)).then_inc(s_wmm, 16)
            e.dma_start(wkT[0:HC, :, :, :], a["wkT"]).then_inc(s_wmm, 16)
            e.dma_start(bk[0:HC, :, :], a["bk"]).then_inc(s_wmm, 16)
            e.dma_start(fcb[64:65, :], a["fc_b"]).then_inc(s_wmm, 16)
            e.dma_start(wfc[:, 0, :], a["fc_w"][0:P, :]).then_inc(s_wmm, 16)
            e.dma_start(wfc[0:64, 1, :], a["fc_w"][P:H, :]).then_inc(s_wmm, 16)
            e.dma_start(wfc[65:66, 3, :], a["fc_w"][H:H + 1, :]).then_inc(s_wmm, 16)

            def step(i, k):
                t = tile_of(i, k, 0)
                i, k, s = t
                after(e, g_hid[k], 16 * i)
                gate(e)
                after(e, g_we[k], 16 * i)
                gate(e)
                e.dma_start(ids[:, k:k + 1], a["ids"][ds(s, 1)].rearrange("t p c -> (t p) c")).then_inc(g_id[k], 16)
                if isinstance(i, int) and i == 0 and k == 0:
                    e.wait_ge(s_zero, 1)
                after(e, t1_done, s - 3)
                gate(e)
                e.dma_start(G[:, k, 449:450], a["vals"][ds(s, 1)].rearrange("t p c -> (t p) c")).then_inc(g_val[k], 16)
            pipeline(e, NB, 4, 0, step)

        def a_pool(e):
            e.memset(G[:, :, :], 0.0).then_inc(s_id0, 1)
            e.wait_ge(s_id0, 1)
            e.memset(G[:, :, 448:449], 1.0).then_inc(s_zero, 1)
            e.wait_ge(s_zero, 1)
            e.memset(qT[96:98, :, 1, :], 1.0).then_inc(s_zero, 1)
            e.wait_ge(s_zero, 2)
            e.memset(eps[:, 0:1], 1e-5).then_inc(s_zero, 1)
            e.wait_ge(s_zero, 3)
            e.memset(eps[:, 1:2], 1e-12).then_inc(s_zero, 1)
            e.wait_ge(s_zero, 4)

            def step(i, k):
                t = tile_of(i, k, 0)
                if t is not None:
                    ti, tk, s = t
                    e.wait_ge(g_id[tk], 16 * (ti + 1))
                    after(e, g_tab[tk], 16 * ti)
                    gate(e)
                    e.indirect_dma_start(out=hid[:, tk:tk + 1], out_offset=None, in_=a["homo"],
                                         in_offset=bass.IndirectOffsetOnAxis(ap=ids[:, tk:tk + 1], axis=0)).then_inc(g_hid[tk], 16)
                    after(e, t1_done, s - 3)
                    gate(e)
                    e.indirect_dma_start(out=G[:, tk, 0:H], out_offset=None, in_=a["word"],
                                         in_offset=bass.IndirectOffsetOnAxis(ap=ids[:, tk:tk + 1], axis=0)).then_inc(g_we[tk], 16)
                t = tile_of(i, k, 1)
                if t is not None:
                    ti, tk, s = t
                    e.wait_ge(g_hid[tk], 16 * (ti + 1))
                    gate(e)
                    e.indirect_dma_start(out=G[:, tk, H:H + NTAB * DK], out_offset=None, in_=a["tabs"],
                                         in_offset=bass.IndirectOffsetOnAxis(ap=hid[:, tk:tk + 1], axis=0)).then_inc(g_tab[tk], 16)
            pipeline(e, NB, 4, 1, step)

        def a_pe(e):
            e.wait_ge(s_wmm, 160)
            for n, (lo, bank, _) in enumerate(FUSED):
                for kt in range(2):
                    m = e.matmul(ps[lo:lo + DK, bank, 0:H], wkT[0:HC, kt, n, :], wc[0:HC, n, kt, :],
                                 start=kt == 0, stop=kt == 1)
                m.then_inc(s_fused, 1)
            for n in range(NTAB):
                for kt in range(2):
                    m = e.matmul(ps[64:65, 4, 0:H], bk[0:HC, kt, n:n + 1], wc[0:HC, n, kt, :],
                                 start=n == 0 and kt == 0, stop=n == NTAB - 1 and kt == 1)
            m.then_inc(s_fused, 1)
            e.wait_ge(s_const, 16)
            e.wait_ge(s_wfc, 5)

            def step(i, k):
                if t := tile_of(i, k, 0):
                    ti, tk, s = t
                    e.wait_ge(g_we[tk], 16 * (ti + 1))
                    e.wait_ge(g_tab[tk], 16 * (ti + 1))
                    e.wait_ge(g_val[tk], 16 * (ti + 1))
                    after(e, gt_ready, s - 1)
                    for c in range(4):
                        m = e.transpose(ps[:, tk % 2, P * c:P * c + P], G[:, tk, P * c:P * c + P], ident)
                    m.then_inc(t1_done, 1)
                    e.wait_ge(gt_ready, s + 1)
                    after(e, c1_done, s - 1)
                    for c in range(4):
                        K = P if c < 3 else 66
                        m = e.matmul(ps[:, 2 + tk % 2, 0:H], GT[0:K, tk % 2, P * c:P * c + P], wfc[0:K, c, :],
                                     start=c == 0, stop=c == 3)
                    m.then_inc(fc_done, 1)
                if t := tile_of(i, k, 1):
                    ti, tk, s = t
                    if isinstance(ti, int) and ti == 0 and tk == 0:
                        e.wait_ge(s_wvec, 64)
                    e.wait_ge(q_ready, s + 1)
                    after(e, qt_ready, s)
                    for kt in range(2):
                        m = e.transpose(ps[0:HC, 4, P * kt:P * kt + P], q[:, tk % 2, HC * kt:HC * kt + HC], ident)
                    m.then_inc(t2_done, 1)
                    e.wait_ge(qt_ready, s + 1)
                    after(e, emb_ready, s - 1)
                    e.matmul(ps[:, 5 + tk % 2, 0:H], qT[0:HC, tk % 2, 0, :], wpj[0:HC, 0, :], start=True, stop=False)
                    e.matmul(ps[:, 5 + tk % 2, 0:H], qT[0:HC + 2, tk % 2, 1, :], wpj[0:HC + 2, 1, :],
                             start=False, stop=True).then_inc(pj_done, 1)
                if t := tile_of(i, k, 3):
                    ti, tk, s = t
                    e.wait_ge(x_ready, s + 1)
                    after(e, xt_ready, s)
                    for kt in range(2):
                        m = e.transpose(ps[0:HC, 7, P * kt:P * kt + P], xn[:, tk % 2, HC * kt:HC * kt + HC], ident)
                    m.then_inc(t3_done, 1)
            pipeline(e, NB, 4, 3, step)

        def rsqrt(e, n, p, s, ecol):
            e.wait_ge(mv_ready[n], s + 1)
            e.activation(lnv[:, n, p:p + 1], mv[:, n, p, 1:2], ACT.Ln, bias=eps[:, ecol:ecol + 1]).then_inc(ln_log[n], 1)
            e.wait_ge(ln_log[n], s + 1)
            e.activation(rstd[:, n, p:p + 1], lnv[:, n, p:p + 1], ACT.Exp, scale=-0.5).then_inc(rs_ready[n], 1)

        def a_act(e):
            e.preload_act_table_set("natural_log_exp_and_others")
            e.dma_start(lnp[:, :, :], a["lnp"]).then_inc(s_wvec, 16)
            e.dma_start(pos[:, :, :], a["pos"].rearrange("(t p) c -> p t c", p=P)).then_inc(s_wvec, 16)
            e.dma_start(wpj[0:HC, 0, :], a["pj"][0:HC, :]).then_inc(s_wvec, 16)
            e.dma_start(wpj[:, 1, :], a["pj"][HC:2 * HC + 2, :]).then_inc(s_wvec, 16)
            e.dma_start(wqkv[0:HC, 0, :], a["qkv"][0:HC, :]).then_inc(s_watt, 16)
            e.dma_start(wqkv[:, 1, :], a["qkv"][HC:2 * HC + 1, :]).then_inc(s_watt, 16)
            e.dma_start(wo[:, :, :], a["wo"]).then_inc(s_watt, 16)
            e.dma_start(wr[:, :, :], a["router"].rearrange("(k p) n -> p k n", k=2)).then_inc(s_watt, 16)
            e.wait_ge(s_fused, 5)
            for lo, bank, chunk in FUSED:
                e.activation(wfc[lo:lo + DK, chunk, :], ps[lo:lo + DK, bank, 0:H], ACT.Copy).then_inc(s_wfc, 1)
            e.wait_ge(s_const, 16)
            e.activation(identb[:, :], ident, ACT.Copy).then_inc(s_identb, 1)
            e.wait_ge(s_zero, 4)

            def step(i, k):
                if t := tile_of(i, k, 0):
                    ti, tk, s = t
                    e.wait_ge(t1_done, s + 1)
                    after(e, fc_done, s - 1)
                    e.activation(GT[:, tk % 2, :], ps[:, tk % 2, :], ACT.Copy).then_inc(gt_ready, 1)
                if t := tile_of(i, k, 1):
                    ti, tk, s = t
                    e.wait_ge(t2_done, s + 1)
                    after(e, pj_done, s - 1)
                    e.activation(qT[0:HC, tk % 2, :, :], ps[0:HC, 4, 0:2 * P].rearrange("p (k n) -> p k n", k=2), ACT.Copy).then_inc(qt_ready, 1)
                if t := tile_of(i, k, 3):
                    ti, tk, s = t
                    e.wait_ge(t3_done, s + 1)
                    e.activation(xT[0:HC, ds(ti, 1), :, P * tk:P * tk + P].rearrange("p b k n -> p (b k) n"),
                                 ps[0:HC, 7, 0:2 * P].rearrange("p (k n) -> p k n", k=2), ACT.Copy).then_inc(xt_ready, 1)
                if t := tile_of(i, k, 0):
                    rsqrt(e, 0, t[1] % 2, t[2], 0)
                if t := tile_of(i, k, 2):
                    rsqrt(e, 1, t[1] % 2, t[2], 1)
                if t := tile_of(i, k, 0):
                    ti, tk, s = t
                    e.wait_ge(u_ready, s + 1)
                    after(e, q_ready, s - 1)
                    e.activation(ex[:, tk % 2, :], u[:, tk % 2, :], ACT.Exp, scale=-1.702).then_inc(e_ready, 1)
                if t := tile_of(i, k, 0):
                    ti, tk, s = t
                    e.wait_ge(den_ready, s + 1)
                    e.activation(sg[:, tk % 2, :], den[:, tk % 2, :], ACT.Ln).then_inc(sg_log, 1)
                    e.wait_ge(sg_log, s + 1)
                    e.activation(ex[:, tk % 2, :], sg[:, tk % 2, :], ACT.Exp, scale=-1.0).then_inc(sg_ready, 1)
                if t := tile_of(i, k, 2):
                    rsqrt(e, 2, t[1] % 2, t[2], 0)
            pipeline(e, NB, 4, 3, step)

        def stats(e, n, p, s, x):
            gate(e)
            e.bn_stats(st[:, n, p, :], x).then_inc(bn_done[n], 1)
            e.wait_ge(bn_done[n], s + 1)
            after(e, rs_ready[n], s - 1)
            gate(e)
            e.bn_aggr(mv[:, n, p, :], st[:, n, p, :]).then_inc(mv_ready[n], 1)

        def a_dve(e):
            e.wait_ge(s_fused, 5)
            e.tensor_tensor(wfc[64:65, 3, :], ps[64:65, 4, 0:H], fcb[64:65, :], ALU.add).then_inc(s_wfc, 1)
            e.wait_ge(s_wvec, 64)

            def step(i, k):
                if t := tile_of(i, k, 0):
                    ti, tk, s = t
                    e.wait_ge(fc_done, s + 1)
                    stats(e, 0, tk % 2, s, ps[:, 2 + tk % 2, 0:H])
                if t := tile_of(i, k, 2):
                    ti, tk, s = t
                    e.wait_ge(pj_done, s + 1)
                    e.tensor_tensor(emb[:, tk % 2, :], ps[:, 5 + tk % 2, 0:H], pos[:, tk, :], ALU.add).then_inc(emb_ready, 1)
                    e.wait_ge(emb_ready, s + 1)
                    stats(e, 1, tk % 2, s, emb[:, tk % 2, :])
                if t := tile_of(i, k, 0):
                    ti, tk, s = t
                    p = tk % 2
                    e.wait_ge(mv_ready[0], s + 1)
                    e.scalar_tensor_tensor(c1[:, p, :], ps[:, 2 + p, 0:H], mv[:, 0, p, 0:1], lnp[:, 0, :],
                                           ALU.subtract, ALU.mult).then_inc(c1_done, 1)
                    e.wait_ge(c1_done, s + 1)
                    e.wait_ge(rs_ready[0], s + 1)
                    e.scalar_tensor_tensor(u[:, p, :], c1[:, p, :], rstd[:, 0, p:p + 1], lnp[:, 1, :],
                                           ALU.mult, ALU.add).then_inc(u_ready, 1)
                if t := tile_of(i, k, 2):
                    ti, tk, s = t
                    p = tk % 2
                    e.wait_ge(mv_ready[1], s + 1)
                    e.scalar_tensor_tensor(c2[:, p, :], emb[:, p, :], mv[:, 1, p, 0:1], lnp[:, 2, :],
                                           ALU.subtract, ALU.mult).then_inc(c2_done, 1)
                    e.wait_ge(c2_done, s + 1)
                    e.wait_ge(rs_ready[1], s + 1)
                    h = hall[:, ds(s, 1), :].rearrange("p a n -> p (a n)")
                    e.scalar_tensor_tensor(h, c2[:, p, :], rstd[:, 1, p:p + 1], lnp[:, 3, :],
                                           ALU.mult, ALU.add).then_inc(h_ready, 1)
                    e.wait_ge(h_ready, s + 1)
                    stats(e, 2, p, s, h)
                if t := tile_of(i, k, 0):
                    ti, tk, s = t
                    p = tk % 2
                    e.wait_ge(e_ready, s + 1)
                    e.tensor_scalar(den[:, p, :], ex[:, p, :], 1e18, 1.0, ALU.min, ALU.add).then_inc(den_ready, 1)
                if t := tile_of(i, k, 2):
                    ti, tk, s = t
                    p = tk % 2
                    e.wait_ge(mv_ready[2], s + 1)
                    e.wait_ge(rs_ready[2], s + 1)
                    after(e, t3_done, s - 1)
                    e.tensor_scalar(xn[:, p, :], hall[:, ds(s, 1), :].rearrange("p a n -> p (a n)"), mv[:, 2, p, 0:1],
                                    rstd[:, 2, p:p + 1], ALU.subtract, ALU.mult).then_inc(x_ready, 1)
                if t := tile_of(i, k, 0):
                    ti, tk, s = t
                    p = tk % 2
                    e.wait_ge(sg_ready, s + 1)
                    after(e, t2_done, s - 1)
                    e.tensor_tensor(q[:, p, :], u[:, p, :], ex[:, p, :], ALU.mult).then_inc(q_ready, 1)
                if t := tile_of(i, k, 3):
                    ti, tk, s = t
                    if tk == 3:
                        e.wait_ge(xt_ready, s + 1)
                        e.tensor_reduce(gmx[:, ds(ti, 1), :].rearrange("p a n -> p (a n)"),
                                        xT[0:HC, ds(ti, 1), :, :].rearrange("p a k n -> p (a k) n"),
                                        AX.X, ALU.max, apply_absolute_value=True).then_inc(gmx_ready, 1)
            pipeline(e, NB, 4, 3, step)
            smoothing(e)

        def smoothing(e):
            gm, wm, lg, lw, z, v, p2, d1, d2, up, cs, ics = (csm[:, n, :] for n in range(12))
            e.wait_ge(s_watt, 64)
            e.wait_ge(gmx_ready, NB)
            e.tensor_reduce(gm, gmx[:, :, :].rearrange("p b k -> p k b"), AX.X, ALU.max).then_inc(cs_dve, 1)
            e.tensor_reduce(wm, wqkv[0:HC, :, :], AX.X, ALU.max, apply_absolute_value=True).then_inc(cs_dve, 1)
            e.wait_ge(cs_act, 2)
            e.tensor_scalar(lw, lw, -(1.0 - ALPHA), None, ALU.mult).then_inc(cs_dve, 1)
            e.wait_ge(cs_dve, 3)
            e.scalar_tensor_tensor(z, lg, ALPHA, lw, ALU.mult, ALU.add).then_inc(cs_dve, 1)
            e.wait_ge(cs_act, 3)
            e.tensor_scalar(p2.bitcast(I32), v.bitcast(I32), 0x7F800000, None, ALU.bitwise_and).then_inc(cs_dve, 1)
            e.wait_ge(cs_dve, 5)
            e.tensor_tensor(d1, v, p2, ALU.subtract).then_inc(cs_dve, 1)
            e.scalar_tensor_tensor(d2, p2, 2.0, v, ALU.mult, ALU.subtract).then_inc(cs_dve, 1)
            e.wait_ge(cs_dve, 7)
            e.tensor_tensor(up, d1, d2, ALU.is_gt).then_inc(cs_dve, 1)
            e.wait_ge(cs_dve, 8)
            e.scalar_tensor_tensor(cs, up, 1.0, p2, ALU.add, ALU.mult).then_inc(cs_dve, 1)
            e.wait_ge(cs_dve, 9)
            e.reciprocal(ics, cs).then_inc(cs_dve, 1)
            for kt in range(2):
                e.tensor_scalar(wqkv[0:HC, kt, :], wqkv[0:HC, kt, :], cs[:, kt:kt + 1], None, ALU.mult).then_inc(w_scaled, 1)
            e.wait_ge(cs_dve, 10)

        def smoothing_act(e):
            gm, wm, lg, lw, z, v = (csm[:, n, :] for n in range(6))
            e.wait_ge(cs_dve, 2)
            e.activation(lg, gm, ACT.Ln).then_inc(cs_act, 1)
            e.activation(lw, wm, ACT.Ln).then_inc(cs_act, 1)
            e.wait_ge(cs_dve, 4)
            e.activation(v, z, ACT.Exp).then_inc(cs_act, 1)

        s_id0 = sem("zero_fill_done")
        ics = csm[:, 11, :]

        S1, S2, PVB, MISC = 0, 2, 6, 7
        xs_ready, qk_done, v_done = sem("xs_ready"), sem("qk_done"), sem("v_done")
        qk_copied, rest_done, mid_done, parts_ready = sem("qk_copied"), sem("rest_done"), sem("mid_done"), sem("parts_ready")
        stored = [sem(f"parts_stored{m}") for m in range(3)]
        stack_in = [sem(f"stack_in{k}") for k in range(2)]
        v_ready, b_fill = sem("v_ready"), sem("attention_fills_done")
        p1_done, max_done, nh_done, np_ready = sem("p1_done"), sem("max_done"), sem("neg_high_done"), sem("neg_parts_ready")
        nt_done, nmt_ready = sem("neg_turned"), sem("neg_rows_ready")
        neg_in = [sem(f"neg_rows_in{k}") for k in range(2)]
        p2_done, exp_done, pv_done, pvs_ready = sem("p2_done"), sem("exp_done"), sem("pv_done"), sem("pvs_ready")
        sum_log, rsum_ready = sem("sum_log_done"), sem("reciprocal_sums_ready")
        shf_done, ot_ready, h2_ready = sem("sums_spread"), sem("ot_ready"), sem("h2_ready")
        op_done = [sem(f"out_proj_done{k}") for k in range(2)]

        def batch_of(i, kb, lag):
            i, kb = i + (kb - lag) // 2, (kb - lag) % 2
            if isinstance(i, int) and not 0 <= 2 * i + kb < NB:
                return None
            return i, kb, 2 * i + kb

        def group_of(i, m, lag):
            i, m = i + (m - lag) // 6, (m - lag) % 6
            if isinstance(i, int) and not 0 <= 6 * i + m < NB * NG:
                return None
            return i, m, 6 * i + m

        def upto(n, most):
            return max(0, min(n, most)) if isinstance(n, int) else n

        def misc_free(e, qk, v, nt, op):
            after(e, qk_copied, 2 * qk)
            after(e, v_ready, v)
            after(e, nmt_ready, nt)
            after(e, h2_ready, op)

        def qk_job(e, i, kb, b, m, counts):
            e.wait_ge(xs_ready, 2 * b + 2)
            misc_free(e, *counts)
            e.matmul(ps[:, MISC, :], wqkv[0:HC, 0, P * m:P * m + P], xs[0:HC, kb, 0, :], start=True, stop=False)
            e.matmul(ps[:, MISC, :], wqkv[0:HC + 1, 1, P * m:P * m + P], xs[0:HC + 1, kb, 1, :],
                     start=False, stop=True).then_inc(qk_done, 1)

        def v_job(e, i, kb, b, jj, counts):
            misc_free(e, *counts)
            for t in range(2):
                sl = slice(P * (2 * jj + t), P * (2 * jj + t) + P)
                e.matmul(ps[:, MISC, H * t:H * t + H], xs[0:HC, kb, 0, sl], wqkv[0:HC, 0, 2 * H:3 * H], start=True, stop=False)
                m = e.matmul(ps[:, MISC, H * t:H * t + H], xs[0:HC + 1, kb, 1, sl], wqkv[0:HC + 1, 1, 2 * H:3 * H],
                             start=False, stop=True)
            m.then_inc(v_done, 1)

        def b_steps(e, step):
            pipeline(e, NB // 2, 2, 2, step)

        def b_pe(e):
            e.wait_ge(w_scaled, 2)
            e.wait_ge(b_fill, 3)
            e.wait_ge(s_identb, 1)
            def p1(n, m, k):
                kb, g, h = m // 3, m % 3, k // 2
                for uu in range(2):
                    qt = 2 * (k % 2) + uu
                    after(e, max_done, 16 * n + 2 * k + uu - 1)
                    e.matmul(ps[:, S1 + uu, :], QS[0:QROWS, kb, HG * g + h, P * qt:P * qt + P], KS[0:QROWS, kb, HG * g + h, :],
                             start=True, stop=True).then_inc(p1_done, 1)

            def p2(n, m, k):
                kb, g, kt, hp = m // 3, m % 3, k // 2, k % 2
                after(e, exp_done, 8 * n + k - 1)
                for uu in range(2):
                    h = HG * g + 2 * hp + uu
                    mm = e.matmul(ps[:, S2 + 2 * (k % 2) + uu, :], KS[0:QROWS + NEG, kb, h, P * kt:P * kt + P],
                                  QS[0:QROWS + NEG, kb, h, :], start=True, stop=True)
                mm.then_inc(p2_done, 1)

            def pv(n, m, kt):
                kb, g = m // 3, m % 3
                e.wait_ge(exp_done, 8 * n + 2 * kt + 2)
                if kt == 0:
                    after(e, pvs_ready, n)
                for h in range(HG):
                    mm = e.matmul(ps[32 * h:32 * h + 32, PVB, :], VV[:, kb, kt, HG * g + h, :], PT[:, kt % 2, h, :],
                                  start=kt == 0, stop=kt == TPB - 1)
                mm.then_inc(pv_done, 1)

            def step(i, kb):
                b = 2 * i + kb - 1
                nxt, att, prv = (batch_of(i, kb, lag) for lag in range(3))
                nqk, nv, nop = 3 * upto(b + 1, NB), 2 * upto(b + 1, NB), 2 * upto(b - 1, NB)
                for g in range(3):
                    cur, neg, old, last = (group_of(i, 3 * kb + g, lag) for lag in (3, 4, 5, 6))
                    nnt = upto(3 * b + g, NB * NG)
                    dqk, dv = (3, 2) if nxt else (0, 0)
                    if att and g == 0:
                        e.wait_ge(stack_in[att[1]], 192 * (att[0] + 1))
                    if att and g == 2:
                        e.wait_ge(v_ready, 2 * att[2] + 2)
                    if old:
                        e.wait_ge(neg_in[old[1] % 2], 32 * (3 * old[0] + old[1] // 2 + 1))
                    for k in range(8):
                        if cur:
                            p1(cur[2], cur[1], k)
                        if old:
                            p2(old[2], old[1], k)
                        if k == 1 and last:
                            pv(last[2], last[1], 3)
                        if k in (3, 5, 7) and old:
                            pv(old[2], old[1], k // 2 - 1)
                        if k == 2 and neg:
                            ng, nm = neg[2], neg[1]
                            e.wait_ge(np_ready, ng + 1)
                            misc_free(e, nqk + (dqk if g else 0), nv, ng, nop)
                            for t in range(TPB):
                                mm = e.transpose(ps[0:2 * HG, MISC, 0:S // 2].bitcast(BF16)[:, P * t:P * t + P],
                                                 npt[:, nm % 2, t, :], identb[:, :])
                            mm.then_inc(nt_done, 1)
                        if nxt:
                            if g == 0 and k in (4, 5, 6):
                                qk_job(e, *nxt, k - 4, (nqk + k - 4, nv, nnt, nop))
                            if g == 2 and k in (3, 4):
                                v_job(e, *nxt, k - 3, (nqk + 3, nv + k - 3, nnt, nop))
                        if prv and g == 2 and k in (5, 7):
                            jj = (k - 5) // 2
                            pi, pk, pb = prv
                            e.wait_ge(ot_ready, 3 * pb + 3)
                            misc_free(e, nqk + dqk, nv + dv, nnt, nop + jj)
                            for t in range(2):
                                sl = slice(P * (2 * jj + t), P * (2 * jj + t) + P)
                                for gg in range(NG):
                                    mm = e.matmul(ps[:, MISC, H * t:H * t + H], OT[:, pk, gg, sl], wo[:, gg, :],
                                                  start=gg == 0, stop=gg == NG - 1)
                            mm.then_inc(op_done[pk], 1)
            b_steps(e, step)

        def qk_evac(e, m, i, kb):
            x = 6 * i + 3 * kb + m
            p = (3 * kb + m) % 2
            e.wait_ge(qk_done, x + 1)
            after(e, parts_ready, x - 1)
            e.activation(qk32[:, p, :], ps[:, MISC, :], ACT.Copy).then_inc(qk_copied, 1)
            if isinstance(x, int):
                if x >= 2:
                    e.wait_ge(stored[(m - 2) % 3], 16 * ((x - 2) // 3 + 1))
            else:
                e.wait_ge(stored[(m - 2) % 3], 16 * (2 * i + kb + (m - 2) // 3 + 1))
            e.activation(parts[:, p, 0, :], ps[:, MISC, :], ACT.Copy).then_inc(qk_copied, 1)

        def v_evac(e, jj, kb, x, used):
            e.wait_ge(v_done, x + 1)
            after(e, pv_done, used)
            e.activation(VV[:, kb, 2 * jj:2 * jj + 2, :, 0:HD],
                         ps[:, MISC, 0:2 * H].rearrange("p (t h d) -> p t h d", t=2, h=NH), ACT.Copy).then_inc(v_ready, 1)

        def b_act(e):
            smoothing_act(e)

            def step(i, kb):
                nxt = batch_of(i, kb, 0)
                for g in range(3):
                    neg, old, last = (group_of(i, 3 * kb + g, lag) for lag in (4, 5, 6))
                    for k in range(8):
                        if old:
                            n, kt, hp = old[2], k // 2, k % 2
                            e.wait_ge(p2_done, 8 * n + k + 1)
                            if hp == 0:
                                after(e, pv_done, 4 * n + kt - 1)
                            e.activation(PT[:, kt % 2, 2 * hp:2 * hp + 2, :], ps[:, S2 + 2 * (k % 2):S2 + 2 * (k % 2) + 2, :],
                                         ACT.Exp, scale=SCALE).then_inc(exp_done, 1)
                        if k == 1 and last:
                            e.wait_ge(pv_done, 4 * last[2] + 4)
                            after(e, ot_ready, last[2])
                            e.activation(pvs[:, :], ps[:, PVB, :], ACT.Copy).then_inc(pvs_ready, 1)
                        if k == 2 and neg:
                            e.wait_ge(nt_done, neg[2] + 1)
                            after(e, neg_in[neg[1] % 2], 32 * (3 * neg[0] + neg[1] // 2))
                            e.activation(nmT[:, neg[1] % 2, :], ps[0:2 * HG, MISC, 0:S // 2].bitcast(BF16),
                                         ACT.Copy).then_inc(nmt_ready, 1)
                        if k == 3 and last:
                            e.wait_ge(shf_done, last[2] + 1)
                            e.activation(sums[:, :], sums[:, :], ACT.Ln).then_inc(sum_log, 1)
                            e.wait_ge(sum_log, last[2] + 1)
                            e.activation(rsum[:, :], sums[:, :], ACT.Exp, scale=-1.0).then_inc(rsum_ready, 1)
                        if k == 3 and neg:
                            e.wait_ge(nmt_ready, neg[2] + 1)
                            nk, ng = neg[1] // 3, neg[1] % 3
                            for pt in range(NEG):
                                e.dma_start(QS[QROWS + pt:QROWS + pt + 1, nk, HG * ng:HG * ng + HG, :],
                                            nmT[HG * pt:HG * pt + HG, neg[1] % 2, :]).then_inc(neg_in[neg[1] % 2], 16)
                        if nxt:
                            if g == 0 and k in (4, 5, 6):
                                qk_evac(e, k - 4, nxt[0], nxt[1])
                            if g == 2 and k in (3, 4):
                                v_evac(e, k - 3, nxt[1], 2 * nxt[2] + k - 3, 4 * NG * (nxt[2] - 1))
            b_steps(e, step)

        def b_pool(e):
            e.wait_ge(t1_done, NT)
            e.wait_ge(pj_done, NT)
            e.wait_ge(fc_done, NT)
            e.wait_ge(x_ready, NT)
            e.wait_ge(t3_done, NT)
            e.memset(VV[:, :, :, :, HD:32], 1.0).then_inc(b_fill, 1)
            e.wait_ge(b_fill, 1)
            e.memset(KS[QROWS:QROWS + NEG, :, :, :], 1.0).then_inc(b_fill, 1)
            e.wait_ge(b_fill, 2)
            e.memset(xs[HC:HC + 1, :, 1, :], 1.0).then_inc(b_fill, 1)
            e.wait_ge(b_fill, 3)

            def split(i, kb, m):
                x = 6 * i + 3 * kb + m
                p = (3 * kb + m) % 2
                e.wait_ge(qk_copied, 2 * x + 2)
                after(e, parts_ready, x)
                e.tensor_tensor(rest[:, :], qk32[:, p, :], parts[:, p, 0, :], ALU.subtract).then_inc(rest_done, 1)
                e.wait_ge(rest_done, x + 1)
                gate(e)
                e.tensor_copy(parts[:, p, 1, :], rest[:, :]).then_inc(mid_done, 1)
                e.wait_ge(mid_done, x + 1)
                e.tensor_tensor(parts[:, p, 2, :], rest[:, :], parts[:, p, 1, :], ALU.subtract).then_inc(parts_ready, 1)
            for kb in range(2):
                for m in range(3):
                    split(0, kb, m)
            with e.Fori(1, NB // 2) as i:
                for kb in range(2):
                    for m in range(3):
                        split(i, kb, m)

        def b_sync(e):
            def stacks(i, kb):
                if not isinstance(i, int):
                    after(e, stack_in[kb], 192 * i)
                    gate(e)
                for m in range(3):
                    x = 6 * i + 3 * kb + m
                    e.wait_ge(parts_ready, x + 1)
                    gate(e)
                    e.dma_start(qkd[kb, m], parts[:, (3 * kb + m) % 2, :, :]).then_inc(stored[m], 16)
                for m in range(3):
                    e.wait_ge(stored[m], 16 * (2 * i + kb + 1))
                    gate(e)
                after(e, p2_done, 8 * 3 * (2 * i + kb - 1))
                gate(e)
                rows = qkd[kb].rearrange("m p j s -> (m p) j s")
                for which, dst, prt in ((0, QS, QPARTS), (1, KS, KPARTS)):
                    src = rows[H * which:H * which + H].rearrange("(h d) j s -> d h j s", h=NH)
                    for j in range(QP):
                        e.dma_start(dst[HD * j:HD * j + HD, kb, :, :], src[:, :, prt[j], :]).then_inc(stack_in[kb], 16)
            for kb in range(2):
                stacks(0, kb)
            with e.Fori(1, NB // 2) as i:
                for kb in range(2):
                    stacks(i, kb)

        def b_dve(e):
            e.wait_ge(b_fill, 3)

            def x_in(i, kb, b):
                after(e, qk_done, 3 * (b - 1))
                after(e, v_done, 2 * (b - 1))
                for kt in range(2):
                    e.tensor_scalar(xs[0:HC, kb, kt, :], xT[0:HC, ds(b, 1), kt, :].rearrange("p a n -> p (a n)"),
                                    ics[:, kt:kt + 1], None, ALU.mult).then_inc(xs_ready, 1)

            def step(i, kb):
                nxt, prv = batch_of(i, kb, 0), batch_of(i, kb, 2)
                if nxt:
                    x_in(*nxt)
                for g in range(3):
                    cur, last = group_of(i, 3 * kb + g, 3), group_of(i, 3 * kb + g, 6)
                    for k in range(8):
                        if cur:
                            n, m = cur[2], cur[1]
                            if k == 0:
                                after(e, nt_done, n - 1)
                            for uu in range(2):
                                x = 16 * n + 2 * k + uu
                                e.wait_ge(p1_done, x + 1)
                                e.tensor_reduce(nmx[:, m % 2, 2 * (k % 2) + uu, k // 2:k // 2 + 1], ps[:, S1 + uu, :],
                                                AX.X, ALU.max, negate=True).then_inc(max_done, 1)
                        if k == 2 and last:
                            n = last[2]
                            e.wait_ge(pvs_ready, n + 1)
                            gate(e)
                            e.stream_shuffle(sums[:, :], pvs[:, :], [HD] * 32).then_inc(shf_done, 1)
                        if k == 4 and last:
                            n, m = last[2], last[1]
                            lk, lg = m // 3, m % 3
                            e.wait_ge(rsum_ready, n + 1)
                            after(e, op_done[lk], 2 * last[0])
                            e.tensor_tensor(OT[:, lk, lg, :], pvs[:, :], rsum[:, :], ALU.mult).then_inc(ot_ready, 1)
                        if prv and g == 2 and k in (6, 7):
                            jj = k - 6
                            e.wait_ge(op_done[prv[1]], 2 * prv[0] + jj + 1)
                            hh = hall[:, ds(4 * prv[2] + 2 * jj, 2), :].rearrange("p a n -> p (a n)")
                            e.tensor_tensor(hh, ps[:, MISC, 0:2 * H], hh, ALU.add).then_inc(h2_ready, 1)
                    if cur:
                        n, m = cur[2], cur[1]
                        e.wait_ge(max_done, 16 * n + 16)
                        e.tensor_copy(npt[:, m % 2, :, 0:HG], nmx[:, m % 2, :, :]).then_inc(nh_done, 1)
                        e.wait_ge(nh_done, n + 1)
                        e.tensor_tensor(npt[:, m % 2, :, HG:2 * HG], nmx[:, m % 2, :, :], npt[:, m % 2, :, 0:HG],
                                        ALU.subtract).then_inc(np_ready, 1)
            b_steps(e, step)


        room = xT[:, :, :, :].rearrange("p b k n -> p (b k n)")
        at = 0

        def room_part(n):
            nonlocal at
            at += n
            assert at <= NB * 2 * S
            return room[:, at - n:at]
        hs = room_part(2 * TPB * H).rearrange("p (b t n) -> p b t n", b=2, t=TPB)
        xf = room_part(2 * TPB * H).rearrange("p (b t n) -> p b t n", b=2, t=TPB)
        entry = room_part(2 * TPB * 2 * 2).rearrange("p (b t a n) -> p b t a n", b=2, t=TPB, a=2)
        xfT = room_part(2 * 2 * P).rearrange("p (b k n) -> p b k n", b=2, k=2)
        c5 = rest[:, 0:2 * H].rearrange("p (b n) -> p b n", b=2)
        sel = room_part(NT * E).rearrange("p (t n) -> p t n", t=NT)
        cum = room_part((NT + 1) * E).rearrange("p (t n) -> p t n", t=NT + 1)
        above = room_part(TPB * E * E)
        equal = room_part(TPB * E * E)
        probs, dif, rk, first, second, slot, tmp, tmp2 = (
            room_part(TPB * E).rearrange("p (t n) -> p t n", t=TPB) for _ in range(8))
        mx, sm, rs, pa, pb_, dn, rd, sa, sb_ = (room_part(TPB) for _ in range(9))
        st4 = room_part(2 * TPB * 6).rearrange("p (l t n) -> p l t n", l=2, t=TPB)
        mv4 = room_part(2 * TPB * 2).rearrange("p (l t n) -> p l t n", l=2, t=TPB)
        lv4 = room_part(2 * TPB).rearrange("p (l t) -> p l t", l=2)
        rs4 = room_part(2 * TPB).rearrange("p (l t) -> p l t", l=2)
        rp1, nmr = room_part(TPB), room_part(TPB)
        slots = room_part(2 * TPB * 2).bitcast(I32).rearrange("p (b t a) -> p b t a", b=2, t=TPB)
        zero = room_part(E * CAP * 2 // P)
        pad_entry = room_part(2)
        cnt, ntl, start, stop_, shift = (room_part(E) for _ in range(5))
        nti = room_part(E).bitcast(I32)
        idx = room_part(DT)
        tef = room_part(DT)
        lt_, in_ = room_part(DT), room_part(DT)
        idi = room_part(DT).bitcast(I32)
        tei = room_part(DT).bitcast(I32)
        idr = room_part(DU).bitcast(I32)
        toki = room_part(DU).bitcast(I32)
        eg = room_part(DU * 2).rearrange("p (b n) -> p b n", b=DU)
        XG = parts[:, :, :, :].rearrange("p b j s -> p (b j s)").bitcast(F32).rearrange("p (b n) -> p b n", b=DU)
        ott = OT[:, :, :, :].rearrange("p b g s -> p (b g s)")
        Hs = ott[:, 0:2 * FF].rearrange("p (b n) -> p b n", b=2)
        hT = ott[:, 2 * FF:4 * FF].rearrange("p (b c n) -> p b c n", b=2, c=FC)
        xgT = pvs[:, :].rearrange("p (b k n) -> p b k n", b=2, k=2)
        Y = sums[:, 0:2 * H].rearrange("p (b n) -> p b n", b=2)
        w1 = big[:, 0:E * 2 * FF].rearrange("p (e k n) -> p e k n", e=E, k=2)
        w2 = big[:, E * 2 * FF:].rearrange("p (e c n) -> p e c n", e=E, c=FC)

        s_w = sem("expert_weights_in")
        c_zero, c_pad = sem("zero_rows_ready"), sem("padding_rows_stored")
        bn4, mv4_ready = [sem(f"route_bn{n}_done") for n in range(2)], [sem(f"route_mean_var{n}_ready") for n in range(2)]
        log4, rs4_ready = [sem(f"route_log{n}_done") for n in range(2)], [sem(f"route_rstd{n}_ready") for n in range(2)]
        aff_ready, hs_ready, res_ready, res_out = sem("residual_scales_ready"), sem("hs_ready"), sem("residual_ready"), sem("residual_stored")
        c5_done, xff_ready = sem("c5_done"), sem("xff_ready")
        xt4_done, xt4_ready, lg_done = sem("xff_turned"), sem("xff_turned_ready"), sem("logits_done")
        route, rexp, rank_done, slots_ready = sem("routing_steps"), sem("routing_exp_done"), sem("rank_done"), sem("slots_ready")
        x_out = [sem(f"x_rows_stored{k}") for k in range(2)]
        scat = [sem(f"rows_listed{k}") for k in range(2)]
        cnt_done, plan, plan_ready = sem("counts_done"), sem("plan_steps"), sem("plan_ready")

        def c_begin(e):
            e.wait_ge(h2_ready, 2 * NB)

        def c_sync(e):
            c_begin(e)
            e.wait_ge(c_zero, 3)
            e.dma_start(lists[0:E * CAP, :].rearrange("(p n) c -> p (n c)", p=P), zero).then_inc(c_pad, 16)
            e.dma_start(lists[E * CAP:E * CAP + P, :], pad_entry).then_inc(c_pad, 16)
            e.dma_start(xrows[NB * S:NB * S + P, :], zero[:, 0:H]).then_inc(c_pad, 16)
            e.dma_start(out_ext[NB * S:NB * S + P, :], zero[:, 0:H]).then_inc(c_pad, 16)

            for x in range(E):
                e.dma_start(w1[0:HC, x, :, :], a["w1"][:, x, :, :]).then_inc(s_w, 16)
                e.dma_start(w2[:, x, :, :], a["w2"][:, x, :, :]).then_inc(s_w, 16)
            def step(i, kb):
                b = 2 * i + kb
                e.wait_ge(res_ready, TPB * b + TPB)
                e.dma_start(out_ext[ds(S * b, S), :].rearrange("(t p) c -> p t c", p=P),
                            hall[:, ds(TPB * b, TPB), :]).then_inc(res_out, 16)
                e.wait_ge(xff_ready, TPB * b + TPB)
                e.dma_start(xrows[ds(S * b, S), :].rearrange("(t p) c -> p t c", p=P), xf[:, kb, :, :]).then_inc(x_out[kb], 16)
            pipeline(e, NB // 2, 2, 0, step)

        def c_pe(e):
            c_begin(e)

            def step(i, kb):
                if pb := batch_of(i, kb, 1):
                    b = pb[2]
                    e.wait_ge(route, R * b + R_CUM)
                    e.matmul(ps[:, 4 + pb[1], 0:TPB * E], const[:, C_TRI:C_TRI + P],
                             sel[:, ds(TPB * b, TPB), :].rearrange("p t n -> p (t n)"), start=True, stop=False)
                    e.matmul(ps[:, 4 + pb[1], 0:TPB * E], const[:, C_ONE:C_ONE + P],
                             cum[:, ds(TPB * b, TPB), :].rearrange("p t n -> p (t n)"), start=False, stop=True).then_inc(rank_done, 1)
                if nb := batch_of(i, kb, 0):
                    b = nb[2]
                    for t in range(TPB):
                        s = TPB * b + t
                        e.wait_ge(xff_ready, s + 1)
                        after(e, xt4_ready, s - 1)
                        for kt in range(2):
                            m = e.transpose(ps[0:HC, t % 2, P * kt:P * kt + P], xf[:, kb, t, HC * kt:HC * kt + HC], ident)
                        m.then_inc(xt4_done, 1)
                        e.wait_ge(xt4_ready, s + 1)
                        if t == 0:
                            after(e, route, R * (b - 2) + 2)
                        for kt in range(2):
                            m = e.matmul(ps[:, 2 + kb, E * t:E * t + E], xfT[0:HC, t % 2, kt, :], wr[:, kt, :],
                                         start=kt == 0, stop=kt == 1)
                        m.then_inc(lg_done, 1)
            pipeline(e, NB // 2, 2, 1, step)
            e.wait_ge(route, R * NB)
            e.matmul(ps[:, 6, 0:E], const[:, C_ONE:C_ONE + P], cum[:, NT, :], start=True, stop=True).then_inc(cnt_done, 1)

        R = 26
        R_EXP, R_CUM = 2, 20

        def c_act(e):
            c_begin(e)

            def norm(n, b):
                e.wait_ge(mv4_ready[n], TPB * b + TPB)
                e.activation(lv4[:, n, :], mv4[:, n, :, 1], ACT.Ln, bias=eps[:, 0:1]).then_inc(log4[n], 1)
                e.wait_ge(log4[n], b + 1)
                e.activation(rs4[:, n, :], lv4[:, n, :], ACT.Exp, scale=-0.5).then_inc(rs4_ready[n], 1)

            def step(i, kb):
                nb, pb = batch_of(i, kb, 0), batch_of(i, kb, 1)
                if nb:
                    norm(0, nb[2])
                if pb:
                    e.wait_ge(route, R * pb[2] + R_EXP)
                    e.activation(probs[:, :, :], dif[:, :, :], ACT.Exp).then_inc(rexp, 1)
                if nb:
                    b = nb[2]
                    e.wait_ge(aff_ready, 2 * b + 2)
                    e.wait_ge(hs_ready, TPB * b + TPB)
                    gate(e)
                    for t in range(TPB):
                        x = hall[:, ds(TPB * b + t, 1), :].rearrange("p a n -> p (a n)")
                        e.activation(x, x, ACT.Identity, bias=nmr[:, t:t + 1], scale=rp1[:, t:t + 1]).then_inc(res_ready, 1)
                    norm(1, b)
                if nb := batch_of(i, kb, 0):
                    b = nb[2]
                    for t in range(TPB):
                        s = TPB * b + t
                        e.wait_ge(xt4_done, s + 1)
                        after(e, lg_done, s - 1)
                        e.activation(xfT[0:HC, t % 2, :, :], ps[0:HC, t % 2, 0:2 * P].rearrange("p (k n) -> p k n", k=2),
                                     ACT.Copy).then_inc(xt4_ready, 1)
            pipeline(e, NB // 2, 2, 1, step)

        def c_pool(e):
            c_begin(e)
            e.memset(zero, 0.0).then_inc(c_zero, 1)
            e.wait_ge(c_zero, 1)
            e.memset(pad_entry[:, 0:1], 0.0).then_inc(c_zero, 1)
            e.wait_ge(c_zero, 2)
            e.tensor_copy(pad_entry[:, 1:2], const[:, C_PADTOK:C_PADTOK + 1]).then_inc(c_zero, 1)
            e.wait_ge(c_pad, 64)

            def step(i, kb):
                if pb := batch_of(i, kb, 1):
                    b = pb[2]
                    e.wait_ge(slots_ready, b + 1)
                    gate(e)
                    for t in range(TPB):
                        for x in range(2):
                            e.indirect_dma_start(out=lists, out_offset=bass.IndirectOffsetOnAxis(ap=slots[:, pb[1], t, x:x + 1], axis=0),
                                                 in_=entry[:, pb[1], t, x, :], in_offset=None).then_inc(scat[pb[1]], 16)
            pipeline(e, NB // 2, 2, 1, step)

        def c_dve(e):
            c_begin(e)
            e.memset(cum[:, 0, :], 0.0).then_inc(c_fill, 1)
            e.wait_ge(c_fill, 1)

            def spread(x):
                return x.unsqueeze(2).broadcast_to((P, TPB, E))

            def lnorm(n, b, src):
                for t in range(TPB):
                    if n == 0:
                        gate(e)
                    e.bn_stats(st4[:, n, t, :], src(t)).then_inc(bn4[n], 1)
                e.wait_ge(bn4[n], TPB * b + TPB)
                after(e, rs4_ready[n], b)
                gate(e)
                for t in range(TPB):
                    e.bn_aggr(mv4[:, n, t, :], st4[:, n, t, :]).then_inc(mv4_ready[n], 1)

            def route_batch(i, kb, b, half):
                n = 0

                def did(ins):
                    nonlocal n
                    n += 1
                    ins.then_inc(route, 1)

                def have(k):
                    e.wait_ge(route, R * b + k)
                if half == 0:
                    lg = ps[:, 2 + kb, 0:TPB * E].rearrange("p (t n) -> p t n", t=TPB)
                    e.wait_ge(lg_done, TPB * b + TPB)
                    did(e.tensor_reduce(mx, lg, AX.X, ALU.max))
                    have(1)
                    did(e.tensor_tensor(dif, lg, spread(mx), ALU.subtract))
                    e.wait_ge(rexp, b + 1)
                    did(e.tensor_reduce(sm, probs, AX.X, ALU.add))
                    have(3)
                    did(e.reciprocal(rs, sm))
                    have(4)
                    did(e.tensor_tensor(probs, probs, spread(rs), ALU.mult))
                    have(5)
                    q4 = probs.unsqueeze(2).broadcast_to((P, TPB, E, E))
                    p4 = probs.unsqueeze(3).broadcast_to((P, TPB, E, E))
                    ab = above.rearrange("p (t e f) -> p t e f", t=TPB, e=E)
                    eq = equal.rearrange("p (t e f) -> p t e f", t=TPB, e=E)
                    low = const[:, C_LOW:C_LOW + E * E].unsqueeze(1).broadcast_to((P, TPB, E * E))
                    did(e.tensor_tensor(ab, q4, p4, ALU.is_gt))
                    did(e.tensor_tensor(eq, q4, p4, ALU.is_equal))
                    have(7)
                    eqt = equal.rearrange("p (t e) -> p t e", t=TPB)
                    did(e.tensor_tensor(eqt, eqt, low, ALU.mult))
                    have(8)
                    did(e.tensor_tensor(above, above, equal, ALU.add))
                    have(9)
                    did(e.tensor_reduce(rk, ab, AX.X, ALU.add))
                    have(10)
                    did(e.tensor_scalar(first, rk, 0.0, None, ALU.is_equal))
                    did(e.tensor_scalar(second, rk, 1.0, None, ALU.is_equal))
                    se = sel[:, ds(TPB * b, TPB), :]
                    did(e.tensor_scalar(se, rk, 2.0, None, ALU.is_lt))
                    have(13)
                    did(e.tensor_tensor(tmp, first, probs, ALU.mult))
                    did(e.tensor_tensor(tmp2, second, probs, ALU.mult))
                    have(15)
                    did(e.tensor_reduce(pa, tmp, AX.X, ALU.add))
                    for t in range(TPB):
                        if t:
                            have(16 + t)
                        did(e.tensor_tensor(cum[:, ds(TPB * b + t + 1, 1), :], cum[:, ds(TPB * b + t, 1), :],
                                            sel[:, ds(TPB * b + t, 1), :], ALU.add))
                    return
                n = R_CUM
                did(e.tensor_reduce(pb_, tmp2, AX.X, ALU.add))
                have(21)
                did(e.tensor_tensor(dn, pa, pb_, ALU.add))
                have(22)
                did(e.reciprocal(rd, dn))
                e.wait_ge(rank_done, b + 1)
                did(e.tensor_tensor(slot, ps[:, 4 + kb, 0:TPB * E].rearrange("p (t n) -> p t n", t=TPB),
                                    const[:, C_CAP:C_CAP + E].unsqueeze(1).broadcast_to((P, TPB, E)), ALU.add))
                have(24)
                did(e.tensor_tensor(tmp, first, slot, ALU.mult))
                did(e.tensor_tensor(tmp2, second, slot, ALU.mult))
                assert n == R
                have(26)
                e.tensor_reduce(sa, tmp, AX.X, ALU.add).then_inc(slot_sum, 1)
                e.tensor_reduce(sb_, tmp2, AX.X, ALU.add).then_inc(slot_sum, 1)
                e.wait_ge(slot_sum, 2 * b + 2)
                after(e, scat[kb], 128 * i)
                for x, pr_ in enumerate((pa, pb_)):
                    e.tensor_tensor(entry[:, kb, :, x, 0], pr_, rd, ALU.mult).then_inc(gates_in, 1)
                    e.tensor_copy(entry[:, kb, :, x, 1], const[:, ds(C_TOK + TPB * b, TPB)]).then_inc(gates_in, 1)
                e.tensor_copy(slots[:, kb, :, 0], sa).then_inc(gates_in, 1)
                e.wait_ge(gates_in, 5 * b + 5)
                e.tensor_copy(slots[:, kb, :, 1], sb_).then_inc(slots_ready, 1)

            def step(i, kb):
                nb, pb = batch_of(i, kb, 0), batch_of(i, kb, 1)
                if nb:
                    b = nb[2]
                    after(e, hs_ready, TPB * b)
                    lnorm(0, b, lambda t: hall[:, ds(TPB * b + t, 1), :].rearrange("p a n -> p (a n)"))
                if pb:
                    route_batch(*pb, 0)
                if nb:
                    e.wait_ge(mv4_ready[0], TPB * b + TPB)
                    e.wait_ge(rs4_ready[0], b + 1)
                    after(e, res_ready, TPB * b)
                    e.tensor_scalar(rp1, rs4[:, 0, :], 1.0, None, ALU.add).then_inc(aff_ready, 1)
                    e.scalar_tensor_tensor(nmr, mv4[:, 0, :, 0], -1.0, rs4[:, 0, :], ALU.mult, ALU.mult).then_inc(aff_ready, 1)
                    for t in range(TPB):
                        e.tensor_scalar(hs[:, kb, t, :], hall[:, ds(TPB * b + t, 1), :].rearrange("p a n -> p (a n)"),
                                        mv4[:, 0, t, 0:1], rs4[:, 0, t:t + 1], ALU.subtract, ALU.mult).then_inc(hs_ready, 1)
                    e.wait_ge(hs_ready, TPB * b + TPB)
                    gate(e)
                    lnorm(1, b, lambda t: hs[:, kb, t, :])
                if pb:
                    route_batch(*pb, 1)
                if nb:
                    e.wait_ge(mv4_ready[1], TPB * b + TPB)
                    e.wait_ge(rs4_ready[1], b + 1)
                    after(e, x_out[kb], 16 * nb[0])
                    for t in range(TPB):
                        s = TPB * b + t
                        after(e, xff_ready, s - 1)
                        e.scalar_tensor_tensor(c5[:, t % 2, :], hs[:, kb, t, :], mv4[:, 1, t, 0:1], lnp[:, 4, :],
                                               ALU.subtract, ALU.mult).then_inc(c5_done, 1)
                        e.wait_ge(c5_done, s + 1)
                        e.scalar_tensor_tensor(xf[:, kb, t, :], c5[:, t % 2, :], rs4[:, 1, t:t + 1], lnp[:, 5, :],
                                               ALU.mult, ALU.add).then_inc(xff_ready, 1)
            pipeline(e, NB // 2, 2, 1, step)
            make_plan(e)
        c_fill, slot_sum, gates_in = sem("routing_fills_done"), sem("slot_sums_done"), sem("gates_in_rows")

        def make_plan(e):
            n = 0

            def did(ins):
                nonlocal n
                n += 1
                ins.then_inc(plan, 1)
                e.wait_ge(plan, n)
            e.wait_ge(cnt_done, 1)
            did(e.tensor_copy(cnt, ps[:, 6, 0:E]))
            did(e.tensor_copy(nti, cnt))
            did(e.tensor_scalar(nti, nti, P - 1, None, ALU.add))
            did(e.tensor_scalar(nti, nti, P.bit_length() - 1, None, ALU.arith_shift_right))
            did(e.tensor_copy(ntl, nti))
            did(e.tensor_scalar(ntl, ntl, float(P), None, ALU.mult))
            pair = above[:, 0:E * E].rearrange("p (e f) -> p e f", e=E)
            did(e.tensor_tensor(pair, ntl.unsqueeze(1).broadcast_to((P, E, E)),
                                const[:, C_LOW:C_LOW + E * E].rearrange("p (e f) -> p e f", e=E), ALU.mult))
            did(e.tensor_reduce(start, pair, AX.X, ALU.add))
            did(e.tensor_tensor(stop_, start, cnt, ALU.add))
            did(e.tensor_tensor(shift, const[:, C_CAP:C_CAP + E], start, ALU.subtract))
            did(e.tensor_scalar(shift, shift, const[:, C_PAD:C_PAD + 1], None, ALU.subtract))
            f, tile_row = const[:, C_F:C_F + DT], const[:, C_I:C_I + DT]
            did(e.tensor_scalar(idx, f, 0.0, const[:, C_PAD:C_PAD + 1], ALU.mult, ALU.add))
            did(e.tensor_scalar(tef, tile_row, start[:, 1:2], None, ALU.is_ge))
            for x in range(E):
                did(e.tensor_scalar(lt_, f, stop_[:, x:x + 1], None, ALU.is_lt))
                did(e.scalar_tensor_tensor(in_, f, start[:, x:x + 1], lt_, ALU.is_ge, ALU.mult))
                did(e.scalar_tensor_tensor(lt_, f, shift[:, x:x + 1], in_, ALU.add, ALU.mult))
                did(e.tensor_tensor(idx, idx, lt_, ALU.add))
                if x >= 2:
                    did(e.scalar_tensor_tensor(tef, tile_row, start[:, x:x + 1], tef, ALU.is_ge, ALU.add))
            did(e.tensor_copy(tei, tef))
            e.tensor_copy(idi, idx).then_inc(plan_ready, 1)

        idr_ready, tok_ready = sem("tile_entries_chosen"), sem("gate_and_tokens_kept")
        egath = [sem(f"entries_in{k}") for k in range(2)]
        gath = [sem(f"x_rows_in{k}") for k in range(DU)]
        xd_done, xd_ready, hd_done, silu_done = sem("x_turned"), sem("x_turned_ready"), sem("inner_done"), sem("silu_done")
        ht_done, ht_ready, y_done, y_ready = sem("inner_turned"), sem("inner_turned_ready"), sem("y_done"), sem("y_ready")
        added = sem("rows_added")

        def dtile(i, k, lag):
            k, i = (k - lag) % DU, i + (k - lag) // DU
            if isinstance(i, int) and not 0 <= i < DT // DU:
                return None
            return i, k, DU * i + k

        def d_pe(e):
            e.wait_ge(s_w, 2 * E * 16)
            e.wait_ge(plan_ready, 1)

            def step(i, k):
                if t := dtile(i, k, 2):
                    ti, tk, s = t
                    e.wait_ge(gath[tk], 16 * (ti + 1))
                    after(e, xd_ready, s)
                    for kt in range(2):
                        m = e.transpose(ps[0:HC, 0, P * kt:P * kt + P], XG[:, tk, HC * kt:HC * kt + HC], ident)
                    m.then_inc(xd_done, 1)
                if t := dtile(i, k, 3):
                    ti, tk, s = t
                    ex_ = e.value_load(tei[0:1, ds(s, 1)], min_val=0, max_val=E - 1)
                    e.wait_ge(xd_ready, s + 1)
                    for hf in range(2):
                        after(e, silu_done, 2 * (s - 2) + hf + 1)
                        for kt in range(2):
                            m = e.matmul(ps[:, 1 + 2 * (tk % 2) + hf, 0:FH], xgT[0:HC, tk % 2, kt, :],
                                         w1[0:HC, ds(ex_, 1), kt, FH * hf:FH * hf + FH].rearrange("p a n -> p (a n)"),
                                         start=kt == 0, stop=kt == 1)
                        m.then_inc(hd_done, 1)
                if t := dtile(i, k, 4):
                    ti, tk, s = t
                    for hf in range(2):
                        e.wait_ge(silu_done, 2 * s + hf + 1)
                        after(e, ht_ready, 2 * (s - 1) + hf + 1)
                        for c in range(3):
                            f0 = P * (3 * hf + c)
                            m = e.transpose(ps[:, 5 + hf, P * c:P * c + P], Hs[:, tk % 2, f0:f0 + P], ident)
                        m.then_inc(ht_done, 1)
                if t := dtile(i, k, 5):
                    ti, tk, s = t
                    ex_ = e.value_load(tei[0:1, ds(s, 1)], min_val=0, max_val=E - 1)
                    after(e, y_ready, s)
                    for c in range(FC):
                        if c % 3 == 0:
                            e.wait_ge(ht_ready, 2 * s + c // 3 + 1)
                        m = e.matmul(ps[:, 7, 0:H], hT[:, tk % 2, c, :], w2[:, ds(ex_, 1), c, :].rearrange("p a n -> p (a n)"),
                                     start=c == 0, stop=c == FC - 1)
                    m.then_inc(y_done, 1)
            pipeline(e, DT // DU, DU, 5, step)

        def d_act(e):
            def step(i, k):
                if t := dtile(i, k, 2):
                    ti, tk, s = t
                    e.wait_ge(xd_done, s + 1)
                    after(e, hd_done, 2 * (s - 2) + 2)
                    e.activation(xgT[0:HC, tk % 2, :, :], ps[0:HC, 0, 0:2 * P].rearrange("p (k n) -> p k n", k=2),
                                 ACT.Copy).then_inc(xd_ready, 1)
                if t := dtile(i, k, 3):
                    ti, tk, s = t
                    for hf in range(2):
                        e.wait_ge(hd_done, 2 * s + hf + 1)
                        after(e, ht_done, 2 * (s - 2) + 2)
                        e.activation(Hs[:, tk % 2, FH * hf:FH * hf + FH], ps[:, 1 + 2 * (tk % 2) + hf, 0:FH],
                                     ACT.Silu).then_inc(silu_done, 1)
            e.wait_ge(rexp, NB)
            e.preload_act_table_set("silu_and_others")
            pipeline(e, DT // DU, DU, 3, step)

        def d_dve(e):
            e.wait_ge(plan_ready, 1)

            def step(i, k):
                if t := dtile(i, k, 0):
                    ti, tk, s = t
                    after(e, y_ready, s - DU + 1)
                    e.tensor_copy(idr[:, tk:tk + 1], idi[:, ds(s, 1)]).then_inc(idr_ready, 1)
                if t := dtile(i, k, 1):
                    ti, tk, s = t
                    e.wait_ge(egath[tk % 2], 16 * (DU // 2 * ti + tk // 2 + 1))
                    after(e, added, 16 * (s - DU + 1))
                    e.tensor_copy(toki[:, tk:tk + 1], eg[:, tk, 1:2]).then_inc(tok_ready, 1)
                if t := dtile(i, k, 4):
                    ti, tk, s = t
                    for hf in range(2):
                        e.wait_ge(ht_done, 2 * s + hf + 1)
                        after(e, y_done, s - 1)
                        e.tensor_copy(hT[:, tk % 2, 3 * hf:3 * hf + 3, :],
                                      ps[:, 5 + hf, 0:3 * P].rearrange("p (c n) -> p c n", c=3)).then_inc(ht_ready, 1)
                if t := dtile(i, k, 5):
                    ti, tk, s = t
                    e.wait_ge(y_done, s + 1)
                    after(e, added, 16 * (s - 1))
                    e.tensor_scalar(Y[:, tk % 2, :], ps[:, 7, 0:H], eg[:, tk, 0:1], None, ALU.mult).then_inc(y_ready, 1)
            pipeline(e, DT // DU, DU, 5, step)

        def d_pool(e):
            e.wait_ge(scat[0], 128 * (NB // 2))
            e.wait_ge(scat[1], 128 * (NB // 2))
            e.wait_ge(x_out[0], 16 * (NB // 2))
            e.wait_ge(x_out[1], 16 * (NB // 2))
            e.wait_ge(c_pad, 64)
            e.wait_ge(res_out, 16 * NB)

            def step(i, k):
                if t := dtile(i, k, 0):
                    ti, tk, s = t
                    e.wait_ge(idr_ready, s + 1)
                    gate(e)
                    after(e, y_ready, s - DU + 1)
                    gate(e)
                    e.indirect_dma_start(out=eg[:, tk, :], out_offset=None, in_=lists,
                                         in_offset=bass.IndirectOffsetOnAxis(ap=idr[:, tk:tk + 1], axis=0)).then_inc(egath[tk % 2], 16)
                if t := dtile(i, k, 1):
                    ti, tk, s = t
                    e.wait_ge(tok_ready, s + 1)
                    gate(e)
                    after(e, xd_done, s - DU + 1)
                    gate(e)
                    e.indirect_dma_start(out=XG[:, tk, :], out_offset=None, in_=xrows,
                                         in_offset=bass.IndirectOffsetOnAxis(ap=toki[:, tk:tk + 1], axis=0)).then_inc(gath[tk], 16)
                if t := dtile(i, k, 6):
                    ti, tk, s = t
                    e.wait_ge(y_ready, s + 1)
                    gate(e)
                    after(e, added, 16 * s)
                    gate(e)
                    e.indirect_dma_start(out=out_ext, out_offset=bass.IndirectOffsetOnAxis(ap=toki[:, tk:tk + 1], axis=0),
                                         in_=Y[:, tk % 2, :], in_offset=None, compute_op=ALU.add).then_inc(added, 16)
            pipeline(e, DT // DU, DU, 6, step)
            e.wait_ge(added, 16 * DT)

        block = ctx.enter_context(nc.Block())

        @block.sync
        def _(e):
            a_sync(e)
            b_sync(e)
            c_sync(e)

        @block.gpsimd
        def _(e):
            a_pool(e)
            b_pool(e)
            c_pool(e)
            d_pool(e)

        @block.tensor
        def _(e):
            a_pe(e)
            b_pe(e)
            c_pe(e)
            d_pe(e)

        @block.scalar
        def _(e):
            a_act(e)
            b_act(e)
            c_act(e)
            d_act(e)

        @block.vector
        def _(e):
            a_dve(e)
            b_dve(e)
            c_dve(e)
            d_dve(e)


def host_arrays(I):
    import numpy as np
    A = {k: np.asarray(v) for k, v in I.items()}
    names = ("promoter", "co_exp", "gene_family", "peca_grn")
    c = np.ascontiguousarray
    f = np.float32
    t = "L0_tok_"
    r = {}
    r["ids"] = c(A["x"].reshape(NT, P, 1))
    r["vals"] = c(A["fside_BS_values"].reshape(NT, P, 1))
    r["homo"] = c(A[t + "homologous_index"].reshape(-1, 1))
    r["word"] = c(A[t + "word_emb"])
    r["tabs"] = np.concatenate([A[t + n + "_k"] for n in names], axis=1)
    r["wkT"] = c(np.stack([A[t + n + "_W"].T.reshape(2, HC, DK) for n in names]).transpose(2, 1, 0, 3))
    r["bk"] = c(np.stack([A[t + n + "_b"].reshape(2, HC) for n in names]).transpose(2, 1, 0))
    r["fc_w"] = c(A[t + "cat_fc_W"])
    r["fc_b"] = c(A[t + "cat_fc_b"].reshape(1, H))
    r["pj"] = np.concatenate([A[t + "cat_proj_W"], A[t + "cat_proj_b"].reshape(1, H), A[t + "tok_type_emb"][0:1]], axis=0)
    r["pos"] = c(A[t + "pos_emb"])
    vec = np.stack([A[t + "cat_ln_g"], A[t + "cat_ln_b"], A[t + "ln_g"], A[t + "ln_b"], A["L0_ffn_ln_gamma"], A["L0_ffn_ln_beta"]])
    r["lnp"] = c(np.broadcast_to(vec[None], (P, 6, H)))
    r["qkv"] = np.concatenate([A["L0_attn_qkv_weight"].T, A["L0_attn_qkv_bias"].reshape(1, -1)], axis=0)
    wo = np.zeros((P, NG, H), f)
    pw = A["L0_attn_proj_weight"].T
    for h in range(NH):
        wo[32 * (h % HG):32 * (h % HG) + HD, h // HG] = pw[HD * h:HD * h + HD]
    wo[HD, 0] = A["L0_attn_proj_bias"]
    r["wo"] = wo
    r["router"] = c(A["L0_ffn_router_w"])
    r["w1"] = c(A["L0_ffn_w1"].reshape(E, 2, HC, FF).transpose(2, 0, 1, 3))
    r["w2"] = c(A["L0_ffn_w2"].reshape(E, FC, P, H).transpose(2, 0, 1, 3))
    k = np.zeros((P, C_END), f)
    k[:, C_ID:C_ID + P] = np.eye(P)
    k[:, C_TRI:C_TRI + P] = np.triu(np.ones((P, P)), 1)
    k[:, C_ONE:C_ONE + P] = 1
    k[:, C_LOW:C_LOW + E * E] = np.tril(np.ones((E, E)), -1).reshape(1, -1)
    k[:, C_CAP:C_CAP + E] = CAP * np.arange(E)
    k[:, C_F:C_F + DT] = P * np.arange(DT)[None] + np.arange(P)[:, None]
    k[:, C_I:C_I + DT] = P * np.arange(DT)
    k[:, C_PAD] = E * CAP + np.arange(P)
    k[:, C_TOK:C_TOK + NT] = P * np.arange(NT)[None] + np.arange(P)[:, None]
    k[:, C_PADTOK] = NB * S + np.arange(P)
    r["const"] = k
    return r


def kernel(**inputs):
    import numpy as np
    import concourse.bacc as bacc
    from concourse.bass_utils import run_bass_kernel_spmd

    nc = bacc.Bacc("TRN2", target_bir_lowering=False, num_devices=1)
    arrays = {f"in_{n}": v for n, v in host_arrays(inputs).items()}
    aps = {n[3:]: nc.dram_tensor(n, v.shape, mybir.dt.from_np(v.dtype), kind="ExternalInput").ap() for n, v in arrays.items()}
    out = nc.dram_tensor("out_0", [NB * S + P, H], F32, kind="ExternalOutput").ap()
    build_program(nc, aps, out)
    got = run_bass_kernel_spmd(nc, [arrays], core_ids=[0]).results[0]["out_0"]
    return np.asarray(got)[0:NB * S].reshape(NB, S, H)
```

```python
from contextlib import ExitStack

import concourse.bass as bass
from concourse import mybir

F32 = mybir.dt.float32
BF16 = mybir.dt.bfloat16
I32 = mybir.dt.int32
ALU = mybir.AluOpType
ACT = mybir.ActivationFunctionType
AX = mybir.AxisListType
ds = bass.ds

P = 128
NB, S = 8, 512
TPB = S // P
NT = NB * TPB
H = 192
HC = H // 2
DK, NTAB = 64, 4
NH, HD = 12, 16
HG = 4
NG = NH // HG
E, FF = 8, 768
FC = FF // P
FH = FF // 2
CAP = NB * S
DU = 8
DT = 2 * NB * S // P + E
QP = 6
QPARTS = (0, 0, 1, 0, 2, 1)
KPARTS = (0, 1, 0, 2, 0, 1)
QROWS = QP * HD
NEG = 2
ALPHA = 0.35
SCALE = HD ** -0.5

FUSED = ((64, 0, 1), (0, 1, 2), (64, 2, 2), (0, 3, 3))

C_ID, C_TRI, C_ONE, C_LOW, C_CAP, C_F, C_I, C_PAD, C_TOK = 0, 128, 256, 384, 448, 456, 528, 600, 601
C_PADTOK = C_TOK + NT
C_END = C_PADTOK + 1


def after(eng, sem, n):
    if not isinstance(n, int) or n > 0:
        eng.wait_ge(sem, n)


def pipeline(eng, count, unroll, lag, step, peel=1):
    for i in range(peel):
        for k in range(unroll):
            step(i, k)
    with eng.Fori(peel, count) as i:
        for k in range(unroll):
            step(i, k)
    for k in range(lag):
        step(count + k // unroll, k % unroll)


def build_program(nc, a, out_ext):
    ctx = ExitStack()
    with ctx:
        def sb(name, shape, dt=F32):
            return ctx.enter_context(nc.sbuf_tensor(name, shape, dt))

        def sem(name):
            return ctx.enter_context(nc.semaphore(name))

        qkd = nc.dram_tensor("qk_parts", [2, 3, P, 3, S], BF16, kind="Internal").ap()

        lists = nc.dram_tensor("expert_lists", [E * CAP + P, 2], F32, kind="Internal").ap()
        xrows = nc.dram_tensor("expert_input_rows", [NB * S + P, H], F32, kind="Internal").ap()

        const = sb("const", [P, C_END])
        ident = const[:, C_ID:C_ID + P]
        identb = sb("identb", [P, P], BF16)
        eps = sb("eps", [P, 2])
        lnp = sb("lnp", [P, 6, H])
        pos = sb("pos", [P, TPB, H])
        wfc = sb("wfc", [P, 4, H])
        wpj = sb("wpj", [HC + 2, 2, H])
        wqkv = sb("wqkv", [HC + 1, 2, 3 * H])
        wo = sb("wo", [P, NG, H])
        wr = sb("wr", [HC, 2, E])
        hall = sb("hall", [P, NT, H])
        xT = sb("xT", [P, NB, 2, S])
        big = sb("big", [P, E * (2 * FF + FC * H)])
        smalls = sb("smalls", [P, 64])

        at = 0

        def part(n):
            nonlocal at
            at += n
            return big[:, at - n:at]
        KS = part(2 * NH * S // 2).bitcast(BF16).rearrange("p (b h s) -> p b h s", b=2, h=NH)
        QS = part(2 * NH * S // 2).bitcast(BF16).rearrange("p (b h s) -> p b h s", b=2, h=NH)
        PT = part(2 * HG * S).rearrange("p (b h s) -> p b h s", b=2, h=HG)
        VV = part(2 * TPB * NH * 32).rearrange("p (b t h d) -> p b t h d", b=2, t=TPB, h=NH)
        xs = part(2 * 2 * S).rearrange("p (b k s) -> p b k s", b=2, k=2)
        at = NH * S
        G = part(4 * 512).rearrange("p (b n) -> p b n", b=4)
        GT = part(2 * 512).rearrange("p (b n) -> p b n", b=2)
        c1 = part(2 * H).rearrange("p (b n) -> p b n", b=2)
        u = part(2 * H).rearrange("p (b n) -> p b n", b=2)
        ex = part(2 * H).rearrange("p (b n) -> p b n", b=2)
        sg = part(2 * H).rearrange("p (b n) -> p b n", b=2)
        den = part(2 * H).rearrange("p (b n) -> p b n", b=2)
        q = part(2 * H).rearrange("p (b n) -> p b n", b=2)
        qT = part(2 * 2 * P).rearrange("p (b k n) -> p b k n", b=2, k=2)
        emb = part(2 * H).rearrange("p (b n) -> p b n", b=2)
        c2 = part(2 * H).rearrange("p (b n) -> p b n", b=2)
        xn = part(2 * H).rearrange("p (b n) -> p b n", b=2)
        wc = part(NTAB * 2 * H).rearrange("p (i k n) -> p i k n", i=NTAB, k=2)
        wkT = part(2 * NTAB * DK).rearrange("p (k i n) -> p k i n", k=2, i=NTAB)
        bk = part(2 * NTAB).rearrange("p (k i) -> p k i", k=2)
        fcb = part(H)
        ids = part(4).bitcast(I32)
        hid = part(4).bitcast(I32)
        assert at <= E * (2 * FF + FC * H)

        OT = sb("OT", [P, 2, NG, S])
        qk32 = sb("qk32", [P, 2, S])
        parts = sb("parts", [P, 2, 3, S], BF16)
        rest = sb("rest", [P, S])
        pvs = sb("pvs", [P, S])
        sums = sb("sums", [P, S])
        rsum = sb("rsum", [P, S])
        nmx = sb("nmx", [P, 2, TPB, HG])
        npt = sb("npt", [P, 2, TPB, 2 * HG], BF16)
        nmT = sb("nmT", [2 * HG, 2, S], BF16)
        gmx = sb("gmx", [HC, NB, 2])
        st = sb("st", [P, 3, 2, 6])
        mv = sb("mv", [P, 3, 2, 2])
        lnv = sb("lnv", [P, 3, 2])
        rstd = sb("rstd", [P, 3, 2])
        csm = sb("csm", [HC, 12, 2])
        
        ps = ctx.enter_context(nc.psum_tensor("ps", [P, 8, 512], F32))

        s_const, s_wmm, s_wvec, s_watt = sem("constants_in"), sem("fuse_weights_in"), sem("vectors_in"), sem("attention_weights_in")
        s_zero = sem("fills_done")
        s_fused, s_wfc = sem("fused_weights_done"), sem("fused_weights_ready")
        s_identb = sem("identity_bf16_ready")
        g_id = [sem(f"ids_in{k}") for k in range(4)]
        g_val = [sem(f"values_in{k}") for k in range(4)]
        g_hid = [sem(f"shifted_ids_in{k}") for k in range(4)]
        g_we = [sem(f"word_rows_in{k}") for k in range(4)]
        g_tab = [sem(f"table_rows_in{k}") for k in range(4)]
        t1_done, gt_ready, fc_done = sem("t1_done"), sem("gt_ready"), sem("fc_done")
        bn_done = [sem(f"bn{n}_done") for n in range(3)]
        mv_ready = [sem(f"mean_var{n}_ready") for n in range(3)]
        ln_log = [sem(f"log_var{n}_done") for n in range(3)]
        rs_ready = [sem(f"rstd{n}_ready") for n in range(3)]
        den_ready, sg_log, sg_ready = sem("den_ready"), sem("sigmoid_log_done"), sem("sigmoid_ready")
        c1_done, u_ready, e_ready, q_ready = sem("c1_done"), sem("u_ready"), sem("e_ready"), sem("q_ready")
        t2_done, qt_ready, pj_done = sem("t2_done"), sem("qt_ready"), sem("pj_done")
        emb_ready, c2_done, h_ready, x_ready = sem("emb_ready"), sem("c2_done"), sem("h_ready"), sem("x_ready")
        t3_done, xt_ready, gmx_ready = sem("t3_done"), sem("xt_ready"), sem("gmx_ready")
        cs_dve, cs_act, w_scaled = sem("scale_steps_vector"), sem("scale_steps_scalar"), sem("weights_scaled")

        def gate(e):
            e.nop(nofuse=True)

        def tile_of(i, k, lag):
            k, i = (k - lag) % 4, i + (k - lag) // 4
            if isinstance(i, int) and not 0 <= i < NB:
                return None
            return i, k, 4 * i + k

        def a_sync(e):
            e.dma_start(const[:, :], a["const"]).then_inc(s_const, 16)
            for n in range(NTAB):
                lo = H + 1 + n * H
                e.dma_start(wc[0:HC, n, :, :], a["fc_w"][lo:lo + H, :].rearrange("(k p) c -> p k c", k=2)).then_inc(s_wmm, 16)
            e.dma_start(wkT[0:HC, :, :, :], a["wkT"]).then_inc(s_wmm, 16)
            e.dma_start(bk[0:HC, :, :], a["bk"]).then_inc(s_wmm, 16)
            e.dma_start(fcb[64:65, :], a["fc_b"]).then_inc(s_wmm, 16)
            e.dma_start(wfc[:, 0, :], a["fc_w"][0:P, :]).then_inc(s_wmm, 16)
            e.dma_start(wfc[0:64, 1, :], a["fc_w"][P:H, :]).then_inc(s_wmm, 16)
            e.dma_start(wfc[65:66, 3, :], a["fc_w"][H:H + 1, :]).then_inc(s_wmm, 16)

            def step(i, k):
                t = tile_of(i, k, 0)
                i, k, s = t
                after(e, g_hid[k], 16 * i)
                gate(e)
                after(e, g_we[k], 16 * i)
                gate(e)
                e.dma_start(ids[:, k:k + 1], a["ids"][ds(s, 1)].rearrange("t p c -> (t p) c")).then_inc(g_id[k], 16)
                if isinstance(i, int) and i == 0 and k == 0:
                    e.wait_ge(s_zero, 1)
                after(e, t1_done, s - 3)
                gate(e)
                e.dma_start(G[:, k, 449:450], a["vals"][ds(s, 1)].rearrange("t p c -> (t p) c")).then_inc(g_val[k], 16)
            pipeline(e, NB, 4, 0, step, 3)

        def a_pool(e):
            e.memset(G[:, :, :], 0.0).then_inc(s_id0, 1)
            e.wait_ge(s_id0, 1)
            e.memset(G[:, :, 448:449], 1.0).then_inc(s_zero, 1)
            e.wait_ge(s_zero, 1)
            e.memset(qT[96:98, :, 1, :], 1.0).then_inc(s_zero, 1)
            e.wait_ge(s_zero, 2)
            e.memset(eps[:, 0:1], 1e-5).then_inc(s_zero, 1)
            e.wait_ge(s_zero, 3)
            e.memset(eps[:, 1:2], 1e-12).then_inc(s_zero, 1)
            e.wait_ge(s_zero, 4)

            def step(i, k):
                t = tile_of(i, k, 0)
                if t is not None:
                    ti, tk, s = t
                    e.wait_ge(g_id[tk], 16 * (ti + 1))
                    after(e, g_tab[tk], 16 * ti)
                    gate(e)
                    e.indirect_dma_start(out=hid[:, tk:tk + 1], out_offset=None, in_=a["homo"],
                                         in_offset=bass.IndirectOffsetOnAxis(ap=ids[:, tk:tk + 1], axis=0)).then_inc(g_hid[tk], 16)
                    after(e, t1_done, s - 3)
                    gate(e)
                    e.indirect_dma_start(out=G[:, tk, 0:H], out_offset=None, in_=a["word"],
                                         in_offset=bass.IndirectOffsetOnAxis(ap=ids[:, tk:tk + 1], axis=0)).then_inc(g_we[tk], 16)
                t = tile_of(i, k, 1)
                if t is not None:
                    ti, tk, s = t
                    e.wait_ge(g_hid[tk], 16 * (ti + 1))
                    gate(e)
                    e.indirect_dma_start(out=G[:, tk, H:H + NTAB * DK], out_offset=None, in_=a["tabs"],
                                         in_offset=bass.IndirectOffsetOnAxis(ap=hid[:, tk:tk + 1], axis=0)).then_inc(g_tab[tk], 16)
            pipeline(e, NB, 4, 1, step, 3)

        def a_pe(e):
            e.wait_ge(s_wmm, 160)
            for n, (lo, bank, _) in enumerate(FUSED):
                for kt in range(2):
                    m = e.matmul(ps[lo:lo + DK, bank, 0:H], wkT[0:HC, kt, n, :], wc[0:HC, n, kt, :],
                                 start=kt == 0, stop=kt == 1)
                m.then_inc(s_fused, 1)
            for n in range(NTAB):
                for kt in range(2):
                    m = e.matmul(ps[64:65, 4, 0:H], bk[0:HC, kt, n:n + 1], wc[0:HC, n, kt, :],
                                 start=n == 0 and kt == 0, stop=n == NTAB - 1 and kt == 1)
            m.then_inc(s_fused, 1)
            e.wait_ge(s_const, 16)
            e.wait_ge(s_wfc, 5)

            def step(i, k):
                if t := tile_of(i, k, 10):
                    ti, tk, s = t
                    e.wait_ge(x_ready, s + 1)
                    after(e, xt_ready, s)
                    for kt in range(2):
                        m = e.transpose(ps[0:HC, 7, P * kt:P * kt + P], xn[:, tk % 2, HC * kt:HC * kt + HC], ident)
                    m.then_inc(t3_done, 1)
                if t := tile_of(i, k, 0):
                    ti, tk, s = t
                    e.wait_ge(g_we[tk], 16 * (ti + 1))
                    e.wait_ge(g_tab[tk], 16 * (ti + 1))
                    e.wait_ge(g_val[tk], 16 * (ti + 1))
                    after(e, gt_ready, s - 1)
                    for c in range(4):
                        m = e.transpose(ps[:, tk % 2, P * c:P * c + P], G[:, tk, P * c:P * c + P], ident)
                    m.then_inc(t1_done, 1)
                if t := tile_of(i, k, 1):
                    ti, tk, s = t
                    e.wait_ge(gt_ready, s + 1)
                    after(e, c1_done, s - 1)
                    for c in range(4):
                        K = P if c < 3 else 66
                        m = e.matmul(ps[:, 2 + tk % 2, 0:H], GT[0:K, tk % 2, P * c:P * c + P], wfc[0:K, c, :],
                                     start=c == 0, stop=c == 3)
                    m.then_inc(fc_done, 1)
                if t := tile_of(i, k, 6):
                    ti, tk, s = t
                    if isinstance(s, int) and s == 0:
                        e.wait_ge(s_wvec, 64)
                    e.wait_ge(qt_ready, s + 1)
                    after(e, emb_ready, s - 1)
                    e.matmul(ps[:, 5 + tk % 2, 0:H], qT[0:HC, tk % 2, 0, :], wpj[0:HC, 0, :], start=True, stop=False)
                    e.matmul(ps[:, 5 + tk % 2, 0:H], qT[0:HC + 2, tk % 2, 1, :], wpj[0:HC + 2, 1, :],
                             start=False, stop=True).then_inc(pj_done, 1)
                if t := tile_of(i, k, 5):
                    ti, tk, s = t
                    e.wait_ge(q_ready, s + 1)
                    after(e, qt_ready, s)
                    for kt in range(2):
                        m = e.transpose(ps[0:HC, 4, P * kt:P * kt + P], q[:, tk % 2, HC * kt:HC * kt + HC], ident)
                    m.then_inc(t2_done, 1)
            pipeline(e, NB, 4, 10, step, 3)

        def rsqrt(e, n, p, s, ecol):
            e.wait_ge(mv_ready[n], s + 1)
            e.activation(lnv[:, n, p:p + 1], mv[:, n, p, 1:2], ACT.Ln, bias=eps[:, ecol:ecol + 1]).then_inc(ln_log[n], 1)
            e.wait_ge(ln_log[n], s + 1)
            e.activation(rstd[:, n, p:p + 1], lnv[:, n, p:p + 1], ACT.Exp, scale=-0.5).then_inc(rs_ready[n], 1)

        def a_act(e):
            e.preload_act_table_set("natural_log_exp_and_others")
            e.dma_start(lnp[:, :, :], a["lnp"]).then_inc(s_wvec, 16)
            e.dma_start(pos[:, :, :], a["pos"].rearrange("(t p) c -> p t c", p=P)).then_inc(s_wvec, 16)
            e.dma_start(wpj[0:HC, 0, :], a["pj"][0:HC, :]).then_inc(s_wvec, 16)
            e.dma_start(wpj[:, 1, :], a["pj"][HC:2 * HC + 2, :]).then_inc(s_wvec, 16)
            e.dma_start(wqkv[0:HC, 0, :], a["qkv"][0:HC, :]).then_inc(s_watt, 16)
            e.dma_start(wqkv[:, 1, :], a["qkv"][HC:2 * HC + 1, :]).then_inc(s_watt, 16)
            e.dma_start(wo[:, :, :], a["wo"]).then_inc(s_watt, 16)
            e.dma_start(wr[:, :, :], a["router"].rearrange("(k p) n -> p k n", k=2)).then_inc(s_watt, 16)
            e.wait_ge(s_fused, 5)
            for lo, bank, chunk in FUSED:
                e.activation(wfc[lo:lo + DK, chunk, :], ps[lo:lo + DK, bank, 0:H], ACT.Copy).then_inc(s_wfc, 1)
            e.wait_ge(s_const, 16)
            e.activation(identb[:, :], ident, ACT.Copy).then_inc(s_identb, 1)
            e.wait_ge(s_zero, 4)

            def step(i, k):
                if t := tile_of(i, k, 10):
                    ti, tk, s = t
                    e.wait_ge(t3_done, s + 1)
                    e.activation(xT[0:HC, ds(ti, 1), :, P * tk:P * tk + P].rearrange("p b k n -> p (b k) n"),
                                 ps[0:HC, 7, 0:2 * P].rearrange("p (k n) -> p k n", k=2), ACT.Copy).then_inc(xt_ready, 1)
                if t := tile_of(i, k, 0):
                    ti, tk, s = t
                    e.wait_ge(t1_done, s + 1)
                    after(e, fc_done, s - 1)
                    e.activation(GT[:, tk % 2, :], ps[:, tk % 2, :], ACT.Copy).then_inc(gt_ready, 1)
                if t := tile_of(i, k, 2):
                    rsqrt(e, 0, t[1] % 2, t[2], 0)
                if t := tile_of(i, k, 3):
                    ti, tk, s = t
                    e.wait_ge(u_ready, s + 1)
                    after(e, q_ready, s - 1)
                    e.activation(ex[:, tk % 2, :], u[:, tk % 2, :], ACT.Exp, scale=-1.702).then_inc(e_ready, 1)
                if t := tile_of(i, k, 4):
                    ti, tk, s = t
                    e.wait_ge(den_ready, s + 1)
                    e.activation(sg[:, tk % 2, :], den[:, tk % 2, :], ACT.Ln).then_inc(sg_log, 1)
                    e.wait_ge(sg_log, s + 1)
                    e.activation(ex[:, tk % 2, :], sg[:, tk % 2, :], ACT.Exp, scale=-1.0).then_inc(sg_ready, 1)
                if t := tile_of(i, k, 5):
                    ti, tk, s = t
                    e.wait_ge(t2_done, s + 1)
                    after(e, pj_done, s - 1)
                    e.activation(qT[0:HC, tk % 2, :, :], ps[0:HC, 4, 0:2 * P].rearrange("p (k n) -> p k n", k=2), ACT.Copy).then_inc(qt_ready, 1)
                if t := tile_of(i, k, 7):
                    rsqrt(e, 1, t[1] % 2, t[2], 1)
                if t := tile_of(i, k, 8):
                    rsqrt(e, 2, t[1] % 2, t[2], 0)
            pipeline(e, NB, 4, 10, step, 3)

        def row_stats(e, n, p, s, x):
            gate(e)
            e.bn_stats(st[:, n, p, :], x).then_inc(bn_done[n], 1)

        def mean_var(e, n, p, s):
            e.wait_ge(bn_done[n], s + 1)
            after(e, rs_ready[n], s - 1)
            gate(e)
            e.bn_aggr(mv[:, n, p, :], st[:, n, p, :]).then_inc(mv_ready[n], 1)

        def a_dve(e):
            e.wait_ge(s_fused, 5)
            e.tensor_tensor(wfc[64:65, 3, :], ps[64:65, 4, 0:H], fcb[64:65, :], ALU.add).then_inc(s_wfc, 1)
            e.wait_ge(s_watt, 64)
            e.tensor_reduce(csm[:, 1, :], wqkv[0:HC, :, :], AX.X, ALU.max, apply_absolute_value=True).then_inc(cs_dve, 1)
            e.wait_ge(s_wvec, 64)

            def step(i, k):
                t1, t2, t3, t4, t5 = (tile_of(i, k, lag) for lag in (2, 3, 4, 5, 7))
                t6, t7, t8 = (tile_of(i, k, lag) for lag in (8, 9, 10))
                if t4:
                    ti, tk, s = t4
                    e.wait_ge(sg_ready, s + 1)
                    after(e, t2_done, s - 1)
                    e.tensor_tensor(q[:, tk % 2, :], u[:, tk % 2, :], ex[:, tk % 2, :], ALU.mult).then_inc(q_ready, 1)
                if t1:
                    ti, tk, s = t1
                    e.wait_ge(fc_done, s + 1)
                    row_stats(e, 0, tk % 2, s, ps[:, 2 + tk % 2, 0:H])
                if t6:
                    ti, tk, s = t6
                    p = tk % 2
                    e.wait_ge(mv_ready[1], s + 1)
                    e.scalar_tensor_tensor(c2[:, p, :], emb[:, p, :], mv[:, 1, p, 0:1], lnp[:, 2, :],
                                           ALU.subtract, ALU.mult).then_inc(c2_done, 1)
                if t1:
                    mean_var(e, 0, t1[1] % 2, t1[2])
                if t6:
                    ti, tk, s = t6
                    e.wait_ge(c2_done, s + 1)
                    e.wait_ge(rs_ready[1], s + 1)
                    e.scalar_tensor_tensor(hall[:, ds(s, 1), :].rearrange("p a n -> p (a n)"), c2[:, tk % 2, :],
                                           rstd[:, 1, tk % 2:tk % 2 + 1], lnp[:, 3, :], ALU.mult, ALU.add).then_inc(h_ready, 1)
                if t1:
                    ti, tk, s = t1
                    p = tk % 2
                    e.wait_ge(mv_ready[0], s + 1)
                    e.scalar_tensor_tensor(c1[:, p, :], ps[:, 2 + p, 0:H], mv[:, 0, p, 0:1], lnp[:, 0, :],
                                           ALU.subtract, ALU.mult).then_inc(c1_done, 1)
                if t6:
                    ti, tk, s = t6
                    e.wait_ge(h_ready, s + 1)
                    row_stats(e, 2, tk % 2, s, hall[:, ds(s, 1), :].rearrange("p a n -> p (a n)"))
                if t2:
                    ti, tk, s = t2
                    p = tk % 2
                    e.wait_ge(c1_done, s + 1)
                    e.wait_ge(rs_ready[0], s + 1)
                    after(e, q_ready, s - 1)
                    e.scalar_tensor_tensor(u[:, p, :], c1[:, p, :], rstd[:, 0, p:p + 1], lnp[:, 1, :],
                                           ALU.mult, ALU.add).then_inc(u_ready, 1)
                if t6:
                    mean_var(e, 2, t6[1] % 2, t6[2])
                if t5:
                    ti, tk, s = t5
                    e.wait_ge(pj_done, s + 1)
                    e.tensor_tensor(emb[:, tk % 2, :], ps[:, 5 + tk % 2, 0:H], pos[:, tk, :], ALU.add).then_inc(emb_ready, 1)
                if t3:
                    ti, tk, s = t3
                    e.wait_ge(e_ready, s + 1)
                    e.tensor_scalar(den[:, tk % 2, :], ex[:, tk % 2, :], 1e18, 1.0, ALU.min, ALU.add).then_inc(den_ready, 1)
                if t5:
                    ti, tk, s = t5
                    e.wait_ge(emb_ready, s + 1)
                    row_stats(e, 1, tk % 2, s, emb[:, tk % 2, :])
                if t7:
                    ti, tk, s = t7
                    p = tk % 2
                    e.wait_ge(mv_ready[2], s + 1)
                    e.wait_ge(rs_ready[2], s + 1)
                    after(e, t3_done, s - 1)
                    e.tensor_scalar(xn[:, p, :], hall[:, ds(s, 1), :].rearrange("p a n -> p (a n)"), mv[:, 2, p, 0:1],
                                    rstd[:, 2, p:p + 1], ALU.subtract, ALU.mult).then_inc(x_ready, 1)
                if t5:
                    mean_var(e, 1, t5[1] % 2, t5[2])
                if t8 and t8[1] == 3:
                    ti, tk, s = t8
                    e.wait_ge(xt_ready, s + 1)
                    e.tensor_reduce(gmx[:, ds(ti, 1), :].rearrange("p a n -> p (a n)"),
                                    xT[0:HC, ds(ti, 1), :, :].rearrange("p a k n -> p (a k) n"),
                                    AX.X, ALU.max, apply_absolute_value=True).then_inc(gmx_ready, 1)
            pipeline(e, NB, 4, 10, step, 3)
            smoothing(e)

        def smoothing(e):
            gm, wm, lg, lw, z, v, p2, d1, d2, up, cs, ics = (csm[:, n, :] for n in range(12))
            e.wait_ge(gmx_ready, NB)
            e.tensor_reduce(gm, gmx[:, :, :].rearrange("p b k -> p k b"), AX.X, ALU.max).then_inc(cs_dve, 1)
            e.wait_ge(cs_act, 2)
            e.tensor_scalar(lw, lw, -(1.0 - ALPHA), None, ALU.mult).then_inc(cs_dve, 1)
            e.wait_ge(cs_dve, 3)
            e.scalar_tensor_tensor(z, lg, ALPHA, lw, ALU.mult, ALU.add).then_inc(cs_dve, 1)
            e.wait_ge(cs_act, 3)
            e.tensor_scalar(p2.bitcast(I32), v.bitcast(I32), 0x7F800000, None, ALU.bitwise_and).then_inc(cs_dve, 1)
            e.wait_ge(cs_dve, 5)
            e.tensor_tensor(d1, v, p2, ALU.subtract).then_inc(cs_dve, 1)
            e.scalar_tensor_tensor(d2, p2, 2.0, v, ALU.mult, ALU.subtract).then_inc(cs_dve, 1)
            e.wait_ge(cs_dve, 7)
            e.tensor_tensor(up, d1, d2, ALU.is_gt).then_inc(cs_dve, 1)
            e.wait_ge(cs_dve, 8)
            e.scalar_tensor_tensor(cs, up, 1.0, p2, ALU.add, ALU.mult).then_inc(cs_dve, 1)
            e.wait_ge(cs_dve, 9)
            e.reciprocal(ics, cs).then_inc(cs_dve, 1)
            for kt in range(2):
                e.tensor_scalar(wqkv[0:HC, kt, :], wqkv[0:HC, kt, :], cs[:, kt:kt + 1], None, ALU.mult).then_inc(w_scaled, 1)
            e.wait_ge(cs_dve, 10)

        def smoothing_act(e):
            gm, wm, lg, lw, z, v = (csm[:, n, :] for n in range(6))
            e.wait_ge(cs_dve, 2)
            e.activation(lg, gm, ACT.Ln).then_inc(cs_act, 1)
            e.activation(lw, wm, ACT.Ln).then_inc(cs_act, 1)
            e.wait_ge(cs_dve, 4)
            e.activation(v, z, ACT.Exp).then_inc(cs_act, 1)

        s_id0 = sem("zero_fill_done")
        ics = csm[:, 11, :]

        S1, S2, PVB, MISC = 0, 2, 6, 7
        xs_ready, qk_done, v_done = sem("xs_ready"), sem("qk_done"), sem("v_done")
        qk_copied, rest_done, mid_done, parts_ready = sem("qk_copied"), sem("rest_done"), sem("mid_done"), sem("parts_ready")
        stored = [sem(f"parts_stored{m}") for m in range(3)]
        stack_in = [sem(f"stack_in{k}") for k in range(2)]
        v_ready, b_fill = sem("v_ready"), sem("attention_fills_done")
        p1_done, max_done, nh_done, np_ready = sem("p1_done"), sem("max_done"), sem("neg_high_done"), sem("neg_parts_ready")
        nt_done, nmt_ready = sem("neg_turned"), sem("neg_rows_ready")
        neg_in = [sem(f"neg_rows_in{k}") for k in range(2)]
        p2_done, exp_done, pv_done, pvs_ready = sem("p2_done"), sem("exp_done"), sem("pv_done"), sem("pvs_ready")
        sum_log, rsum_ready = sem("sum_log_done"), sem("reciprocal_sums_ready")
        shf_done, ot_ready, h2_ready = sem("sums_spread"), sem("ot_ready"), sem("h2_ready")
        op_done = [sem(f"out_proj_done{k}") for k in range(2)]

        def batch_of(i, kb, lag):
            i, kb = i + (kb - lag) // 2, (kb - lag) % 2
            if isinstance(i, int) and not 0 <= 2 * i + kb < NB:
                return None
            return i, kb, 2 * i + kb

        def group_of(i, m, lag):
            i, m = i + (m - lag) // 6, (m - lag) % 6
            if isinstance(i, int) and not 0 <= 6 * i + m < NB * NG:
                return None
            return i, m, 6 * i + m

        def upto(n, most):
            return max(0, min(n, most)) if isinstance(n, int) else n

        def misc_free(e, qk, v, nt, op):
            after(e, qk_copied, 2 * qk)
            after(e, v_ready, v)
            after(e, nmt_ready, nt)
            after(e, h2_ready, op)

        def qk_job(e, i, kb, b, m, counts):
            e.wait_ge(xs_ready, 2 * b + 2)
            misc_free(e, *counts)
            e.matmul(ps[:, MISC, :], wqkv[0:HC, 0, P * m:P * m + P], xs[0:HC, kb, 0, :], start=True, stop=False)
            e.matmul(ps[:, MISC, :], wqkv[0:HC + 1, 1, P * m:P * m + P], xs[0:HC + 1, kb, 1, :],
                     start=False, stop=True).then_inc(qk_done, 1)

        def v_job(e, i, kb, b, jj, counts):
            misc_free(e, *counts)
            for t in range(2):
                sl = slice(P * (2 * jj + t), P * (2 * jj + t) + P)
                e.matmul(ps[:, MISC, H * t:H * t + H], xs[0:HC, kb, 0, sl], wqkv[0:HC, 0, 2 * H:3 * H], start=True, stop=False)
                m = e.matmul(ps[:, MISC, H * t:H * t + H], xs[0:HC + 1, kb, 1, sl], wqkv[0:HC + 1, 1, 2 * H:3 * H],
                             start=False, stop=True)
            m.then_inc(v_done, 1)

        def b_steps(e, step):
            pipeline(e, NB // 2, 2, 2, step)

        def b_pe(e):
            e.wait_ge(w_scaled, 2)
            e.wait_ge(b_fill, 3)
            e.wait_ge(s_identb, 1)
            def p1(n, m, k, uu):
                kb, g, h = m // 3, m % 3, k // 2
                qt = 2 * (k % 2) + uu
                after(e, max_done, 16 * n + 2 * k + uu - 1)
                e.matmul(ps[:, S1 + uu, :], QS[0:QROWS, kb, HG * g + h, P * qt:P * qt + P], KS[0:QROWS, kb, HG * g + h, :],
                         start=True, stop=True).then_inc(p1_done, 1)

            def p2(n, m, k):
                kb, g, kt, hp = m // 3, m % 3, k // 2, k % 2
                after(e, exp_done, 8 * n + k - 1)
                for uu in range(2):
                    h = HG * g + 2 * hp + uu
                    mm = e.matmul(ps[:, S2 + 2 * (k % 2) + uu, :], KS[0:QROWS + NEG, kb, h, P * kt:P * kt + P],
                                  QS[0:QROWS + NEG, kb, h, :], start=True, stop=True)
                mm.then_inc(p2_done, 1)

            def pv(n, m, kt):
                kb, g = m // 3, m % 3
                e.wait_ge(exp_done, 8 * n + 2 * kt + 2)
                if kt == 0:
                    after(e, pvs_ready, n)
                for h in range(HG):
                    mm = e.matmul(ps[32 * h:32 * h + 32, PVB, :], VV[:, kb, kt, HG * g + h, :], PT[:, kt % 2, h, :],
                                  start=kt == 0, stop=kt == TPB - 1)
                mm.then_inc(pv_done, 1)

            def step(i, kb):
                b = 2 * i + kb - 1
                nxt, att, prv = (batch_of(i, kb, lag) for lag in range(3))
                nqk, nv, nop = 3 * upto(b + 1, NB), 2 * upto(b + 1, NB), 2 * upto(b - 1, NB)
                for g in range(3):
                    cur, neg, old, last = (group_of(i, 3 * kb + g, lag) for lag in (3, 4, 5, 6))
                    nnt = upto(3 * b + g, NB * NG)
                    dqk, dv = (3, 2) if nxt else (0, 0)
                    if att and g == 0:
                        e.wait_ge(stack_in[att[1]], 192 * (att[0] + 1))
                    if att and g == 2:
                        e.wait_ge(v_ready, 2 * att[2] + 2)
                    if old:
                        e.wait_ge(neg_in[old[1] % 2], 32 * (3 * old[0] + old[1] // 2 + 1))
                    for k in range(8):
                        if cur:
                            p1(cur[2], cur[1], k, 0)
                        if old:
                            p2(old[2], old[1], k)
                        if cur:
                            p1(cur[2], cur[1], k, 1)
                        if k == 1 and last:
                            pv(last[2], last[1], 3)
                        if k in (3, 5, 7) and old:
                            pv(old[2], old[1], k // 2 - 1)
                        if k == 2 and neg:
                            ng, nm = neg[2], neg[1]
                            e.wait_ge(np_ready, ng + 1)
                            misc_free(e, nqk + (dqk if g else 0), nv, ng, nop)
                            for t in range(TPB):
                                mm = e.transpose(ps[0:2 * HG, MISC, 0:S // 2].bitcast(BF16)[:, P * t:P * t + P],
                                                 npt[:, nm % 2, t, :], identb[:, :])
                            mm.then_inc(nt_done, 1)
                        if nxt:
                            if g == 0 and k in (4, 5, 6):
                                qk_job(e, *nxt, k - 4, (nqk + k - 4, nv, nnt, nop))
                            if g == 2 and k in (3, 4):
                                v_job(e, *nxt, k - 3, (nqk + 3, nv + k - 3, nnt, nop))
                        if prv and g == 2 and k in (5, 7):
                            jj = (k - 5) // 2
                            pi, pk, pb = prv
                            e.wait_ge(ot_ready, 3 * pb + 3)
                            misc_free(e, nqk + dqk, nv + dv, nnt, nop + jj)
                            for t in range(2):
                                sl = slice(P * (2 * jj + t), P * (2 * jj + t) + P)
                                for gg in range(NG):
                                    mm = e.matmul(ps[:, MISC, H * t:H * t + H], OT[:, pk, gg, sl], wo[:, gg, :],
                                                  start=gg == 0, stop=gg == NG - 1)
                            mm.then_inc(op_done[pk], 1)
            b_steps(e, step)

        def qk_evac(e, m, i, kb):
            x = 6 * i + 3 * kb + m
            p = (3 * kb + m) % 2
            e.wait_ge(qk_done, x + 1)
            after(e, parts_ready, x - 1)
            e.activation(qk32[:, p, :], ps[:, MISC, :], ACT.Copy).then_inc(qk_copied, 1)
            if isinstance(x, int):
                if x >= 2:
                    e.wait_ge(stored[(m - 2) % 3], 16 * ((x - 2) // 3 + 1))
            else:
                e.wait_ge(stored[(m - 2) % 3], 16 * (2 * i + kb + (m - 2) // 3 + 1))
            e.activation(parts[:, p, 0, :], ps[:, MISC, :], ACT.Copy).then_inc(qk_copied, 1)

        def v_evac(e, jj, kb, x, used):
            e.wait_ge(v_done, x + 1)
            after(e, pv_done, used)
            e.activation(VV[:, kb, 2 * jj:2 * jj + 2, :, 0:HD],
                         ps[:, MISC, 0:2 * H].rearrange("p (t h d) -> p t h d", t=2, h=NH), ACT.Copy).then_inc(v_ready, 1)

        def b_act(e):
            smoothing_act(e)

            def step(i, kb):
                nxt = batch_of(i, kb, 0)
                for g in range(3):
                    neg, old, last = (group_of(i, 3 * kb + g, lag) for lag in (4, 5, 6))
                    for k in range(8):
                        if old:
                            n, kt, hp = old[2], k // 2, k % 2
                            e.wait_ge(p2_done, 8 * n + k + 1)
                            if hp == 0:
                                after(e, pv_done, 4 * n + kt - 1)
                            e.activation(PT[:, kt % 2, 2 * hp:2 * hp + 2, :], ps[:, S2 + 2 * (k % 2):S2 + 2 * (k % 2) + 2, :],
                                         ACT.Exp, scale=SCALE).then_inc(exp_done, 1)
                        if k == 1 and last:
                            e.wait_ge(pv_done, 4 * last[2] + 4)
                            after(e, ot_ready, last[2])
                            e.activation(pvs[:, :], ps[:, PVB, :], ACT.Copy).then_inc(pvs_ready, 1)
                        if k == 2 and neg:
                            e.wait_ge(nt_done, neg[2] + 1)
                            after(e, neg_in[neg[1] % 2], 32 * (3 * neg[0] + neg[1] // 2))
                            e.activation(nmT[:, neg[1] % 2, :], ps[0:2 * HG, MISC, 0:S // 2].bitcast(BF16),
                                         ACT.Copy).then_inc(nmt_ready, 1)
                        if k == 3 and last:
                            e.wait_ge(shf_done, last[2] + 1)
                            e.activation(sums[:, :], sums[:, :], ACT.Ln).then_inc(sum_log, 1)
                            e.wait_ge(sum_log, last[2] + 1)
                            e.activation(rsum[:, :], sums[:, :], ACT.Exp, scale=-1.0).then_inc(rsum_ready, 1)
                        if k == 3 and neg:
                            e.wait_ge(nmt_ready, neg[2] + 1)
                            nk, ng = neg[1] // 3, neg[1] % 3
                            for pt in range(NEG):
                                e.dma_start(QS[QROWS + pt:QROWS + pt + 1, nk, HG * ng:HG * ng + HG, :],
                                            nmT[HG * pt:HG * pt + HG, neg[1] % 2, :]).then_inc(neg_in[neg[1] % 2], 16)
                        if nxt:
                            if g == 0 and k in (4, 5, 6):
                                qk_evac(e, k - 4, nxt[0], nxt[1])
                            if g == 2 and k in (3, 4):
                                v_evac(e, k - 3, nxt[1], 2 * nxt[2] + k - 3, 4 * NG * (nxt[2] - 1))
            b_steps(e, step)

        def split(e, i, kb, m):
            x = 6 * i + 3 * kb + m
            p = (3 * kb + m) % 2
            e.wait_ge(qk_copied, 2 * x + 2)
            after(e, parts_ready, x)
            e.tensor_tensor(rest[:, :], qk32[:, p, :], parts[:, p, 0, :], ALU.subtract).then_inc(rest_done, 1)
            e.wait_ge(rest_done, x + 1)
            gate(e)
            e.tensor_copy(parts[:, p, 1, :], rest[:, :]).then_inc(mid_done, 1)
            e.wait_ge(mid_done, x + 1)
            e.tensor_tensor(parts[:, p, 2, :], rest[:, :], parts[:, p, 1, :], ALU.subtract).then_inc(parts_ready, 1)

        def b_pool(e):
            e.memset(VV[:, :, :, :, HD:32], 1.0).then_inc(b_fill, 1)
            e.wait_ge(b_fill, 1)
            e.memset(KS[QROWS:QROWS + NEG, :, :, :], 1.0).then_inc(b_fill, 1)
            e.wait_ge(b_fill, 2)
            e.memset(xs[HC:HC + 1, :, 1, :], 1.0).then_inc(b_fill, 1)
            e.wait_ge(b_fill, 3)

            for m in range(3):
                split(e, 0, 1, m)
            with e.Fori(1, NB // 2) as i:
                for kb in range(2):
                    for m in range(3):
                        split(e, i, kb, m)

        def b_sync(e):
            def stacks(i, kb):
                if not isinstance(i, int):
                    after(e, stack_in[kb], 192 * i)
                    gate(e)
                for m in range(3):
                    x = 6 * i + 3 * kb + m
                    e.wait_ge(parts_ready, x + 1)
                    gate(e)
                    e.dma_start(qkd[kb, m], parts[:, (3 * kb + m) % 2, :, :]).then_inc(stored[m], 16)
                for m in range(3):
                    e.wait_ge(stored[m], 16 * (2 * i + kb + 1))
                    gate(e)
                after(e, p2_done, 8 * 3 * (2 * i + kb - 1))
                gate(e)
                rows = qkd[kb].rearrange("m p j s -> (m p) j s")
                for which, dst, prt in ((0, QS, QPARTS), (1, KS, KPARTS)):
                    src = rows[H * which:H * which + H].rearrange("(h d) j s -> d h j s", h=NH)
                    for j in range(QP):
                        e.dma_start(dst[HD * j:HD * j + HD, kb, :, :], src[:, :, prt[j], :]).then_inc(stack_in[kb], 16)
            for kb in range(2):
                stacks(0, kb)
            with e.Fori(1, NB // 2) as i:
                for kb in range(2):
                    stacks(i, kb)

        def b_dve(e):
            e.wait_ge(b_fill, 3)

            def x_in(i, kb, b):
                after(e, qk_done, 3 * (b - 1))
                after(e, v_done, 2 * (b - 1))
                for kt in range(2):
                    e.tensor_scalar(xs[0:HC, kb, kt, :], xT[0:HC, ds(b, 1), kt, :].rearrange("p a n -> p (a n)"),
                                    ics[:, kt:kt + 1], None, ALU.mult).then_inc(xs_ready, 1)

            def step(i, kb):
                nxt, prv = batch_of(i, kb, 0), batch_of(i, kb, 2)
                if nxt:
                    x_in(*nxt)
                    if isinstance(i, int) and i == 0 and kb == 0:
                        for m in range(3):
                            split(e, 0, 0, m)
                for g in range(3):
                    cur, last = group_of(i, 3 * kb + g, 3), group_of(i, 3 * kb + g, 6)
                    for k in range(8):
                        if cur:
                            n, m = cur[2], cur[1]
                            if k == 0:
                                after(e, nt_done, n - 1)
                            for uu in range(2):
                                x = 16 * n + 2 * k + uu
                                e.wait_ge(p1_done, x + 1)
                                e.tensor_reduce(nmx[:, m % 2, 2 * (k % 2) + uu, k // 2:k // 2 + 1], ps[:, S1 + uu, :],
                                                AX.X, ALU.max, negate=True).then_inc(max_done, 1)
                        if k == 2 and last:
                            n = last[2]
                            e.wait_ge(pvs_ready, n + 1)
                            gate(e)
                            e.stream_shuffle(sums[:, :], pvs[:, :], [HD] * 32).then_inc(shf_done, 1)
                        if k == 4 and last:
                            n, m = last[2], last[1]
                            lk, lg = m // 3, m % 3
                            e.wait_ge(rsum_ready, n + 1)
                            after(e, op_done[lk], 2 * last[0])
                            e.tensor_tensor(OT[:, lk, lg, :], pvs[:, :], rsum[:, :], ALU.mult).then_inc(ot_ready, 1)
                        if prv and g == 2 and k in (6, 7):
                            jj = k - 6
                            e.wait_ge(op_done[prv[1]], 2 * prv[0] + jj + 1)
                            hh = hall[:, ds(4 * prv[2] + 2 * jj, 2), :].rearrange("p a n -> p (a n)")
                            e.tensor_tensor(hh, ps[:, MISC, 0:2 * H], hh, ALU.add).then_inc(h2_ready, 1)
                    if cur:
                        n, m = cur[2], cur[1]
                        e.wait_ge(max_done, 16 * n + 16)
                        e.tensor_copy(npt[:, m % 2, :, 0:HG], nmx[:, m % 2, :, :]).then_inc(nh_done, 1)
                        e.wait_ge(nh_done, n + 1)
                        e.tensor_tensor(npt[:, m % 2, :, HG:2 * HG], nmx[:, m % 2, :, :], npt[:, m % 2, :, 0:HG],
                                        ALU.subtract).then_inc(np_ready, 1)
            b_steps(e, step)


        room = xT[:, :, :, :].rearrange("p b k n -> p (b k n)")
        at = 0

        def room_part(n):
            nonlocal at
            at += n
            assert at <= NB * 2 * S
            return room[:, at - n:at]
        hs = room_part(2 * TPB * H).rearrange("p (b t n) -> p b t n", b=2, t=TPB)
        xf = room_part(2 * TPB * H).rearrange("p (b t n) -> p b t n", b=2, t=TPB)
        entry = room_part(2 * TPB * 2 * 2).rearrange("p (b t a n) -> p b t a n", b=2, t=TPB, a=2)
        xfT = room_part(2 * 2 * P).rearrange("p (b k n) -> p b k n", b=2, k=2)
        c5 = rest[:, 0:2 * H].rearrange("p (b n) -> p b n", b=2)
        sel = room_part(2 * TPB * E).rearrange("p (b t n) -> p b t n", b=2, t=TPB)
        cum = room_part(2 * E).rearrange("p (b n) -> p b n", b=2)
        bsel = room_part(E)
        above = room_part(TPB * E * E)
        equal = room_part(TPB * E * E)
        probs, dif, rk, first, second, slot, tmp, tmp2 = (
            room_part(TPB * E).rearrange("p (t n) -> p t n", t=TPB) for _ in range(8))
        mx, sm, rs, pa, pb_, dn, rd, sa, sb_ = (room_part(TPB) for _ in range(9))
        st4 = room_part(2 * TPB * 6).rearrange("p (l t n) -> p l t n", l=2, t=TPB)
        mv4 = room_part(2 * TPB * 2).rearrange("p (l t n) -> p l t n", l=2, t=TPB)
        lv4 = room_part(2 * TPB).rearrange("p (l t) -> p l t", l=2)
        rs4 = room_part(2 * TPB).rearrange("p (l t) -> p l t", l=2)
        rp1 = room_part(TPB)
        nmr = room_part(2 * TPB).rearrange("p (l t) -> p l t", l=2)
        slots = room_part(2 * TPB * 2).bitcast(I32).rearrange("p (b t a) -> p b t a", b=2, t=TPB)
        zero = room_part(E * CAP * 2 // P)
        pad_entry = room_part(2)
        cnt, ntl, start, stop_, shift = (room_part(E) for _ in range(5))
        nti = room_part(E).bitcast(I32)
        idx = room_part(DT)
        tef = room_part(DT)
        lt_, in_ = room_part(DT), room_part(DT)
        idi = room_part(DT).bitcast(I32)
        tei = room_part(DT).bitcast(I32)
        idr = room_part(DU).bitcast(I32)
        toki = room_part(DU).bitcast(I32)
        eg = room_part(DU * 2).rearrange("p (b n) -> p b n", b=DU)
        XG = parts[:, :, :, :].rearrange("p b j s -> p (b j s)").bitcast(F32).rearrange("p (b n) -> p b n", b=DU)
        ott = OT[:, :, :, :].rearrange("p b g s -> p (b g s)")
        hT = ott[:, 0:2 * FF].rearrange("p (b c n) -> p b c n", b=2, c=FC)
        xgT = pvs[:, :].rearrange("p (b k n) -> p b k n", b=2, k=2)
        Y = sums[:, 0:2 * H].rearrange("p (b n) -> p b n", b=2)
        w1s = room[:, 0:2 * 2 * FF].rearrange("p (b k n) -> p b k n", b=2, k=2)
        w1 = big[:, 0:E * 2 * FF].rearrange("p (e k n) -> p e k n", e=E, k=2)
        w2 = big[:, E * 2 * FF:].rearrange("p (e c n) -> p e c n", e=E, c=FC)

        s_w = sem("expert_weights_in")
        c_zero, c_pad = sem("zero_rows_ready"), sem("padding_rows_stored")
        bn4, mv4_ready = [sem(f"route_bn{n}_done") for n in range(2)], [sem(f"route_mean_var{n}_ready") for n in range(2)]
        log4, rs4_ready = [sem(f"route_log{n}_done") for n in range(2)], [sem(f"route_rstd{n}_ready") for n in range(2)]
        aff_ready = [sem(f"scale_offset{n}_ready") for n in range(2)]
        hs_ready, res_ready, res_out, xhat_ready = sem("hs_ready"), sem("residual_ready"), sem("residual_stored"), sem("xhat_ready")
        c5_done, xff_ready = sem("c5_done"), sem("xff_ready")
        xt4_done, xt4_ready, lg_done = sem("xff_turned"), sem("xff_turned_ready"), sem("logits_done")
        route, rexp, rank_done, slots_ready = sem("routing_steps"), sem("routing_exp_done"), sem("rank_done"), sem("slots_ready")
        x_out = [sem(f"x_rows_stored{k}") for k in range(2)]
        scat = [sem(f"rows_listed{k}") for k in range(2)]
        cnt_done, plan, plan_ready = sem("counts_done"), sem("plan_steps"), sem("plan_ready")

        def c_begin(e):
            e.wait_ge(h2_ready, 2 * NB)

        def c_sync(e):
            c_begin(e)
            e.wait_ge(c_zero, 3)
            e.dma_start(lists[0:E * CAP, :].rearrange("(p n) c -> p (n c)", p=P), zero).then_inc(c_pad, 16)
            e.dma_start(lists[E * CAP:E * CAP + P, :], pad_entry).then_inc(c_pad, 16)
            e.dma_start(xrows[NB * S:NB * S + P, :], zero[:, 0:H]).then_inc(c_pad, 16)
            e.dma_start(out_ext[NB * S:NB * S + P, :], zero[:, 0:H]).then_inc(c_pad, 16)

            for x in range(E):
                e.dma_start(w1[0:HC, x, :, :], a["w1"][:, x, :, :]).then_inc(s_w, 16)
                e.dma_start(w2[:, x, :, :], a["w2"][:, x, :, :]).then_inc(s_w, 16)
            def step(i, kb):
                b = 2 * i + kb
                e.wait_ge(res_ready, TPB * b + TPB)
                e.dma_start(out_ext[ds(S * b, S), :].rearrange("(t p) c -> p t c", p=P),
                            hall[:, ds(TPB * b, TPB), :]).then_inc(res_out, 16)
                e.wait_ge(xff_ready, 2 * b + 2)
                e.dma_start(xrows[ds(S * b, S), :].rearrange("(t p) c -> p t c", p=P), xf[:, kb, :, :]).then_inc(x_out[kb], 16)
            pipeline(e, NB // 2, 2, 0, step)

        def c_pe(e):
            c_begin(e)

            def step(i, kb):
                if nb := batch_of(i, kb, 1):
                    i1, p, b = nb

                    def turn(t):
                        s = TPB * b + t
                        if t % 2 == 0:
                            e.wait_ge(xff_ready, 2 * b + t // 2 + 1)
                        after(e, xt4_ready, s - 1)
                        for kt in range(2):
                            m = e.transpose(ps[0:HC, t % 2, P * kt:P * kt + P], xf[:, p, t, HC * kt:HC * kt + HC], ident)
                        m.then_inc(xt4_done, 1)

                    def logits(t):
                        e.wait_ge(xt4_ready, TPB * b + t + 1)
                        if t == 0:
                            after(e, route, R * (b - 2) + 2)
                        for kt in range(2):
                            m = e.matmul(ps[:, 2 + p, E * t:E * t + E], xfT[0:HC, t % 2, kt, :], wr[:, kt, :],
                                         start=kt == 0, stop=kt == 1)
                        m.then_inc(lg_done, 1)
                    turn(0)
                    for t in range(TPB):
                        if t + 1 < TPB:
                            turn(t + 1)
                        logits(t)
                if pb := batch_of(i, kb, 2):
                    i2, p, b = pb
                    one = const[:, C_ONE:C_ONE + P]
                    e.wait_ge(route, R * b + R_SEL)
                    e.matmul(ps[:, 4 + p, 0:TPB * E], const[:, C_TRI:C_TRI + P],
                             sel[:, p, :, :].rearrange("p t n -> p (t n)"), start=True, stop=False)
                    for t in range(1, TPB):
                        e.matmul(ps[:, 4 + p, E * t:TPB * E], one,
                                 sel[:, p, 0:TPB - t, :].rearrange("p t n -> p (t n)"), start=False, stop=False)
                    for t in range(TPB):
                        m = e.matmul(ps[:, 4 + p, E * t:E * t + E], one, cum[:, p, :], start=False, stop=t == TPB - 1)
                    m.then_inc(rank_done, 1)
            pipeline(e, NB // 2, 2, 2, step, 2)
            e.wait_ge(route, R * NB)
            e.matmul(ps[:, 6, 0:E], const[:, C_ONE:C_ONE + P], cum[:, NB % 2, :], start=True, stop=True).then_inc(cnt_done, 1)

        R = 23
        R_EXP, R_SEL = 2, 14

        def c_act(e):
            c_begin(e)

            def norm(n, b):
                e.wait_ge(mv4_ready[n], TPB * b + TPB)
                e.activation(lv4[:, n, :], mv4[:, n, :, 1], ACT.Ln, bias=eps[:, 0:1]).then_inc(log4[n], 1)
                e.wait_ge(log4[n], b + 1)
                e.activation(rs4[:, n, :], lv4[:, n, :], ACT.Exp, scale=-0.5).then_inc(rs4_ready[n], 1)

            def step(i, kb):
                nb, tb, pb = batch_of(i, kb, 0), batch_of(i, kb, 1), batch_of(i, kb, 2)
                if nb:
                    norm(0, nb[2])
                if pb:
                    e.wait_ge(route, R * pb[2] + R_EXP)
                    e.activation(probs[:, :, :], dif[:, :, :], ACT.Exp).then_inc(rexp, 1)
                if nb:
                    b = nb[2]
                    e.wait_ge(aff_ready[0], 2 * b + 2)
                    gate(e)
                    for t in range(TPB):
                        e.activation(hs[:, kb, t, :], hall[:, ds(TPB * b + t, 1), :].rearrange("p a n -> p (a n)"),
                                     ACT.Identity, bias=nmr[:, 0, t:t + 1], scale=rs4[:, 0, t:t + 1]).then_inc(hs_ready, 1)
                if tb:
                    for t in range(TPB):
                        s = TPB * tb[2] + t
                        e.wait_ge(xt4_done, s + 1)
                        after(e, lg_done, s - 1)
                        e.activation(xfT[0:HC, t % 2, :, :], ps[0:HC, t % 2, 0:2 * P].rearrange("p (k n) -> p k n", k=2),
                                     ACT.Copy).then_inc(xt4_ready, 1)
                if nb:
                    b = nb[2]
                    norm(1, b)
                    e.wait_ge(aff_ready[1], b + 1)
                    after(e, x_out[kb], 16 * nb[0])
                    after(e, xt4_done, TPB * (b - 1))
                    for t in range(TPB):
                        e.activation(xf[:, kb, t, :], hs[:, kb, t, :], ACT.Identity, bias=nmr[:, 1, t:t + 1],
                                     scale=rs4[:, 1, t:t + 1]).then_inc(xhat_ready, 1)
                    e.wait_ge(hs_ready, TPB * b + TPB)
                    gate(e)
                    for t in range(TPB):
                        x = hall[:, ds(TPB * b + t, 1), :].rearrange("p a n -> p (a n)")
                        e.activation(x, x, ACT.Identity, bias=nmr[:, 0, t:t + 1], scale=rp1[:, t:t + 1]).then_inc(res_ready, 1)
            pipeline(e, NB // 2, 2, 2, step, 2)

        def c_pool(e):
            c_begin(e)
            e.memset(zero, 0.0).then_inc(c_zero, 1)
            e.wait_ge(c_zero, 1)
            e.memset(pad_entry[:, 0:1], 0.0).then_inc(c_zero, 1)
            e.wait_ge(c_zero, 2)
            e.tensor_copy(pad_entry[:, 1:2], const[:, C_PADTOK:C_PADTOK + 1]).then_inc(c_zero, 1)
            e.wait_ge(c_pad, 64)

            def step(i, kb):
                if pb := batch_of(i, kb, 3):
                    b = pb[2]
                    e.wait_ge(slots_ready, b + 1)
                    gate(e)
                    for t in range(TPB):
                        for x in range(2):
                            e.indirect_dma_start(out=lists, out_offset=bass.IndirectOffsetOnAxis(ap=slots[:, pb[1], t, x:x + 1], axis=0),
                                                 in_=entry[:, pb[1], t, x, :], in_offset=None).then_inc(scat[pb[1]], 16)
            pipeline(e, NB // 2, 2, 3, step, 2)

        def c_dve(e):
            c_begin(e)
            e.memset(cum[:, 0, :], 0.0).then_inc(c_fill, 1)
            e.wait_ge(c_fill, 1)

            def spread(x):
                return x.unsqueeze(2).broadcast_to((P, TPB, E))

            def row_stats4(n, b, src):
                for t in range(TPB):
                    if n == 0:
                        gate(e)
                    e.bn_stats(st4[:, n, t, :], src(t)).then_inc(bn4[n], 1)
                e.wait_ge(bn4[n], TPB * b + TPB)
                after(e, rs4_ready[n], b)
                gate(e)
                for t in range(TPB):
                    e.bn_aggr(mv4[:, n, t, :], st4[:, n, t, :]).then_inc(mv4_ready[n], 1)

            def offsets(n, b):
                e.wait_ge(mv4_ready[n], TPB * b + TPB)
                e.wait_ge(rs4_ready[n], b + 1)
                after(e, (res_ready, xhat_ready)[n], TPB * b)
                if n == 0:
                    e.tensor_scalar(rp1, rs4[:, 0, :], 1.0, None, ALU.add).then_inc(aff_ready[0], 1)
                e.scalar_tensor_tensor(nmr[:, n, :], mv4[:, n, :, 0], -1.0, rs4[:, n, :], ALU.mult, ALU.mult).then_inc(aff_ready[n], 1)

            def gamma_beta(p, b):
                for hf in range(2):
                    x = xf[:, p, 2 * hf:2 * hf + 2, :]
                    c = c5[:, :, :]
                    e.wait_ge(xhat_ready, TPB * b + 2 * hf + 2)
                    after(e, xff_ready, 2 * b + hf)
                    e.tensor_tensor(c, x, lnp[:, 4, :].unsqueeze(1).broadcast_to((P, 2, H)), ALU.mult).then_inc(c5_done, 1)
                    e.wait_ge(c5_done, 2 * b + hf + 1)
                    e.tensor_tensor(x, c, lnp[:, 5, :].unsqueeze(1).broadcast_to((P, 2, H)), ALU.add).then_inc(xff_ready, 1)

            def choose(i, p, b, first_part):
                n = 0 if first_part else 2

                def did(ins):
                    nonlocal n
                    n += 1
                    ins.then_inc(route, 1)

                def have(k):
                    e.wait_ge(route, R * b + k)
                if first_part:
                    lg = ps[:, 2 + p, 0:TPB * E].rearrange("p (t n) -> p t n", t=TPB)
                    e.wait_ge(lg_done, TPB * b + TPB)
                    did(e.tensor_reduce(mx, lg, AX.X, ALU.max))
                    have(1)
                    did(e.tensor_tensor(dif, lg, spread(mx), ALU.subtract))
                    return
                e.wait_ge(rexp, b + 1)
                did(e.tensor_reduce(sm, probs, AX.X, ALU.add))
                have(3)
                did(e.reciprocal(rs, sm))
                have(4)
                did(e.tensor_tensor(probs, probs, spread(rs), ALU.mult))
                have(5)
                q4 = probs.unsqueeze(2).broadcast_to((P, TPB, E, E))
                p4 = probs.unsqueeze(3).broadcast_to((P, TPB, E, E))
                ab = above.rearrange("p (t e f) -> p t e f", t=TPB, e=E)
                eq = equal.rearrange("p (t e f) -> p t e f", t=TPB, e=E)
                low = const[:, C_LOW:C_LOW + E * E].unsqueeze(1).broadcast_to((P, TPB, E * E))
                did(e.tensor_tensor(eq, q4, p4, ALU.is_equal))
                did(e.tensor_tensor(ab, q4, p4, ALU.is_gt))
                have(6)
                eqt = equal.rearrange("p (t e) -> p t e", t=TPB)
                did(e.tensor_tensor(eqt, eqt, low, ALU.mult))
                have(8)
                did(e.tensor_tensor(above, above, equal, ALU.add))
                have(9)
                did(e.tensor_reduce(rk, ab, AX.X, ALU.add))
                have(10)
                did(e.tensor_scalar(sel[:, p, :, :], rk, 2.0, None, ALU.is_lt))
                did(e.tensor_scalar(first, rk, 0.0, None, ALU.is_equal))
                have(11)
                did(e.tensor_reduce(bsel, sel[:, p, :, :].rearrange("p t n -> p n t"), AX.X, ALU.add))
                did(e.tensor_scalar(second, rk, 1.0, None, ALU.is_equal))
                have(13)
                after(e, rank_done, b)
                did(e.tensor_tensor(cum[:, (p + 1) % 2, :], cum[:, p, :], bsel, ALU.add))
                assert n == 15

            def place(i, p, b):
                n = 15

                def did(ins):
                    nonlocal n
                    n += 1
                    ins.then_inc(route, 1)

                def have(k):
                    e.wait_ge(route, R * b + k)
                have(15)
                did(e.tensor_tensor(tmp, first, probs, ALU.mult))
                e.wait_ge(rank_done, b + 1)
                did(e.tensor_tensor(slot, ps[:, 4 + p, 0:TPB * E].rearrange("p (t n) -> p t n", t=TPB),
                                    const[:, C_CAP:C_CAP + E].unsqueeze(1).broadcast_to((P, TPB, E)), ALU.add))
                did(e.tensor_tensor(tmp2, second, probs, ALU.mult))
                have(16)
                did(e.tensor_reduce(pa, tmp, AX.X, ALU.add))
                have(18)
                did(e.tensor_reduce(pb_, tmp2, AX.X, ALU.add))
                did(e.tensor_tensor(first, first, slot, ALU.mult))
                have(20)
                did(e.tensor_tensor(dn, pa, pb_, ALU.add))
                did(e.tensor_tensor(second, second, slot, ALU.mult))
                assert n == R
                have(22)
                e.reciprocal(rd, dn).then_inc(slot_sum, 1)
                e.tensor_reduce(sa, first, AX.X, ALU.add).then_inc(slot_sum, 1)
                have(R)
                e.tensor_reduce(sb_, second, AX.X, ALU.add).then_inc(slot_sum, 1)
                e.wait_ge(slot_sum, 3 * b + 3)
                after(e, scat[p], 128 * i)
                for x, pr_ in enumerate((pa, pb_)):
                    e.tensor_tensor(entry[:, p, :, x, 0], pr_, rd, ALU.mult).then_inc(gates_in, 1)
                    e.tensor_copy(entry[:, p, :, x, 1], const[:, ds(C_TOK + TPB * b, TPB)]).then_inc(gates_in, 1)
                e.tensor_copy(slots[:, p, :, 0], sa).then_inc(gates_in, 1)
                e.wait_ge(gates_in, 5 * b + 5)
                e.tensor_copy(slots[:, p, :, 1], sb_).then_inc(slots_ready, 1)

            def step(i, kb):
                nb, tb, cb, pb = (batch_of(i, kb, lag) for lag in range(4))
                if nb:
                    b = nb[2]
                    row_stats4(0, b, lambda t: hall[:, ds(TPB * b + t, 1), :].rearrange("p a n -> p (a n)"))
                if tb:
                    gamma_beta(tb[1], tb[2])
                if pb:
                    place(*pb)
                if cb:
                    choose(*cb, True)
                if nb:
                    offsets(0, b)
                if cb:
                    choose(*cb, False)
                if nb:
                    e.wait_ge(hs_ready, TPB * b + TPB)
                    gate(e)
                    row_stats4(1, b, lambda t: hs[:, kb, t, :])
                    offsets(1, b)
            pipeline(e, NB // 2, 2, 3, step, 2)
            make_plan(e)
        c_fill, slot_sum, gates_in = sem("routing_fills_done"), sem("slot_sums_done"), sem("gates_in_rows")

        def make_plan(e):
            n = 0

            def did(ins):
                nonlocal n
                n += 1
                ins.then_inc(plan, 1)
                e.wait_ge(plan, n)
            e.wait_ge(cnt_done, 1)
            did(e.tensor_copy(cnt, ps[:, 6, 0:E]))
            did(e.tensor_copy(nti, cnt))
            did(e.tensor_scalar(nti, nti, P - 1, None, ALU.add))
            did(e.tensor_scalar(nti, nti, P.bit_length() - 1, None, ALU.arith_shift_right))
            did(e.tensor_copy(ntl, nti))
            did(e.tensor_scalar(ntl, ntl, float(P), None, ALU.mult))
            pair = above[:, 0:E * E].rearrange("p (e f) -> p e f", e=E)
            did(e.tensor_tensor(pair, ntl.unsqueeze(1).broadcast_to((P, E, E)),
                                const[:, C_LOW:C_LOW + E * E].rearrange("p (e f) -> p e f", e=E), ALU.mult))
            did(e.tensor_reduce(start, pair, AX.X, ALU.add))
            did(e.tensor_tensor(stop_, start, cnt, ALU.add))
            did(e.tensor_tensor(shift, const[:, C_CAP:C_CAP + E], start, ALU.subtract))
            did(e.tensor_scalar(shift, shift, const[:, C_PAD:C_PAD + 1], None, ALU.subtract))
            f, tile_row = const[:, C_F:C_F + DT], const[:, C_I:C_I + DT]
            did(e.tensor_scalar(idx, f, 0.0, const[:, C_PAD:C_PAD + 1], ALU.mult, ALU.add))
            did(e.tensor_scalar(tef, tile_row, start[:, 1:2], None, ALU.is_ge))
            for x in range(E):
                did(e.tensor_scalar(lt_, f, stop_[:, x:x + 1], None, ALU.is_lt))
                did(e.scalar_tensor_tensor(in_, f, start[:, x:x + 1], lt_, ALU.is_ge, ALU.mult))
                did(e.scalar_tensor_tensor(lt_, f, shift[:, x:x + 1], in_, ALU.add, ALU.mult))
                did(e.tensor_tensor(idx, idx, lt_, ALU.add))
                if x >= 2:
                    did(e.scalar_tensor_tensor(tef, tile_row, start[:, x:x + 1], tef, ALU.is_ge, ALU.add))
            did(e.tensor_copy(tei, tef))
            e.tensor_copy(idi, idx).then_inc(plan_ready, 1)

        idr_ready, tok_ready = sem("tile_entries_chosen"), sem("gate_and_tokens_kept")
        egath = [sem(f"entries_in{k}") for k in range(2)]
        gath = [sem(f"x_rows_in{k}") for k in range(DU)]
        xd_done, xd_ready, hd_done, silu_done = sem("x_turned"), sem("x_turned_ready"), sem("inner_done"), sem("silu_done")
        w1_ready = [sem(f"expert_w1_chosen{k}") for k in range(2)]
        y_done, y_ready = sem("y_done"), sem("y_ready")
        added = sem("rows_added")

        def dtile(i, k, lag):
            k, i = (k - lag) % DU, i + (k - lag) // DU
            if isinstance(i, int) and not 0 <= i < DT // DU:
                return None
            return i, k, DU * i + k

        def choose_w1(e, kt, tk, s):
            after(e, hd_done, 2 * (s - 1))
            gate(e)
            x = e.value_load(tei[0:1, ds(s, 1)], min_val=0, max_val=E - 1)
            return w1s[0:HC, tk % 2, kt, :], w1[0:HC, ds(x, 1), kt, :].rearrange("p a n -> p (a n)")

        def d_pe(e):
            e.wait_ge(s_w, 2 * E * 16)
            e.wait_ge(plan_ready, 1)

            def step(i, k):
                if t := dtile(i, k, 3):
                    ti, tk, s = t
                    e.wait_ge(xd_ready, s + 1)
                    e.wait_ge(w1_ready[0], s + 1)
                    e.wait_ge(w1_ready[1], s + 1)
                    for hf in range(2):
                        after(e, silu_done, 2 * (s - 2) + hf + 1)
                        for c in range(3):
                            f0 = FH * hf + P * c
                            for kt in range(2):
                                m = e.matmul(ps[:, 1 + 2 * (tk % 2) + hf, P * c:P * c + P], w1s[0:HC, tk % 2, kt, f0:f0 + P],
                                             xgT[0:HC, tk % 2, kt, :], start=kt == 0, stop=kt == 1)
                        m.then_inc(hd_done, 1)
                if t := dtile(i, k, 2):
                    ti, tk, s = t
                    e.wait_ge(gath[tk], 16 * (ti + 1))
                    after(e, xd_ready, s)
                    for kt in range(2):
                        m = e.transpose(ps[0:HC, 0, P * kt:P * kt + P], XG[:, tk, HC * kt:HC * kt + HC], ident)
                    m.then_inc(xd_done, 1)
                if t := dtile(i, k, 4):
                    ti, tk, s = t
                    ex_ = e.value_load(tei[0:1, ds(s, 1)], min_val=0, max_val=E - 1)
                    after(e, y_ready, s - 1)
                    for c in range(FC):
                        if c % 3 == 0:
                            e.wait_ge(silu_done, 2 * s + c // 3 + 1)
                        m = e.matmul(ps[:, 6 + tk % 2, 0:H], hT[:, tk % 2, c, :], w2[:, ds(ex_, 1), c, :].rearrange("p a n -> p (a n)"),
                                     start=c == 0, stop=c == FC - 1)
                    m.then_inc(y_done, 1)
            pipeline(e, DT // DU, DU, 4, step)

        def d_act(e):
            def step(i, k):
                if t := dtile(i, k, 3):
                    ti, tk, s = t
                    for hf in range(2):
                        e.wait_ge(hd_done, 2 * s + hf + 1)
                        after(e, y_done, s - 1)
                        e.activation(hT[:, tk % 2, 3 * hf:3 * hf + 3, :],
                                     ps[:, 1 + 2 * (tk % 2) + hf, 0:FH].rearrange("p (c n) -> p c n", c=3), ACT.Silu).then_inc(silu_done, 1)
                        if hf == 0 and (t2 := dtile(i, k, 2)):
                            dst, src = choose_w1(e, 1, t2[1], t2[2])
                            e.activation(dst, src, ACT.Copy).then_inc(w1_ready[1], 1)
                elif t2 := dtile(i, k, 2):
                    dst, src = choose_w1(e, 1, t2[1], t2[2])
                    e.activation(dst, src, ACT.Copy).then_inc(w1_ready[1], 1)
                if t := dtile(i, k, 2):
                    ti, tk, s = t
                    e.wait_ge(xd_done, s + 1)
                    after(e, hd_done, 2 * (s - 2) + 2)
                    e.activation(xgT[0:HC, tk % 2, :, :], ps[0:HC, 0, 0:2 * P].rearrange("p (k n) -> p k n", k=2),
                                 ACT.Copy).then_inc(xd_ready, 1)
            e.wait_ge(rexp, NB)
            e.preload_act_table_set("silu_and_others")
            e.wait_ge(s_w, 2 * E * 16)
            e.wait_ge(plan_ready, 1)
            pipeline(e, DT // DU, DU, 3, step)

        def d_dve(e):
            e.wait_ge(s_w, 2 * E * 16)
            e.wait_ge(plan_ready, 1)
            e.wait_ge(x_out[0], 16 * (NB // 2))
            e.wait_ge(x_out[1], 16 * (NB // 2))

            def step(i, k):
                if t := dtile(i, k, 0):
                    ti, tk, s = t
                    after(e, y_ready, s - DU + 1)
                    e.tensor_copy(idr[:, tk:tk + 1], idi[:, ds(s, 1)]).then_inc(idr_ready, 1)
                if t := dtile(i, k, 1):
                    ti, tk, s = t
                    e.wait_ge(egath[tk % 2], 16 * (DU // 2 * ti + tk // 2 + 1))
                    after(e, added, 16 * (s - DU + 1))
                    e.tensor_copy(toki[:, tk:tk + 1], eg[:, tk, 1:2]).then_inc(tok_ready, 1)
                if t := dtile(i, k, 2):
                    dst, src = choose_w1(e, 0, t[1], t[2])
                    e.tensor_copy(dst, src).then_inc(w1_ready[0], 1)
                if t := dtile(i, k, 4):
                    ti, tk, s = t
                    e.wait_ge(y_done, s + 1)
                    after(e, added, 16 * (s - 1))
                    e.tensor_scalar(Y[:, tk % 2, :], ps[:, 6 + tk % 2, 0:H], eg[:, tk, 0:1], None, ALU.mult).then_inc(y_ready, 1)
            pipeline(e, DT // DU, DU, 4, step)

        def d_pool(e):
            e.wait_ge(scat[0], 128 * (NB // 2))
            e.wait_ge(scat[1], 128 * (NB // 2))
            e.wait_ge(x_out[0], 16 * (NB // 2))
            e.wait_ge(x_out[1], 16 * (NB // 2))
            e.wait_ge(c_pad, 64)
            e.wait_ge(res_out, 16 * NB)

            def step(i, k):
                if t := dtile(i, k, 0):
                    ti, tk, s = t
                    e.wait_ge(idr_ready, s + 1)
                    gate(e)
                    after(e, y_ready, s - DU + 1)
                    gate(e)
                    e.indirect_dma_start(out=eg[:, tk, :], out_offset=None, in_=lists,
                                         in_offset=bass.IndirectOffsetOnAxis(ap=idr[:, tk:tk + 1], axis=0)).then_inc(egath[tk % 2], 16)
                if t := dtile(i, k, 1):
                    ti, tk, s = t
                    e.wait_ge(tok_ready, s + 1)
                    gate(e)
                    after(e, xd_done, s - DU + 1)
                    gate(e)
                    e.indirect_dma_start(out=XG[:, tk, :], out_offset=None, in_=xrows,
                                         in_offset=bass.IndirectOffsetOnAxis(ap=toki[:, tk:tk + 1], axis=0)).then_inc(gath[tk], 16)
                if t := dtile(i, k, 5):
                    ti, tk, s = t
                    e.wait_ge(y_ready, s + 1)
                    gate(e)
                    after(e, added, 16 * s)
                    gate(e)
                    e.indirect_dma_start(out=out_ext, out_offset=bass.IndirectOffsetOnAxis(ap=toki[:, tk:tk + 1], axis=0),
                                         in_=Y[:, tk % 2, :], in_offset=None, compute_op=ALU.add).then_inc(added, 16)
            pipeline(e, DT // DU, DU, 5, step)
            e.wait_ge(added, 16 * DT)

        block = ctx.enter_context(nc.Block())

        @block.sync
        def _(e):
            a_sync(e)
            b_sync(e)
            c_sync(e)

        @block.gpsimd
        def _(e):
            a_pool(e)
            b_pool(e)
            c_pool(e)
            d_pool(e)

        @block.tensor
        def _(e):
            a_pe(e)
            b_pe(e)
            c_pe(e)
            d_pe(e)

        @block.scalar
        def _(e):
            a_act(e)
            b_act(e)
            c_act(e)
            d_act(e)

        @block.vector
        def _(e):
            a_dve(e)
            b_dve(e)
            c_dve(e)
            d_dve(e)


def host_arrays(I):
    import numpy as np
    A = {k: np.asarray(v) for k, v in I.items()}
    names = ("promoter", "co_exp", "gene_family", "peca_grn")
    c = np.ascontiguousarray
    f = np.float32
    t = "L0_tok_"
    r = {}
    r["ids"] = c(A["x"].reshape(NT, P, 1))
    r["vals"] = c(A["fside_BS_values"].reshape(NT, P, 1))
    r["homo"] = c(A[t + "homologous_index"].reshape(-1, 1))
    r["word"] = c(A[t + "word_emb"])
    r["tabs"] = np.concatenate([A[t + n + "_k"] for n in names], axis=1)
    r["wkT"] = c(np.stack([A[t + n + "_W"].T.reshape(2, HC, DK) for n in names]).transpose(2, 1, 0, 3))
    r["bk"] = c(np.stack([A[t + n + "_b"].reshape(2, HC) for n in names]).transpose(2, 1, 0))
    r["fc_w"] = c(A[t + "cat_fc_W"])
    r["fc_b"] = c(A[t + "cat_fc_b"].reshape(1, H))
    r["pj"] = np.concatenate([A[t + "cat_proj_W"], A[t + "cat_proj_b"].reshape(1, H), A[t + "tok_type_emb"][0:1]], axis=0)
    r["pos"] = c(A[t + "pos_emb"])
    vec = np.stack([A[t + "cat_ln_g"], A[t + "cat_ln_b"], A[t + "ln_g"], A[t + "ln_b"], A["L0_ffn_ln_gamma"], A["L0_ffn_ln_beta"]])
    r["lnp"] = c(np.broadcast_to(vec[None], (P, 6, H)))
    r["qkv"] = np.concatenate([A["L0_attn_qkv_weight"].T, A["L0_attn_qkv_bias"].reshape(1, -1)], axis=0)
    wo = np.zeros((P, NG, H), f)
    pw = A["L0_attn_proj_weight"].T
    for h in range(NH):
        wo[32 * (h % HG):32 * (h % HG) + HD, h // HG] = pw[HD * h:HD * h + HD]
    wo[HD, 0] = A["L0_attn_proj_bias"]
    r["wo"] = wo
    r["router"] = c(A["L0_ffn_router_w"])
    r["w1"] = c(A["L0_ffn_w1"].reshape(E, 2, HC, FF).transpose(2, 0, 1, 3))
    r["w2"] = c(A["L0_ffn_w2"].reshape(E, FC, P, H).transpose(2, 0, 1, 3))
    k = np.zeros((P, C_END), f)
    k[:, C_ID:C_ID + P] = np.eye(P)
    k[:, C_TRI:C_TRI + P] = np.triu(np.ones((P, P)), 1)
    k[:, C_ONE:C_ONE + P] = 1
    k[:, C_LOW:C_LOW + E * E] = np.tril(np.ones((E, E)), -1).reshape(1, -1)
    k[:, C_CAP:C_CAP + E] = CAP * np.arange(E)
    k[:, C_F:C_F + DT] = P * np.arange(DT)[None] + np.arange(P)[:, None]
    k[:, C_I:C_I + DT] = P * np.arange(DT)
    k[:, C_PAD] = E * CAP + np.arange(P)
    k[:, C_TOK:C_TOK + NT] = P * np.arange(NT)[None] + np.arange(P)[:, None]
    k[:, C_PADTOK] = NB * S + np.arange(P)
    r["const"] = k
    return r


def kernel(**inputs):
    import numpy as np
    import concourse.bacc as bacc
    from concourse.bass_utils import run_bass_kernel_spmd

    nc = bacc.Bacc("TRN2", target_bir_lowering=False, num_devices=1)
    arrays = {f"in_{n}": v for n, v in host_arrays(inputs).items()}
    aps = {n[3:]: nc.dram_tensor(n, v.shape, mybir.dt.from_np(v.dtype), kind="ExternalInput").ap() for n, v in arrays.items()}
    out = nc.dram_tensor("out_0", [NB * S + P, H], F32, kind="ExternalOutput").ap()
    build_program(nc, aps, out)
    got = run_bass_kernel_spmd(nc, [arrays], core_ids=[0]).results[0]["out_0"]
    return np.asarray(got)[0:NB * S].reshape(NB, S, H)
```

```python
from contextlib import ExitStack

import concourse.bass as bass
from concourse import mybir

F32 = mybir.dt.float32
BF16 = mybir.dt.bfloat16
I32 = mybir.dt.int32
ALU = mybir.AluOpType
ACT = mybir.ActivationFunctionType
AX = mybir.AxisListType
ds = bass.ds

P = 128
NB, S = 8, 512
TPB = S // P
NT = NB * TPB
H = 192
HC = H // 2
DK, NTAB = 64, 4
NH, HD = 12, 16
HG = 4
NG = NH // HG
E, FF = 8, 768
FC = FF // P
FH = FF // 2
CAP = NB * S
DU = 8
DT = 2 * NB * S // P + E
QP = 6
QPARTS = (0, 0, 1, 0, 2, 1)
KPARTS = (0, 1, 0, 2, 0, 1)
QROWS = QP * HD
NEG = 2
ROUTING = 2600
ALPHA = 0.35
SCALE = HD ** -0.5

FUSED = ((64, 0, 1), (0, 1, 2), (64, 2, 2), (0, 3, 3))

C_ID, C_TRI, C_ONE, C_LOW, C_CAP, C_F, C_PAD, C_TOK = 0, 128, 256, 384, 448, 456, 528, 529
C_PADTOK = C_TOK + NT
C_END = C_PADTOK + 1


def after(eng, sem, n):
    if not isinstance(n, int) or n > 0:
        eng.wait_ge(sem, n)


def pipeline(eng, count, unroll, lag, step, peel=1):
    for i in range(peel):
        for k in range(unroll):
            step(i, k)
    with eng.Fori(peel, count) as i:
        for k in range(unroll):
            step(i, k)
    for k in range(lag):
        step(count + k // unroll, k % unroll)


def build_program(nc, a, out_ext):
    ctx = ExitStack()
    with ctx:
        def sb(name, shape, dt=F32):
            return ctx.enter_context(nc.sbuf_tensor(name, shape, dt))

        def sem(name):
            return ctx.enter_context(nc.semaphore(name))

        qkd = nc.dram_tensor("qk_parts", [2, 3, P, 3, S], BF16, kind="Internal").ap()

        lists = nc.dram_tensor("expert_lists", [E * CAP + P, 2], F32, kind="Internal").ap()
        xrows = nc.dram_tensor("expert_input_rows", [NB * S + P, H], F32, kind="Internal").ap()

        const = sb("const", [P, C_END])
        ident = const[:, C_ID:C_ID + P]
        identb = sb("identb", [P, P], BF16)
        eps = sb("eps", [P, 2])
        lnp = sb("lnp", [P, 6, H])
        pos = sb("pos", [P, TPB, H])
        wfc = sb("wfc", [P, 4, H])
        wpj = sb("wpj", [HC + 2, 2, H])
        wqkv = sb("wqkv", [HC + 1, 2, 3 * H])
        wo = sb("wo", [P, NG, H])
        wr = sb("wr", [HC, 2, E])
        hall = sb("hall", [P, NT, H])
        xT = sb("xT", [P, NB, 2, S])
        big = sb("big", [P, E * (2 * FF + FC * H)])

        at = 0

        def part(n):
            nonlocal at
            at += n
            return big[:, at - n:at]
        KS = part(2 * NH * S // 2).bitcast(BF16).rearrange("p (b h s) -> p b h s", b=2, h=NH)
        QS = part(2 * NH * S // 2).bitcast(BF16).rearrange("p (b h s) -> p b h s", b=2, h=NH)
        PT = part(2 * HG * S).rearrange("p (b h s) -> p b h s", b=2, h=HG)
        VV = part(2 * TPB * NH * 32).rearrange("p (b t h d) -> p b t h d", b=2, t=TPB, h=NH)
        xs = part(2 * 2 * S).rearrange("p (b k s) -> p b k s", b=2, k=2)
        at = NH * S
        G = part(4 * 512).rearrange("p (b n) -> p b n", b=4)
        GT = part(2 * 512).rearrange("p (b n) -> p b n", b=2)
        c1 = part(2 * H).rearrange("p (b n) -> p b n", b=2)
        u = part(2 * H).rearrange("p (b n) -> p b n", b=2)
        ex = part(2 * H).rearrange("p (b n) -> p b n", b=2)
        sg = part(2 * H).rearrange("p (b n) -> p b n", b=2)
        den = part(2 * H).rearrange("p (b n) -> p b n", b=2)
        q = part(2 * H).rearrange("p (b n) -> p b n", b=2)
        qT = part(2 * 2 * P).rearrange("p (b k n) -> p b k n", b=2, k=2)
        c2 = part(2 * H).rearrange("p (b n) -> p b n", b=2)
        xn = part(2 * H).rearrange("p (b n) -> p b n", b=2)
        wc = part(NTAB * 2 * H).rearrange("p (i k n) -> p i k n", i=NTAB, k=2)
        wkT = part(2 * NTAB * DK).rearrange("p (k i n) -> p k i n", k=2, i=NTAB)
        bk = part(2 * NTAB).rearrange("p (k i) -> p k i", k=2)
        fcb = part(H)
        ids = part(4).bitcast(I32)
        hid = part(4).bitcast(I32)
        assert at <= E * (2 * FF + FC * H)

        OT = sb("OT", [P, 2, NG, S])
        qk32 = sb("qk32", [P, 2, S])
        parts = sb("parts", [P, 2, 3, S], BF16)
        rest = sb("rest", [P, S])
        pvs = sb("pvs", [P, S])
        sums = sb("sums", [P, S])
        rsum = sb("rsum", [P, S])
        nmx = sb("nmx", [P, 2, TPB, HG])
        npt = sb("npt", [P, 2, TPB, 2 * HG], BF16)
        nmT = sb("nmT", [2 * HG, 2, S], BF16)
        gmx = sb("gmx", [HC, NB, 2])
        st = sb("st", [P, 3, 2, 6])
        mv = sb("mv", [P, 3, 2, 2])
        lnv = sb("lnv", [P, 3, 2])
        rstd = sb("rstd", [P, 3, 2])
        csm = sb("csm", [HC, 12, 2])
        xoff = sb("xoff", [P, 2])
        
        ps = ctx.enter_context(nc.psum_tensor("ps", [P, 8, 512], F32))

        s_const, s_wmm, s_wvec, s_watt = sem("constants_in"), sem("fuse_weights_in"), sem("vectors_in"), sem("attention_weights_in")
        s_zero = sem("fills_done")
        s_fused, s_wfc = sem("fused_weights_done"), sem("fused_weights_ready")
        s_identb = sem("identity_bf16_ready")
        g_id = [sem(f"ids_in{k}") for k in range(4)]
        g_val = [sem(f"values_in{k}") for k in range(4)]
        g_hid = [sem(f"shifted_ids_in{k}") for k in range(4)]
        g_we = [sem(f"word_rows_in{k}") for k in range(4)]
        g_tab = [sem(f"table_rows_in{k}") for k in range(4)]
        t1_done, gt_ready, fc_done = sem("t1_done"), sem("gt_ready"), sem("fc_done")
        bn_done = [sem(f"bn{n}_done") for n in range(3)]
        mv_ready = [sem(f"mean_var{n}_ready") for n in range(3)]
        ln_log = [sem(f"log_var{n}_done") for n in range(3)]
        rs_ready = [sem(f"rstd{n}_ready") for n in range(3)]
        den_ready, sg_log, sg_ready = sem("den_ready"), sem("sigmoid_log_done"), sem("sigmoid_ready")
        c1_done, u_ready, e_ready, q_ready = sem("c1_done"), sem("u_ready"), sem("e_ready"), sem("q_ready")
        t2_done, qt_ready, pj_done = sem("t2_done"), sem("qt_ready"), sem("pj_done")
        c2_done, h_ready, xoff_ready, x_ready = sem("c2_done"), sem("h_ready"), sem("xoff_ready"), sem("x_ready")
        t3_done, xt_ready, gmx_ready = sem("t3_done"), sem("xt_ready"), sem("gmx_ready")
        cs_dve, cs_act, w_scaled = sem("scale_steps_vector"), sem("scale_steps_scalar"), sem("weights_scaled")

        def gate(e):
            e.nop(nofuse=True)

        def tile_of(i, k, lag):
            k, i = (k - lag) % 4, i + (k - lag) // 4
            if isinstance(i, int) and not 0 <= i < NB:
                return None
            return i, k, 4 * i + k

        def a_sync(e):
            e.dma_start(const[:, :], a["const"]).then_inc(s_const, 16)

            def step(i, k):
                t = tile_of(i, k, 0)
                i, k, s = t
                after(e, g_hid[k], 16 * i)
                gate(e)
                after(e, g_we[k], 16 * i)
                gate(e)
                e.dma_start(ids[:, k:k + 1], a["ids"][ds(s, 1)].rearrange("t p c -> (t p) c")).then_inc(g_id[k], 16)
                if isinstance(i, int) and i == 0 and k == 0:
                    e.wait_ge(s_zero, 1)
                after(e, t1_done, s - 3)
                gate(e)
                e.dma_start(G[:, k, 449:450], a["vals"][ds(s, 1)].rearrange("t p c -> (t p) c")).then_inc(g_val[k], 16)
                if isinstance(s, int) and s == 0:
                    for n in range(NTAB):
                        lo = H + 1 + n * H
                        e.dma_start(wc[0:HC, n, :, :], a["fc_w"][lo:lo + H, :].rearrange("(k p) c -> p k c", k=2)).then_inc(s_wmm, 16)
                    e.dma_start(wkT[0:HC, :, :, :], a["wkT"]).then_inc(s_wmm, 16)
                    e.dma_start(bk[0:HC, :, :], a["bk"]).then_inc(s_wmm, 16)
                    e.dma_start(fcb[64:65, :], a["fc_b"]).then_inc(s_wmm, 16)
                    e.dma_start(wfc[:, 0, :], a["fc_w"][0:P, :]).then_inc(s_wmm, 16)
                    e.dma_start(wfc[0:64, 1, :], a["fc_w"][P:H, :]).then_inc(s_wmm, 16)
                    e.dma_start(wfc[65:66, 3, :], a["fc_w"][H:H + 1, :]).then_inc(s_wmm, 16)
            pipeline(e, NB, 4, 0, step, 3)

        def a_pool(e):
            e.memset(G[:, :, :], 0.0).then_inc(s_id0, 1)
            e.wait_ge(s_id0, 1)
            e.memset(G[:, :, 448:449], 1.0).then_inc(s_zero, 1)
            e.wait_ge(s_zero, 1)
            e.memset(qT[96:98, :, 1, :], 1.0).then_inc(s_zero, 1)
            e.wait_ge(s_zero, 2)
            e.memset(eps[:, 0:1], 1e-5).then_inc(s_zero, 1)
            e.wait_ge(s_zero, 3)
            e.memset(eps[:, 1:2], 1e-12).then_inc(s_zero, 1)
            e.wait_ge(s_zero, 4)

            def step(i, k):
                t = tile_of(i, k, 0)
                if t is not None:
                    ti, tk, s = t
                    e.wait_ge(g_id[tk], 16 * (ti + 1))
                    after(e, g_tab[tk], 16 * ti)
                    gate(e)
                    e.indirect_dma_start(out=hid[:, tk:tk + 1], out_offset=None, in_=a["homo"],
                                         in_offset=bass.IndirectOffsetOnAxis(ap=ids[:, tk:tk + 1], axis=0)).then_inc(g_hid[tk], 16)
                    after(e, t1_done, s - 3)
                    gate(e)
                    e.indirect_dma_start(out=G[:, tk, 0:H], out_offset=None, in_=a["word"],
                                         in_offset=bass.IndirectOffsetOnAxis(ap=ids[:, tk:tk + 1], axis=0)).then_inc(g_we[tk], 16)
                t = tile_of(i, k, 1)
                if t is not None:
                    ti, tk, s = t
                    e.wait_ge(g_hid[tk], 16 * (ti + 1))
                    gate(e)
                    e.indirect_dma_start(out=G[:, tk, H:H + NTAB * DK], out_offset=None, in_=a["tabs"],
                                         in_offset=bass.IndirectOffsetOnAxis(ap=hid[:, tk:tk + 1], axis=0)).then_inc(g_tab[tk], 16)
            pipeline(e, NB, 4, 1, step, 3)

        def a_pe(e):
            e.wait_ge(s_wmm, 160)
            for n, (lo, bank, _) in enumerate(FUSED):
                for kt in range(2):
                    m = e.matmul(ps[lo:lo + DK, bank, 0:H], wkT[0:HC, kt, n, :], wc[0:HC, n, kt, :],
                                 start=kt == 0, stop=kt == 1)
                m.then_inc(s_fused, 1)
            for n in range(NTAB):
                for kt in range(2):
                    m = e.matmul(ps[64:65, 4, 0:H], bk[0:HC, kt, n:n + 1], wc[0:HC, n, kt, :],
                                 start=n == 0 and kt == 0, stop=n == NTAB - 1 and kt == 1)
            m.then_inc(s_fused, 1)
            e.wait_ge(s_const, 16)
            e.wait_ge(s_wfc, 5)

            def step(i, k):
                if t := tile_of(i, k, 0):
                    ti, tk, s = t
                    e.wait_ge(g_we[tk], 16 * (ti + 1))
                    e.wait_ge(g_tab[tk], 16 * (ti + 1))
                    e.wait_ge(g_val[tk], 16 * (ti + 1))
                    after(e, gt_ready, s - 1)
                    for c in range(4):
                        m = e.transpose(ps[:, tk % 2, P * c:P * c + P], G[:, tk, P * c:P * c + P], ident)
                    m.then_inc(t1_done, 1)
                if t := tile_of(i, k, 10):
                    ti, tk, s = t
                    e.wait_ge(x_ready, s + 1)
                    after(e, xt_ready, s)
                    for kt in range(2):
                        m = e.transpose(ps[0:HC, 7, P * kt:P * kt + P], xn[:, tk % 2, HC * kt:HC * kt + HC], ident)
                    m.then_inc(t3_done, 1)
                if t := tile_of(i, k, 1):
                    ti, tk, s = t
                    e.wait_ge(gt_ready, s + 1)
                    after(e, c1_done, s - 1)
                    for c in range(4):
                        K = P if c < 3 else 66
                        m = e.matmul(ps[:, 2 + tk % 2, 0:H], GT[0:K, tk % 2, P * c:P * c + P], wfc[0:K, c, :],
                                     start=c == 0, stop=c == 3)
                    m.then_inc(fc_done, 1)
                if t := tile_of(i, k, 6):
                    ti, tk, s = t
                    if isinstance(s, int) and s == 0:
                        e.wait_ge(s_wvec, 64)
                    e.wait_ge(qt_ready, s + 1)
                    after(e, c2_done, s - 1)
                    e.matmul(ps[:, 5 + tk % 2, 0:H], ident, pos[:, tk, :], start=True, stop=False)
                    e.matmul(ps[:, 5 + tk % 2, 0:H], qT[0:HC, tk % 2, 0, :], wpj[0:HC, 0, :], start=False, stop=False)
                    e.matmul(ps[:, 5 + tk % 2, 0:H], qT[0:HC + 2, tk % 2, 1, :], wpj[0:HC + 2, 1, :],
                             start=False, stop=True).then_inc(pj_done, 1)
                if t := tile_of(i, k, 5):
                    ti, tk, s = t
                    e.wait_ge(q_ready, s + 1)
                    after(e, qt_ready, s)
                    for kt in range(2):
                        m = e.transpose(ps[0:HC, 4, P * kt:P * kt + P], q[:, tk % 2, HC * kt:HC * kt + HC], ident)
                    m.then_inc(t2_done, 1)
            pipeline(e, NB, 4, 10, step, 3)

        def rsqrt(e, n, p, s, ecol):
            e.wait_ge(mv_ready[n], s + 1)
            e.activation(lnv[:, n, p:p + 1], mv[:, n, p, 1:2], ACT.Ln, bias=eps[:, ecol:ecol + 1]).then_inc(ln_log[n], 1)
            e.wait_ge(ln_log[n], s + 1)
            e.activation(rstd[:, n, p:p + 1], lnv[:, n, p:p + 1], ACT.Exp, scale=-0.5).then_inc(rs_ready[n], 1)

        def a_act(e):
            e.preload_act_table_set("natural_log_exp_and_others")
            e.dma_start(lnp[:, :, :], a["lnp"]).then_inc(s_wvec, 16)
            e.dma_start(pos[:, :, :], a["pos"].rearrange("(t p) c -> p t c", p=P)).then_inc(s_wvec, 16)
            e.dma_start(wpj[0:HC, 0, :], a["pj"][0:HC, :]).then_inc(s_wvec, 16)
            e.dma_start(wpj[:, 1, :], a["pj"][HC:2 * HC + 2, :]).then_inc(s_wvec, 16)
            e.wait_ge(s_fused, 5)
            for lo, bank, chunk in FUSED:
                e.activation(wfc[lo:lo + DK, chunk, :], ps[lo:lo + DK, bank, 0:H], ACT.Copy).then_inc(s_wfc, 1)
            e.wait_ge(s_const, 16)
            e.activation(identb[:, :], ident, ACT.Copy).then_inc(s_identb, 1)
            e.dma_start(wqkv[0:HC, 0, :], a["qkv"][0:HC, :]).then_inc(s_watt, 16)
            e.dma_start(wqkv[:, 1, :], a["qkv"][HC:2 * HC + 1, :]).then_inc(s_watt, 16)
            e.dma_start(wo[:, :, :], a["wo"]).then_inc(s_watt, 16)
            e.dma_start(wr[:, :, :], a["router"].rearrange("(k p) n -> p k n", k=2)).then_inc(s_watt, 16)
            e.wait_ge(s_zero, 4)

            def step(i, k):
                if t := tile_of(i, k, 0):
                    ti, tk, s = t
                    e.wait_ge(t1_done, s + 1)
                    after(e, fc_done, s - 1)
                    e.activation(GT[:, tk % 2, :], ps[:, tk % 2, :], ACT.Copy).then_inc(gt_ready, 1)
                if t := tile_of(i, k, 10):
                    ti, tk, s = t
                    e.wait_ge(t3_done, s + 1)
                    e.activation(xT[0:HC, ds(ti, 1), :, P * tk:P * tk + P].rearrange("p b k n -> p (b k) n"),
                                 ps[0:HC, 7, 0:2 * P].rearrange("p (k n) -> p k n", k=2), ACT.Copy).then_inc(xt_ready, 1)
                if t := tile_of(i, k, 9):
                    ti, tk, s = t
                    p = tk % 2
                    e.wait_ge(xoff_ready, s + 1)
                    after(e, t3_done, s - 1)
                    gate(e)
                    e.activation(xn[:, p, :], hall[:, ds(s, 1), :].rearrange("p a n -> p (a n)"), ACT.Identity,
                                 bias=xoff[:, p:p + 1], scale=rstd[:, 2, p:p + 1]).then_inc(x_ready, 1)
                if t := tile_of(i, k, 2):
                    rsqrt(e, 0, t[1] % 2, t[2], 0)
                if t := tile_of(i, k, 7):
                    rsqrt(e, 1, t[1] % 2, t[2], 1)
                if t := tile_of(i, k, 8):
                    rsqrt(e, 2, t[1] % 2, t[2], 0)
                if t := tile_of(i, k, 5):
                    ti, tk, s = t
                    e.wait_ge(t2_done, s + 1)
                    after(e, pj_done, s - 1)
                    e.activation(qT[0:HC, tk % 2, :, :], ps[0:HC, 4, 0:2 * P].rearrange("p (k n) -> p k n", k=2), ACT.Copy).then_inc(qt_ready, 1)
                if t := tile_of(i, k, 3):
                    ti, tk, s = t
                    e.wait_ge(u_ready, s + 1)
                    after(e, q_ready, s - 1)
                    e.activation(ex[:, tk % 2, :], u[:, tk % 2, :], ACT.Exp, scale=-1.702).then_inc(e_ready, 1)
                if t := tile_of(i, k, 4):
                    ti, tk, s = t
                    e.wait_ge(den_ready, s + 1)
                    e.activation(sg[:, tk % 2, :], den[:, tk % 2, :], ACT.Ln).then_inc(sg_log, 1)
                    e.wait_ge(sg_log, s + 1)
                    e.activation(ex[:, tk % 2, :], sg[:, tk % 2, :], ACT.Exp, scale=-1.0).then_inc(sg_ready, 1)
            pipeline(e, NB, 4, 10, step, 3)

        def row_stats(e, n, p, s, x):
            gate(e)
            e.bn_stats(st[:, n, p, :], x).then_inc(bn_done[n], 1)

        def mean_var(e, n, p, s):
            e.wait_ge(bn_done[n], s + 1)
            after(e, rs_ready[n], s - 1)
            gate(e)
            e.bn_aggr(mv[:, n, p, :], st[:, n, p, :]).then_inc(mv_ready[n], 1)

        def a_dve(e):
            e.wait_ge(s_fused, 5)
            e.tensor_tensor(wfc[64:65, 3, :], ps[64:65, 4, 0:H], fcb[64:65, :], ALU.add).then_inc(s_wfc, 1)
            e.wait_ge(s_wvec, 64)

            def step(i, k):
                t1, t2, t3, t4, t5 = (tile_of(i, k, lag) for lag in (2, 3, 4, 5, 7))
                t6, t7, t8 = (tile_of(i, k, lag) for lag in (8, 9, 10))
                if t1:
                    ti, tk, s = t1
                    e.wait_ge(fc_done, s + 1)
                    row_stats(e, 0, tk % 2, s, ps[:, 2 + tk % 2, 0:H])
                if t5:
                    ti, tk, s = t5
                    e.wait_ge(pj_done, s + 1)
                    row_stats(e, 1, tk % 2, s, ps[:, 5 + tk % 2, 0:H])
                if t6:
                    ti, tk, s = t6
                    e.wait_ge(c2_done, s + 1)
                    e.wait_ge(rs_ready[1], s + 1)
                    e.scalar_tensor_tensor(hall[:, ds(s, 1), :].rearrange("p a n -> p (a n)"), c2[:, tk % 2, :],
                                           rstd[:, 1, tk % 2:tk % 2 + 1], lnp[:, 3, :], ALU.mult, ALU.add).then_inc(h_ready, 1)
                if t7:
                    ti, tk, s = t7
                    p = tk % 2
                    e.wait_ge(mv_ready[2], s + 1)
                    e.wait_ge(rs_ready[2], s + 1)
                    after(e, x_ready, s - 1)
                    e.scalar_tensor_tensor(xoff[:, p:p + 1], mv[:, 2, p, 0:1], -1.0, rstd[:, 2, p:p + 1],
                                           ALU.mult, ALU.mult).then_inc(xoff_ready, 1)
                if t1:
                    mean_var(e, 0, t1[1] % 2, t1[2])
                if t5:
                    mean_var(e, 1, t5[1] % 2, t5[2])
                if t6:
                    ti, tk, s = t6
                    e.wait_ge(h_ready, s + 1)
                    row_stats(e, 2, tk % 2, s, hall[:, ds(s, 1), :].rearrange("p a n -> p (a n)"))
                if t1:
                    ti, tk, s = t1
                    p = tk % 2
                    e.wait_ge(mv_ready[0], s + 1)
                    e.scalar_tensor_tensor(c1[:, p, :], ps[:, 2 + p, 0:H], mv[:, 0, p, 0:1], lnp[:, 0, :],
                                           ALU.subtract, ALU.mult).then_inc(c1_done, 1)
                if t5:
                    ti, tk, s = t5
                    p = tk % 2
                    e.wait_ge(mv_ready[1], s + 1)
                    e.scalar_tensor_tensor(c2[:, p, :], ps[:, 5 + p, 0:H], mv[:, 1, p, 0:1], lnp[:, 2, :],
                                           ALU.subtract, ALU.mult).then_inc(c2_done, 1)
                if t4:
                    ti, tk, s = t4
                    e.wait_ge(sg_ready, s + 1)
                    after(e, t2_done, s - 1)
                    e.tensor_tensor(q[:, tk % 2, :], u[:, tk % 2, :], ex[:, tk % 2, :], ALU.mult).then_inc(q_ready, 1)
                if t6:
                    mean_var(e, 2, t6[1] % 2, t6[2])
                if t2:
                    ti, tk, s = t2
                    p = tk % 2
                    e.wait_ge(c1_done, s + 1)
                    e.wait_ge(rs_ready[0], s + 1)
                    after(e, q_ready, s - 1)
                    e.scalar_tensor_tensor(u[:, p, :], c1[:, p, :], rstd[:, 0, p:p + 1], lnp[:, 1, :],
                                           ALU.mult, ALU.add).then_inc(u_ready, 1)
                if t3:
                    ti, tk, s = t3
                    e.wait_ge(e_ready, s + 1)
                    e.tensor_scalar(den[:, tk % 2, :], ex[:, tk % 2, :], 1e18, 1.0, ALU.min, ALU.add).then_inc(den_ready, 1)
                if isinstance(i, int) and i == 1 and k == 0:
                    e.wait_ge(s_watt, 64)
                    e.tensor_reduce(csm[:, 1, :], wqkv[0:HC, :, :], AX.X, ALU.max, apply_absolute_value=True).then_inc(cs_dve, 1)
                if t8 and t8[1] == 3:
                    ti, tk, s = t8
                    e.wait_ge(xt_ready, s + 1)
                    e.tensor_reduce(gmx[:, ds(ti, 1), :].rearrange("p a n -> p (a n)"),
                                    xT[0:HC, ds(ti, 1), :, :].rearrange("p a k n -> p (a k) n"),
                                    AX.X, ALU.max, apply_absolute_value=True).then_inc(gmx_ready, 1)
            pipeline(e, NB, 4, 10, step, 3)
            smoothing(e)

        def smoothing(e):
            gm, wm, lg, lw, z, v, p2, d1, d2, up, cs, ics = (csm[:, n, :] for n in range(12))
            e.wait_ge(gmx_ready, NB)
            e.tensor_reduce(gm, gmx[:, :, :].rearrange("p b k -> p k b"), AX.X, ALU.max).then_inc(cs_dve, 1)
            e.wait_ge(cs_act, 2)
            e.tensor_scalar(lw, lw, -(1.0 - ALPHA), None, ALU.mult).then_inc(cs_dve, 1)
            e.wait_ge(cs_dve, 3)
            e.scalar_tensor_tensor(z, lg, ALPHA, lw, ALU.mult, ALU.add).then_inc(cs_dve, 1)
            e.wait_ge(cs_act, 3)
            e.tensor_scalar(p2.bitcast(I32), v.bitcast(I32), 0x7F800000, None, ALU.bitwise_and).then_inc(cs_dve, 1)
            e.wait_ge(cs_dve, 5)
            e.tensor_tensor(d1, v, p2, ALU.subtract).then_inc(cs_dve, 1)
            e.scalar_tensor_tensor(d2, p2, 2.0, v, ALU.mult, ALU.subtract).then_inc(cs_dve, 1)
            e.wait_ge(cs_dve, 7)
            e.tensor_tensor(up, d1, d2, ALU.is_gt).then_inc(cs_dve, 1)
            e.wait_ge(cs_dve, 8)
            e.scalar_tensor_tensor(cs, up, 1.0, p2, ALU.add, ALU.mult).then_inc(cs_dve, 1)
            e.wait_ge(cs_dve, 9)
            e.reciprocal(ics, cs).then_inc(cs_dve, 1)
            for kt in range(2):
                e.tensor_scalar(wqkv[0:HC, kt, :], wqkv[0:HC, kt, :], cs[:, kt:kt + 1], None, ALU.mult).then_inc(w_scaled, 1)
            e.wait_ge(cs_dve, 10)

        def smoothing_act(e):
            gm, wm, lg, lw, z, v = (csm[:, n, :] for n in range(6))
            e.wait_ge(cs_dve, 2)
            e.activation(lg, gm, ACT.Ln).then_inc(cs_act, 1)
            e.activation(lw, wm, ACT.Ln).then_inc(cs_act, 1)
            e.wait_ge(cs_dve, 4)
            e.activation(v, z, ACT.Exp).then_inc(cs_act, 1)

        s_id0 = sem("zero_fill_done")
        ics = csm[:, 11, :]

        room = xT[:, :, :, :].rearrange("p b k n -> p (b k n)")
        at = 0

        def room_part(n):
            nonlocal at
            at += n
            assert at <= NB * 2 * S
            return room[:, at - n:at]
        hs = room_part(TPB * H).rearrange("p (t n) -> p t n", t=TPB)
        xf = room_part(2 * TPB * H).rearrange("p (b t n) -> p b t n", b=2, t=TPB)
        assert at <= 3 * 2 * S
        routing = sb("routing", [P, ROUTING])
        at2 = 0

        def rpart(n):
            nonlocal at2
            at2 += n
            assert at2 <= ROUTING
            return routing[:, at2 - n:at2]
        xfT = rpart(TPB * 2 * P).rearrange("p (t k n) -> p t k n", t=TPB, k=2)
        c5 = rpart(2 * H).rearrange("p (b n) -> p b n", b=2)
        entry = rpart(2 * TPB * 2 * 2).rearrange("p (b t a n) -> p b t a n", b=2, t=TPB, a=2)
        sel = rpart(2 * TPB * E).rearrange("p (b t n) -> p b t n", b=2, t=TPB)
        cum = rpart(2 * E).rearrange("p (b n) -> p b n", b=2)
        bsel = rpart(E)
        above = rpart(TPB * E * E)
        equal = rpart(TPB * E * E)
        probs, dif, rk, first, second, slot, tmp, tmp2 = (
            rpart(TPB * E).rearrange("p (t n) -> p t n", t=TPB) for _ in range(8))
        mx, sm, rs, pa, pb_, dn, rd, sa, sb_ = (rpart(TPB) for _ in range(9))
        st4 = rpart(2 * TPB * 6).rearrange("p (l t n) -> p l t n", l=2, t=TPB)
        mv4 = rpart(2 * TPB * 2).rearrange("p (l t n) -> p l t n", l=2, t=TPB)
        lv4 = rpart(2 * TPB).rearrange("p (l t) -> p l t", l=2)
        rs4 = rpart(2 * TPB).rearrange("p (l t) -> p l t", l=2)
        rp1 = rpart(TPB)
        nmr = rpart(2 * TPB).rearrange("p (l t) -> p l t", l=2)
        slots = rpart(2 * TPB * 2).bitcast(I32).rearrange("p (b t a) -> p b t a", b=2, t=TPB)
        pad_entry = rpart(2)
        zero = rsum[:, :]
        R = 23
        R_DIF, R_SEL, R_SLOT = 2, 14, 17
        at = 3 * 2 * S
        cnt, ntl, start, stop_, shift = (room_part(E) for _ in range(5))
        nti = room_part(E).bitcast(I32)
        idx = room_part(DT)
        tef = room_part(DT)
        behind, within, number = (room_part(DT * E).rearrange("p (t n) -> p t n", t=DT) for _ in range(3))
        idi = room_part(DT).bitcast(I32)
        tei = room_part(DT).bitcast(I32)
        idr = room_part(DU).bitcast(I32)
        toki = room_part(DU).bitcast(I32)
        eg = room_part(DU * 2).rearrange("p (b n) -> p b n", b=DU)
        XG = parts[:, :, :, :].rearrange("p b j s -> p (b j s)").bitcast(F32).rearrange("p (b n) -> p b n", b=DU)
        ott = OT[:, :, :, :].rearrange("p b g s -> p (b g s)")
        hT = ott[:, 0:2 * FF].rearrange("p (b c n) -> p b c n", b=2, c=FC)
        xgT = pvs[:, :].rearrange("p (b k n) -> p b k n", b=2, k=2)
        Y = sums[:, 0:2 * H].rearrange("p (b n) -> p b n", b=2)
        w1s = room[:, 0:2 * 2 * FF].rearrange("p (b k n) -> p b k n", b=2, k=2)
        w1 = big[:, 0:E * 2 * FF].rearrange("p (e k n) -> p e k n", e=E, k=2)
        w2 = big[:, E * 2 * FF:].rearrange("p (e c n) -> p e c n", e=E, c=FC)

        EARLY = [x for x in range(E) if 2 * FF * x % (NH * S) < NH * S // 2]
        s_w = sem("expert_weights_in")
        c_zero, c_pad = sem("zero_rows_ready"), sem("padding_rows_stored")
        bn4, mv4_ready = [sem(f"route_bn{n}_done") for n in range(2)], [sem(f"route_mean_var{n}_ready") for n in range(2)]
        log4, rs4_ready = [sem(f"route_log{n}_done") for n in range(2)], [sem(f"route_rstd{n}_ready") for n in range(2)]
        aff_ready = [sem(f"scale_offset{n}_ready") for n in range(2)]
        hs_ready, res_ready, res_out, xhat_ready = sem("hs_ready"), sem("residual_ready"), sem("residual_stored"), sem("xhat_ready")
        c5_done, xff_ready = sem("c5_done"), sem("xff_ready")
        xt4_done, xt4_ready, lg_done = sem("xff_turned"), sem("xff_turned_ready"), sem("logits_done")
        route, rexp, rank_done, slots_ready = sem("routing_steps"), sem("routing_exp_done"), sem("rank_done"), sem("slots_ready")
        x_out = [sem(f"x_rows_stored{k}") for k in range(2)]
        scat = [sem(f"rows_listed{k}") for k in range(2)]
        c_fill, slot_sum, gates_in = sem("routing_fills_done"), sem("slot_sums_done"), sem("gates_in_rows")
        cnt_done, plan, plan_ready = sem("counts_done"), sem("plan_steps"), sem("plan_ready")


        SB = 3
        S1, S2, PVB, MISC = 0, SB, 6, 7
        NS = TPB * HG
        xs_ready, qk_done, v_done = sem("xs_ready"), sem("qk_done"), sem("v_done")
        qk_copied, rest_done, mid_done, parts_ready = sem("qk_copied"), sem("rest_done"), sem("mid_done"), sem("parts_ready")
        stored = [sem(f"parts_stored{m}") for m in range(3)]
        stack_in = [sem(f"stack_in{k}") for k in range(2)]
        v_ready, b_fill = sem("v_ready"), sem("attention_fills_done")
        p1_done, max_done, nh_done, np_ready = sem("p1_done"), sem("max_done"), sem("neg_high_done"), sem("neg_parts_ready")
        nt_done, nmt_ready = sem("neg_turned"), sem("neg_rows_ready")
        neg_in = [sem(f"neg_rows_in{k}") for k in range(2)]
        p2_done, exp_done, pv_done, pvs_ready = sem("p2_done"), sem("exp_done"), sem("pv_done"), sem("pvs_ready")
        sum_log, rsum_ready = sem("sum_log_done"), sem("reciprocal_sums_ready")
        shf_done, ot_ready, h2_ready = sem("sums_spread"), sem("ot_ready"), sem("h2_ready")
        op_done = [sem(f"out_proj_done{k}") for k in range(2)]

        def batch_of(i, kb, lag):
            i, kb = i + (kb - lag) // 2, (kb - lag) % 2
            if isinstance(i, int) and not 0 <= 2 * i + kb < NB:
                return None
            return i, kb, 2 * i + kb

        def group_of(i, m, lag):
            i, m = i + (m - lag) // 6, (m - lag) % 6
            if isinstance(i, int) and not 0 <= 6 * i + m < NB * NG:
                return None
            return i, m, 6 * i + m

        def upto(n, most):
            return max(0, min(n, most)) if isinstance(n, int) else n

        def qk_job(e, i, kb, b, m, free):
            e.wait_ge(xs_ready, 2 * b + 2)
            free()
            e.matmul(ps[:, MISC, :], wqkv[0:HC, 0, P * m:P * m + P], xs[0:HC, kb, 0, :], start=True, stop=False)
            e.matmul(ps[:, MISC, :], wqkv[0:HC + 1, 1, P * m:P * m + P], xs[0:HC + 1, kb, 1, :],
                     start=False, stop=True).then_inc(qk_done, 1)

        def v_job(e, i, kb, b, jj, free):
            free()
            for t in range(2):
                sl = slice(P * (2 * jj + t), P * (2 * jj + t) + P)
                e.matmul(ps[:, MISC, H * t:H * t + H], xs[0:HC, kb, 0, sl], wqkv[0:HC, 0, 2 * H:3 * H], start=True, stop=False)
                m = e.matmul(ps[:, MISC, H * t:H * t + H], xs[0:HC + 1, kb, 1, sl], wqkv[0:HC + 1, 1, 2 * H:3 * H],
                             start=False, stop=True)
            m.then_inc(v_done, 1)

        def b_steps(e, step):
            pipeline(e, NB // 2, 2, 4, step, 2)

        def b_pe(e):
            e.wait_ge(w_scaled, 2)
            e.wait_ge(b_fill, 3)
            e.wait_ge(s_identb, 1)

            def p1(n, m, x):
                kb, g, h, qt = m // 3, m % 3, x // TPB, x % TPB
                after(e, max_done, NS * n + x + 1 - SB)
                e.matmul(ps[:, S1 + (NS * m + x) % SB, :], QS[0:QROWS, kb, HG * g + h, P * qt:P * qt + P],
                         KS[0:QROWS, kb, HG * g + h, :], start=True, stop=True).then_inc(p1_done, 1)

            def p2(n, m, x):
                kb, kt, h = m // 3, x // HG, HG * (m % 3) + x % HG
                after(e, exp_done, NS * n + x + 1 - SB)
                e.matmul(ps[:, S2 + (NS * m + x) % SB, :], KS[0:QROWS + NEG, kb, h, P * kt:P * kt + P],
                         QS[0:QROWS + NEG, kb, h, :], start=True, stop=True).then_inc(p2_done, 1)

            def pv(n, m, kt):
                kb, g = m // 3, m % 3
                e.wait_ge(exp_done, NS * n + HG * kt + HG)
                if kt == 0:
                    after(e, pvs_ready, n)
                for h in range(HG):
                    mm = e.matmul(ps[32 * h:32 * h + 32, PVB, :], VV[:, kb, kt, HG * g + h, :], PT[:, kt % 2, h, :],
                                  start=kt == 0, stop=kt == TPB - 1)
                mm.then_inc(pv_done, 1)

            def turn(rt, hf):
                _, p, b = rt
                e.wait_ge(xff_ready, 2 * b + hf + 1)
                for t in range(2):
                    for kt in range(2):
                        m = e.transpose(ps[0:HC, MISC, P * (2 * t + kt):P * (2 * t + kt) + P],
                                        xf[:, p, 2 * hf + t, HC * kt:HC * kt + HC], ident)
                m.then_inc(xt4_done, 1)

            def logits(rt):
                e.wait_ge(xt4_ready, 2 * rt[2] + 2)
                for t in range(TPB):
                    for kt in range(2):
                        m = e.matmul(ps[:, MISC, E * t:E * t + E], xfT[0:HC, t, kt, :], wr[:, kt, :], start=kt == 0, stop=kt == 1)
                m.then_inc(lg_done, 1)

            def ranks(rt):
                _, p, b = rt
                one = const[:, C_ONE:C_ONE + P]
                e.wait_ge(route, R * b + R_SEL)
                e.matmul(ps[:, MISC, 0:TPB * E], const[:, C_TRI:C_TRI + P],
                         sel[:, p, :, :].rearrange("p t n -> p (t n)"), start=True, stop=False)
                for t in range(1, TPB):
                    e.matmul(ps[:, MISC, E * t:TPB * E], one,
                             sel[:, p, 0:TPB - t, :].rearrange("p t n -> p (t n)"), start=False, stop=False)
                e.matmul(ps[:, MISC, 0:TPB * E], one, cum[:, p, :].unsqueeze(1).broadcast_to((P, TPB, E)),
                         start=False, stop=True).then_inc(rank_done, 1)

            def step(i, kb):
                b = 2 * i + kb - 1
                nxt, att, prv = (batch_of(i, kb, lag) for lag in range(3))
                rt = batch_of(i, kb, 4)
                had = lambda lag: upto(b + 1 - lag, NB)
                pending = [(qk_copied, 6 * had(0)), (v_ready, 2 * had(0)), (nmt_ready, upto(3 * b - 1, NB * NG)),
                           (h2_ready, 2 * had(2))]
                if isinstance(i, int):
                    pending += [(xt4_ready, 2 * had(4)), (route, R * (had(4) - 1) + R_SLOT)]
                else:
                    pending = [(h2_ready, 2 * had(2))]

                def free():
                    for which, n in pending:
                        after(e, which, n)

                def job(which, n):
                    pending[:] = [(which, n)]
                for g in range(3):
                    cur, neg, old, last = (group_of(i, 3 * kb + g, lag) for lag in (3, 4, 5, 6))
                    if att and g == 0:
                        e.wait_ge(stack_in[att[1]], 192 * (att[0] + 1))
                    if att and g == 2:
                        e.wait_ge(v_ready, 2 * att[2] + 2)
                    if old:
                        e.wait_ge(neg_in[old[1] % 2], 32 * (3 * old[0] + old[1] // 2 + 1))
                    for k in range(8):
                        if cur:
                            p1(cur[2], cur[1], 2 * k)
                        if old:
                            p2(old[2], old[1], 2 * k)
                        if cur:
                            p1(cur[2], cur[1], 2 * k + 1)
                        if old:
                            p2(old[2], old[1], 2 * k + 1)
                        if k == 1 and last:
                            pv(last[2], last[1], 3)
                        if k in (3, 5, 7) and old:
                            pv(old[2], old[1], k // 2 - 1)
                        if k == 1 and neg:
                            ng, nm = neg[2], neg[1]
                            e.wait_ge(np_ready, ng + 1)
                            free()
                            for t in range(TPB):
                                mm = e.transpose(ps[0:2 * HG, MISC, 0:S // 2].bitcast(BF16)[:, P * t:P * t + P],
                                                 npt[:, nm % 2, t, :], identb[:, :])
                            mm.then_inc(nt_done, 1)
                            job(nmt_ready, ng + 1)
                        if rt and g == 0 and k in (0, 2):
                            free()
                            turn(rt, k // 2)
                            job(xt4_ready, 2 * rt[2] + k // 2 + 1)
                        if nxt:
                            if g == 0 and k in (4, 5, 6):
                                qk_job(e, *nxt, k - 4, free)
                                job(qk_copied, 6 * nxt[2] + 2 * (k - 3))
                            if g == 2 and k in (3, 4):
                                v_job(e, *nxt, k - 3, free)
                                job(v_ready, 2 * nxt[2] + k - 2)
                        if rt and g == 1 and k == 0:
                            free()
                            logits(rt)
                            job(route, R * rt[2] + R_DIF)
                        if rt and g == 2 and k == 0:
                            free()
                            ranks(rt)
                            job(route, R * rt[2] + R_SLOT)
                        if prv and g == 2 and k in (5, 7):
                            jj = (k - 5) // 2
                            pi, pk, pb = prv
                            e.wait_ge(ot_ready, 3 * pb + 3)
                            free()
                            for t in range(2):
                                sl = slice(P * (2 * jj + t), P * (2 * jj + t) + P)
                                for gg in range(NG):
                                    mm = e.matmul(ps[:, MISC, H * t:H * t + H], OT[:, pk, gg, sl], wo[:, gg, :],
                                                  start=gg == 0, stop=gg == NG - 1)
                            mm.then_inc(op_done[pk], 1)
                            job(h2_ready, 2 * pb + jj + 1)
            b_steps(e, step)
            e.wait_ge(route, R * NB)
            e.matmul(ps[:, PVB, 0:E], const[:, C_ONE:C_ONE + P], cum[:, NB % 2, :], start=True, stop=True).then_inc(cnt_done, 1)

        def qk_evac(e, m, i, kb):
            x = 6 * i + 3 * kb + m
            p = (3 * kb + m) % 2
            e.wait_ge(qk_done, x + 1)
            after(e, parts_ready, x - 1)
            e.activation(qk32[:, p, :], ps[:, MISC, :], ACT.Copy).then_inc(qk_copied, 1)
            if isinstance(x, int):
                if x >= 2:
                    e.wait_ge(stored[(m - 2) % 3], 16 * ((x - 2) // 3 + 1))
            else:
                e.wait_ge(stored[(m - 2) % 3], 16 * (2 * i + kb + (m - 2) // 3 + 1))
            e.activation(parts[:, p, 0, :], ps[:, MISC, :], ACT.Copy).then_inc(qk_copied, 1)

        def v_evac(e, jj, kb, x, used):
            e.wait_ge(v_done, x + 1)
            after(e, pv_done, used)
            e.activation(VV[:, kb, 2 * jj:2 * jj + 2, :, 0:HD],
                         ps[:, MISC, 0:2 * H].rearrange("p (t h d) -> p t h d", t=2, h=NH), ACT.Copy).then_inc(v_ready, 1)

        def b_act(e):
            smoothing_act(e)

            def norm(n, b):
                e.wait_ge(mv4_ready[n], TPB * b + TPB)
                e.activation(lv4[:, n, :], mv4[:, n, :, 1], ACT.Ln, bias=eps[:, 0:1]).then_inc(log4[n], 1)
                e.wait_ge(log4[n], b + 1)
                e.activation(rs4[:, n, :], lv4[:, n, :], ACT.Exp, scale=-0.5).then_inc(rs4_ready[n], 1)

            def route_act(g, k, i, kb, nm, rt):
                if rt and g == 0 and k in (0, 2):
                    hf = k // 2
                    e.wait_ge(xt4_done, 2 * rt[2] + hf + 1)
                    after(e, lg_done, rt[2])
                    e.activation(xfT[0:HC, 2 * hf:2 * hf + 2, :, :],
                                 ps[0:HC, MISC, :].rearrange("p (t k n) -> p t k n", t=2, k=2), ACT.Copy).then_inc(xt4_ready, 1)
                if nm and g == 0 and k == 7:
                    norm(0, nm[2])
                if nm and g == 1 and k in (0, 1):
                    b = nm[2]
                    e.wait_ge(aff_ready[0], 2 * b + 2)
                    after(e, xhat_ready, TPB * b)
                    gate(e)
                    for t in range(2 * k, 2 * k + 2):
                        e.activation(hs[:, t, :], hall[:, ds(TPB * b + t, 1), :].rearrange("p a n -> p (a n)"),
                                     ACT.Identity, bias=nmr[:, 0, t:t + 1], scale=rs4[:, 0, t:t + 1]).then_inc(hs_ready, 1)
                if rt and g == 1 and k == 1:
                    e.wait_ge(route, R * rt[2] + R_DIF)
                    e.activation(probs[:, :, :], dif[:, :, :], ACT.Exp).then_inc(rexp, 1)
                if nm and g == 1 and k in (6, 7):
                    b = nm[2]
                    e.wait_ge(hs_ready, TPB * b + TPB)
                    gate(e)
                    for t in range(2 * (k - 6), 2 * (k - 6) + 2):
                        x = hall[:, ds(TPB * b + t, 1), :].rearrange("p a n -> p (a n)")
                        e.activation(x, x, ACT.Identity, bias=nmr[:, 0, t:t + 1], scale=rp1[:, t:t + 1]).then_inc(res_ready, 1)
                if nm and g == 2 and k == 1:
                    norm(1, nm[2])
                if nm and g == 2 and k in (6, 7):
                    ni, p, b = nm
                    e.wait_ge(aff_ready[1], b + 1)
                    after(e, x_out[p], 16 * ni)
                    after(e, xt4_done, 2 * (b - 1))
                    for t in range(2 * (k - 6), 2 * (k - 6) + 2):
                        e.activation(xf[:, p, t, :], hs[:, t, :], ACT.Identity, bias=nmr[:, 1, t:t + 1],
                                     scale=rs4[:, 1, t:t + 1]).then_inc(xhat_ready, 1)

            def step(i, kb):
                nxt, nm, rt = batch_of(i, kb, 0), batch_of(i, kb, 3), batch_of(i, kb, 4)
                for g in range(3):
                    neg, old, last = (group_of(i, 3 * kb + g, lag) for lag in (4, 5, 6))
                    for k in range(8):
                        if old:
                            n, m = old[2], old[1]
                            for x in (2 * k, 2 * k + 1):
                                kt, h = x // HG, x % HG
                                e.wait_ge(p2_done, NS * n + x + 1)
                                if h == 0:
                                    after(e, pv_done, 4 * n + kt - 1)
                                e.activation(PT[:, kt % 2, h, :], ps[:, S2 + (NS * m + x) % SB, :],
                                             ACT.Exp, scale=SCALE).then_inc(exp_done, 1)
                        if k == 1 and last:
                            e.wait_ge(pv_done, 4 * last[2] + 4)
                            after(e, ot_ready, last[2])
                            e.activation(pvs[:, :], ps[:, PVB, :], ACT.Copy).then_inc(pvs_ready, 1)
                        if k == 1 and neg:
                            e.wait_ge(nt_done, neg[2] + 1)
                            after(e, neg_in[neg[1] % 2], 32 * (3 * neg[0] + neg[1] // 2))
                            e.activation(nmT[:, neg[1] % 2, :], ps[0:2 * HG, MISC, 0:S // 2].bitcast(BF16),
                                         ACT.Copy).then_inc(nmt_ready, 1)
                        if k == 2 and last:
                            if isinstance(i, int) and last[2] == 0:
                                e.wait_ge(c_pad, 64)
                            e.wait_ge(shf_done, last[2] + 1)
                            e.activation(sums[:, :], sums[:, :], ACT.Ln).then_inc(sum_log, 1)
                            e.wait_ge(sum_log, last[2] + 1)
                            e.activation(rsum[:, :], sums[:, :], ACT.Exp, scale=-1.0).then_inc(rsum_ready, 1)
                        if k == 3 and neg:
                            e.wait_ge(nmt_ready, neg[2] + 1)
                            nk, ng = neg[1] // 3, neg[1] % 3
                            for pt in range(NEG):
                                e.dma_start(QS[QROWS + pt:QROWS + pt + 1, nk, HG * ng:HG * ng + HG, :],
                                            nmT[HG * pt:HG * pt + HG, neg[1] % 2, :]).then_inc(neg_in[neg[1] % 2], 16)
                        if nxt:
                            if g == 0 and k in (4, 5, 6):
                                qk_evac(e, k - 4, nxt[0], nxt[1])
                            if g == 2 and k in (3, 4):
                                v_evac(e, k - 3, nxt[1], 2 * nxt[2] + k - 3, 4 * NG * (nxt[2] - 1))
                        route_act(g, k, i, kb, nm, rt)
            b_steps(e, step)

        def split(e, i, kb, m):
            x = 6 * i + 3 * kb + m
            p = (3 * kb + m) % 2
            e.wait_ge(qk_copied, 2 * x + 2)
            after(e, parts_ready, x)
            e.tensor_tensor(rest[:, :], qk32[:, p, :], parts[:, p, 0, :], ALU.subtract).then_inc(rest_done, 1)
            e.wait_ge(rest_done, x + 1)
            gate(e)
            e.tensor_copy(parts[:, p, 1, :], rest[:, :]).then_inc(mid_done, 1)
            e.wait_ge(mid_done, x + 1)
            e.tensor_tensor(parts[:, p, 2, :], rest[:, :], parts[:, p, 1, :], ALU.subtract).then_inc(parts_ready, 1)

        def b_pool(e):
            e.memset(VV[:, :, :, :, HD:32], 1.0).then_inc(b_fill, 1)
            e.wait_ge(b_fill, 1)
            e.memset(KS[QROWS:QROWS + NEG, :, :, :], 1.0).then_inc(b_fill, 1)
            e.wait_ge(b_fill, 2)
            e.memset(xs[HC:HC + 1, :, 1, :], 1.0).then_inc(b_fill, 1)
            e.wait_ge(b_fill, 3)
            e.memset(zero, 0.0).then_inc(c_zero, 1)
            e.wait_ge(c_zero, 1)
            e.memset(pad_entry[:, 0:1], 0.0).then_inc(c_zero, 1)
            e.wait_ge(c_zero, 2)
            e.tensor_copy(pad_entry[:, 1:2], const[:, C_PADTOK:C_PADTOK + 1]).then_inc(c_zero, 1)

            def gamma_beta(p, b, hf):
                x = xf[:, p, 2 * hf:2 * hf + 2, :]
                c = c5[:, :, :]
                e.wait_ge(xhat_ready, TPB * b + 2 * hf + 2)
                after(e, xff_ready, 2 * b + hf)
                e.tensor_tensor(c, x, lnp[:, 4, :].unsqueeze(1).broadcast_to((P, 2, H)), ALU.mult).then_inc(c5_done, 1)
                e.wait_ge(c5_done, 2 * b + hf + 1)
                e.tensor_tensor(x, c, lnp[:, 5, :].unsqueeze(1).broadcast_to((P, 2, H)), ALU.add).then_inc(xff_ready, 1)

            def before_it(b):
                e.wait_ge(route, R * b + 7)
                low = const[:, C_LOW:C_LOW + E * E].unsqueeze(1).broadcast_to((P, TPB, E * E))
                eqt = equal.rearrange("p (t e) -> p t e", t=TPB)
                e.tensor_tensor(eqt, eqt, low, ALU.mult).then_inc(route, 1)
                e.wait_ge(route, R * b + 8)
                e.tensor_tensor(above, above, equal, ALU.add).then_inc(route, 1)

            def step(i, kb):
                nxt, nm, rt = batch_of(i, kb, 0), batch_of(i, kb, 3), batch_of(i, kb, 4)
                if nxt and not (isinstance(i, int) and nxt[2] == 0):
                    for m in range(3):
                        split(e, nxt[0], nxt[1], m)
                if rt:
                    before_it(rt[2])
                if nm:
                    gamma_beta(nm[1], nm[2], 0)
                    gamma_beta(nm[1], nm[2], 1)
                if rt:
                    e.wait_ge(slots_ready, rt[2] + 1)
                    gate(e)
                    if isinstance(i, int) and rt[2] == 0:
                        e.wait_ge(c_pad, 64)
                    for t in range(TPB):
                        for x in range(2):
                            e.indirect_dma_start(out=lists, out_offset=bass.IndirectOffsetOnAxis(ap=slots[:, rt[1], t, x:x + 1], axis=0),
                                                 in_=entry[:, rt[1], t, x, :], in_offset=None).then_inc(scat[rt[1]], 16)
            b_steps(e, step)

        def b_sync(e):
            def stacks(i, kb):
                if not isinstance(i, int) or i > 0:
                    after(e, stack_in[kb], 192 * i)
                    gate(e)
                for m in range(3):
                    x = 6 * i + 3 * kb + m
                    e.wait_ge(parts_ready, x + 1)
                    gate(e)
                    e.dma_start(qkd[kb, m], parts[:, (3 * kb + m) % 2, :, :]).then_inc(stored[m], 16)
                for m in range(3):
                    e.wait_ge(stored[m], 16 * (2 * i + kb + 1))
                    gate(e)
                after(e, p2_done, NS * NG * (2 * i + kb - 1))
                gate(e)
                rows = qkd[kb].rearrange("m p j s -> (m p) j s")
                for which, dst, prt in ((0, QS, QPARTS), (1, KS, KPARTS)):
                    src = rows[H * which:H * which + H].rearrange("(h d) j s -> d h j s", h=NH)
                    for j in range(QP):
                        e.dma_start(dst[HD * j:HD * j + HD, kb, :, :], src[:, :, prt[j], :]).then_inc(stack_in[kb], 16)
            e.wait_ge(c_zero, 3)
            e.dma_start(lists[0:E * CAP, :].rearrange("(p n) c -> p (n c)", p=P), zero).then_inc(c_pad, 16)
            e.dma_start(lists[E * CAP:E * CAP + P, :], pad_entry).then_inc(c_pad, 16)
            e.dma_start(xrows[NB * S:NB * S + P, :], zero[:, 0:H]).then_inc(c_pad, 16)
            e.dma_start(out_ext[NB * S:NB * S + P, :], zero[:, 0:H]).then_inc(c_pad, 16)

            def step(i, kb):
                nxt, nm, rt = batch_of(i, kb, 0), batch_of(i, kb, 3), batch_of(i, kb, 4)
                if rt:
                    b = rt[2]
                    e.wait_ge(xff_ready, 2 * b + 2)
                    e.dma_start(xrows[ds(S * b, S), :].rearrange("(t p) c -> p t c", p=P), xf[:, rt[1], :, :]).then_inc(x_out[rt[1]], 16)
                if nxt:
                    stacks(nxt[0], nxt[1])
                if nm:
                    b = nm[2]
                    e.wait_ge(res_ready, TPB * b + TPB)
                    e.dma_start(out_ext[ds(S * b, S), :].rearrange("(t p) c -> p t c", p=P),
                                hall[:, ds(TPB * b, TPB), :]).then_inc(res_out, 16)
                if isinstance(i, int) and 2 * i + kb == NB:
                    e.wait_ge(p2_done, NS * NG * (NB - 1))
                    e.wait_ge(v_done, 2 * NB)
                    for x in EARLY:
                        e.dma_start(w1[0:HC, x, :, :], a["w1"][:, x, :, :]).then_inc(s_w, 16)
                    e.dma_start(w2[:, E - 1, :, :], a["w2"][:, E - 1, :, :]).then_inc(s_w, 16)
            b_steps(e, step)

        def b_dve(e):
            e.wait_ge(b_fill, 3)
            e.memset(cum[:, 0, :], 0.0).then_inc(c_fill, 1)
            e.wait_ge(c_fill, 1)

            def spread(x):
                return x.unsqueeze(2).broadcast_to((P, TPB, E))

            def sums4(n, b, hf):
                for t in (2 * hf, 2 * hf + 1):
                    if n == 0:
                        gate(e)
                        e.bn_stats(st4[:, 0, t, :], hall[:, ds(TPB * b + t, 1), :].rearrange("p a n -> p (a n)")).then_inc(bn4[0], 1)
                    else:
                        e.wait_ge(hs_ready, TPB * b + TPB)
                        gate(e)
                        e.bn_stats(st4[:, 1, t, :], hs[:, t, :]).then_inc(bn4[1], 1)

            def mean_var4(n, b):
                e.wait_ge(bn4[n], TPB * b + TPB)
                after(e, rs4_ready[n], b)
                gate(e)
                for t in range(TPB):
                    e.bn_aggr(mv4[:, n, t, :], st4[:, n, t, :]).then_inc(mv4_ready[n], 1)

            def offsets(n, b):
                e.wait_ge(mv4_ready[n], TPB * b + TPB)
                e.wait_ge(rs4_ready[n], b + 1)
                after(e, (res_ready, xhat_ready)[n], TPB * b)
                if n == 0:
                    e.tensor_scalar(rp1, rs4[:, 0, :], 1.0, None, ALU.add).then_inc(aff_ready[0], 1)
                e.scalar_tensor_tensor(nmr[:, n, :], mv4[:, n, :, 0], -1.0, rs4[:, n, :], ALU.mult, ALU.mult).then_inc(aff_ready[n], 1)

            def choose(part, i, p, b):
                n = (0, 2, 5, 9)[part]

                def did(ins):
                    nonlocal n
                    n += 1
                    ins.then_inc(route, 1)

                def have(k):
                    e.wait_ge(route, R * b + k)
                if part == 0:
                    lg = ps[:, MISC, 0:TPB * E].rearrange("p (t n) -> p t n", t=TPB)
                    e.wait_ge(lg_done, b + 1)
                    did(e.tensor_reduce(mx, lg, AX.X, ALU.max))
                    have(1)
                    did(e.tensor_tensor(dif, lg, spread(mx), ALU.subtract))
                    return
                if part == 1:
                    e.wait_ge(rexp, b + 1)
                    did(e.tensor_reduce(sm, probs, AX.X, ALU.add))
                    have(3)
                    did(e.reciprocal(rs, sm))
                    have(4)
                    did(e.tensor_tensor(probs, probs, spread(rs), ALU.mult))
                    return
                ab = above.rearrange("p (t e f) -> p t e f", t=TPB, e=E)
                if part == 2:
                    q4 = probs.unsqueeze(2).broadcast_to((P, TPB, E, E))
                    p4 = probs.unsqueeze(3).broadcast_to((P, TPB, E, E))
                    eq = equal.rearrange("p (t e f) -> p t e f", t=TPB, e=E)
                    have(5)
                    did(e.tensor_tensor(eq, q4, p4, ALU.is_equal))
                    did(e.tensor_tensor(ab, q4, p4, ALU.is_gt))
                    return
                have(9)
                did(e.tensor_reduce(rk, ab, AX.X, ALU.add))
                have(10)
                did(e.tensor_scalar(sel[:, p, :, :], rk, 2.0, None, ALU.is_lt))
                did(e.tensor_scalar(first, rk, 0.0, None, ALU.is_equal))
                have(11)
                did(e.tensor_reduce(bsel, sel[:, p, :, :].rearrange("p t n -> p n t"), AX.X, ALU.add))
                did(e.tensor_scalar(second, rk, 1.0, None, ALU.is_equal))
                have(13)
                after(e, rank_done, b)
                did(e.tensor_tensor(cum[:, (p + 1) % 2, :], cum[:, p, :], bsel, ALU.add))
                assert n == 15

            def place(part, i, p, b):
                n = 15 if part == 0 else R

                def did(ins):
                    nonlocal n
                    n += 1
                    ins.then_inc(route, 1)

                def have(k):
                    e.wait_ge(route, R * b + k)
                if part == 0:
                    have(15)
                    did(e.tensor_tensor(tmp, first, probs, ALU.mult))
                    e.wait_ge(rank_done, b + 1)
                    did(e.tensor_tensor(slot, ps[:, MISC, 0:TPB * E].rearrange("p (t n) -> p t n", t=TPB),
                                        const[:, C_CAP:C_CAP + E].unsqueeze(1).broadcast_to((P, TPB, E)), ALU.add))
                    did(e.tensor_tensor(tmp2, second, probs, ALU.mult))
                    have(16)
                    did(e.tensor_reduce(pa, tmp, AX.X, ALU.add))
                    have(18)
                    did(e.tensor_reduce(pb_, tmp2, AX.X, ALU.add))
                    did(e.tensor_tensor(first, first, slot, ALU.mult))
                    have(20)
                    did(e.tensor_tensor(dn, pa, pb_, ALU.add))
                    did(e.tensor_tensor(second, second, slot, ALU.mult))
                    assert n == R
                    return
                have(22)
                e.reciprocal(rd, dn).then_inc(slot_sum, 1)
                e.tensor_reduce(sa, first, AX.X, ALU.add).then_inc(slot_sum, 1)
                have(R)
                e.tensor_reduce(sb_, second, AX.X, ALU.add).then_inc(slot_sum, 1)
                e.wait_ge(slot_sum, 3 * b + 3)
                after(e, scat[p], 128 * i)
                for x, pr_ in enumerate((pa, pb_)):
                    e.tensor_tensor(entry[:, p, :, x, 0], pr_, rd, ALU.mult).then_inc(gates_in, 1)
                    e.tensor_copy(entry[:, p, :, x, 1], const[:, ds(C_TOK + TPB * b, TPB)]).then_inc(gates_in, 1)
                e.tensor_copy(slots[:, p, :, 0], sa).then_inc(gates_in, 1)
                e.wait_ge(gates_in, 5 * b + 5)
                e.tensor_copy(slots[:, p, :, 1], sb_).then_inc(slots_ready, 1)

            def route_dve(g, k, nm, rt):
                if nm and g == 1 and k == 0:
                    offsets(0, nm[2])
                if rt:
                    if (g, k) in ((1, 0), (1, 2), (1, 3), (1, 6)):
                        choose((k + 1) // 2, *rt)
                    if g == 2 and k in (1, 3):
                        place(k // 2, *rt)
                if nm:
                    b = nm[2]
                    if g == 0 and k in (3, 5):
                        e.wait_ge(h2_ready, 2 * b + k // 4 + 1)
                        sums4(0, b, k // 4)
                    if g == 0 and k == 6:
                        mean_var4(0, b)
                    if g == 1 and k in (6, 7):
                        sums4(1, b, k - 6)
                    if g == 2 and k == 0:
                        mean_var4(1, b)
                    if g == 2 and k == 5:
                        offsets(1, b)


            def x_in(i, kb, b, kt):
                if kt == 0:
                    after(e, qk_done, 3 * (b - 1))
                    after(e, v_done, 2 * (b - 1))
                e.tensor_scalar(xs[0:HC, kb, kt, :], xT[0:HC, ds(b, 1), kt, :].rearrange("p a n -> p (a n)"),
                                ics[:, kt:kt + 1], None, ALU.mult).then_inc(xs_ready, 1)

            def step(i, kb):
                nxt, prv, nm, rt = (batch_of(i, kb, lag) for lag in (0, 2, 3, 4))
                if isinstance(i, int) and i == 0 and kb == 0:
                    x_in(*nxt, 0)
                    x_in(*nxt, 1)
                    for m in range(3):
                        split(e, 0, 0, m)
                    nxt = None
                for g in range(3):
                    cur, neg, last = (group_of(i, 3 * kb + g, lag) for lag in (3, 4, 6))
                    for k in range(8):
                        if cur:
                            n, m = cur[2], cur[1]
                            if k == 0:
                                after(e, nt_done, n - 1)
                            for uu in range(2):
                                x = NS * n + 2 * k + uu
                                e.wait_ge(p1_done, x + 1)
                                e.tensor_reduce(nmx[:, m % 2, 2 * (k % 2) + uu, k // 2:k // 2 + 1], ps[:, S1 + (NS * m + 2 * k + uu) % SB, :],
                                                AX.X, ALU.max, negate=True).then_inc(max_done, 1)
                        if k == 0 and neg:
                            n, m = neg[2], neg[1]
                            e.wait_ge(max_done, NS * n + NS)
                            e.tensor_copy(npt[:, m % 2, :, 0:HG], nmx[:, m % 2, :, :]).then_inc(nh_done, 1)
                            e.wait_ge(nh_done, n + 1)
                            e.tensor_tensor(npt[:, m % 2, :, HG:2 * HG], nmx[:, m % 2, :, :], npt[:, m % 2, :, 0:HG],
                                            ALU.subtract).then_inc(np_ready, 1)
                        route_dve(g, k, nm, rt)
                        if nxt and g == 0 and k in (1, 2):
                            x_in(*nxt, k - 1)
                        if k == 1 and last:
                            n = last[2]
                            e.wait_ge(pvs_ready, n + 1)
                            gate(e)
                            e.stream_shuffle(sums[:, :], pvs[:, :], [HD] * 32).then_inc(shf_done, 1)
                        if k == 4 and last:
                            n, m = last[2], last[1]
                            lk, lg = m // 3, m % 3
                            e.wait_ge(rsum_ready, n + 1)
                            after(e, op_done[lk], 2 * last[0])
                            e.tensor_tensor(OT[:, lk, lg, :], pvs[:, :], rsum[:, :], ALU.mult).then_inc(ot_ready, 1)
                        if prv and g == 2 and k in (6, 7):
                            jj = k - 6
                            e.wait_ge(op_done[prv[1]], 2 * prv[0] + jj + 1)
                            hh = hall[:, ds(4 * prv[2] + 2 * jj, 2), :].rearrange("p a n -> p (a n)")
                            e.tensor_tensor(hh, ps[:, MISC, 0:2 * H], hh, ALU.add).then_inc(h2_ready, 1)
            b_steps(e, step)


        def c_begin(e):
            e.wait_ge(h2_ready, 2 * NB)

        def c_sync(e):
            c_begin(e)
            for x in range(E):
                if x not in EARLY:
                    e.dma_start(w1[0:HC, x, :, :], a["w1"][:, x, :, :]).then_inc(s_w, 16)
            for x in range(E - 1):
                e.dma_start(w2[:, x, :, :], a["w2"][:, x, :, :]).then_inc(s_w, 16)

        def make_plan(e):
            n = 0

            def did(ins):
                nonlocal n
                n += 1
                ins.then_inc(plan, 1)
                e.wait_ge(plan, n)
            e.wait_ge(cnt_done, 1)
            did(e.tensor_copy(cnt, ps[:, PVB, 0:E]))
            did(e.tensor_copy(nti, cnt))
            did(e.tensor_scalar(nti, nti, P - 1, None, ALU.add))
            did(e.tensor_scalar(nti, nti, P.bit_length() - 1, None, ALU.arith_shift_right))
            did(e.tensor_copy(ntl, nti))
            did(e.tensor_scalar(ntl, ntl, float(P), None, ALU.mult))
            pair = above[:, 0:E * E].rearrange("p (e f) -> p e f", e=E)
            did(e.tensor_tensor(pair, ntl.unsqueeze(1).broadcast_to((P, E, E)),
                                const[:, C_LOW:C_LOW + E * E].rearrange("p (e f) -> p e f", e=E), ALU.mult))
            did(e.tensor_reduce(start, pair, AX.X, ALU.add))
            did(e.tensor_tensor(stop_, start, cnt, ALU.add))
            did(e.tensor_tensor(shift, const[:, C_CAP:C_CAP + E], start, ALU.subtract))
            did(e.tensor_scalar(shift, shift, const[:, C_PAD:C_PAD + 1], None, ALU.subtract))
            f = const[:, C_F:C_F + DT].unsqueeze(2).broadcast_to((P, DT, E))

            def per_expert(x):
                return x.unsqueeze(1).broadcast_to((P, DT, E))
            e.tensor_tensor(behind, f, per_expert(start), ALU.is_ge).then_inc(plan, 1)
            e.tensor_tensor(within, f, per_expert(stop_), ALU.is_lt).then_inc(plan, 1)
            e.tensor_tensor(number, f, per_expert(shift), ALU.add).then_inc(plan, 1)
            n += 3
            e.wait_ge(plan, n)
            e.tensor_tensor(within, within, behind, ALU.mult).then_inc(plan, 1)
            e.tensor_reduce(tef, behind, AX.X, ALU.add).then_inc(plan, 1)
            n += 2
            e.wait_ge(plan, n)
            did(e.tensor_tensor(number, number, within, ALU.mult))
            e.tensor_scalar(tei, tef, -1.0, None, ALU.add).then_inc(plan, 1)
            e.tensor_reduce(idx, number, AX.X, ALU.add).then_inc(plan, 1)
            n += 2
            e.wait_ge(plan, n)
            e.tensor_scalar(idi, idx, const[:, C_PAD:C_PAD + 1], None, ALU.add).then_inc(plan_ready, 1)

        idr_ready, tok_ready = sem("tile_entries_chosen"), sem("gate_and_tokens_kept")
        egath = [sem(f"entries_in{k}") for k in range(2)]
        gath = [sem(f"x_rows_in{k}") for k in range(DU)]
        xd_done, xd_ready, hd_done, silu_done = sem("x_turned"), sem("x_turned_ready"), sem("inner_done"), sem("silu_done")
        w1_ready = [sem(f"expert_w1_chosen{k}") for k in range(2)]
        y_done, y_ready = sem("y_done"), sem("y_ready")
        added = sem("rows_added")

        def dtile(i, k, lag):
            k, i = (k - lag) % DU, i + (k - lag) // DU
            if isinstance(i, int) and not 0 <= i < DT // DU:
                return None
            return i, k, DU * i + k

        def choose_w1(e, kt, tk, s):
            if isinstance(s, int) and s == 0:
                e.wait_ge(s_w, 2 * E * 16)
                e.wait_ge(x_out[0], 16 * (NB // 2))
                e.wait_ge(x_out[1], 16 * (NB // 2))
            after(e, hd_done, 2 * (s - 1))
            gate(e)
            x = e.value_load(tei[0:1, ds(s, 1)], min_val=0, max_val=E - 1)
            return w1s[0:HC, tk % 2, kt, :], w1[0:HC, ds(x, 1), kt, :].rearrange("p a n -> p (a n)")

        def d_pe(e):
            e.wait_ge(plan_ready, 1)

            def step(i, k):
                if t := dtile(i, k, 3):
                    ti, tk, s = t
                    e.wait_ge(xd_ready, s + 1)
                    e.wait_ge(w1_ready[0], s + 1)
                    e.wait_ge(w1_ready[1], s + 1)
                    for hf in range(2):
                        after(e, silu_done, 2 * (s - 2) + hf + 1)
                        for c in range(3):
                            f0 = FH * hf + P * c
                            for kt in range(2):
                                m = e.matmul(ps[:, 1 + 2 * (tk % 2) + hf, P * c:P * c + P], w1s[0:HC, tk % 2, kt, f0:f0 + P],
                                             xgT[0:HC, tk % 2, kt, :], start=kt == 0, stop=kt == 1)
                        m.then_inc(hd_done, 1)
                if t := dtile(i, k, 2):
                    ti, tk, s = t
                    e.wait_ge(gath[tk], 16 * (ti + 1))
                    after(e, xd_ready, s)
                    for kt in range(2):
                        m = e.transpose(ps[0:HC, 0, P * kt:P * kt + P], XG[:, tk, HC * kt:HC * kt + HC], ident)
                    m.then_inc(xd_done, 1)
                if t := dtile(i, k, 4):
                    ti, tk, s = t
                    if isinstance(s, int) and s == 0:
                        e.wait_ge(s_w, 2 * E * 16)
                    ex_ = e.value_load(tei[0:1, ds(s, 1)], min_val=0, max_val=E - 1)
                    after(e, y_ready, s - 1)
                    for c in range(FC):
                        if c % 3 == 0:
                            e.wait_ge(silu_done, 2 * s + c // 3 + 1)
                        m = e.matmul(ps[:, 6 + tk % 2, 0:H], hT[:, tk % 2, c, :], w2[:, ds(ex_, 1), c, :].rearrange("p a n -> p (a n)"),
                                     start=c == 0, stop=c == FC - 1)
                    m.then_inc(y_done, 1)
            pipeline(e, DT // DU, DU, 4, step)

        def d_act(e):
            def step(i, k):
                if t := dtile(i, k, 3):
                    ti, tk, s = t
                    for hf in range(2):
                        e.wait_ge(hd_done, 2 * s + hf + 1)
                        after(e, y_done, s - 1)
                        e.activation(hT[:, tk % 2, 3 * hf:3 * hf + 3, :],
                                     ps[:, 1 + 2 * (tk % 2) + hf, 0:FH].rearrange("p (c n) -> p c n", c=3), ACT.Silu).then_inc(silu_done, 1)
                        if hf == 0 and (t2 := dtile(i, k, 2)):
                            dst, src = choose_w1(e, 1, t2[1], t2[2])
                            e.activation(dst, src, ACT.Copy).then_inc(w1_ready[1], 1)
                elif t2 := dtile(i, k, 2):
                    dst, src = choose_w1(e, 1, t2[1], t2[2])
                    e.activation(dst, src, ACT.Copy).then_inc(w1_ready[1], 1)
                if t := dtile(i, k, 2):
                    ti, tk, s = t
                    e.wait_ge(xd_done, s + 1)
                    after(e, hd_done, 2 * (s - 2) + 2)
                    e.activation(xgT[0:HC, tk % 2, :, :], ps[0:HC, 0, 0:2 * P].rearrange("p (k n) -> p k n", k=2),
                                 ACT.Copy).then_inc(xd_ready, 1)
            e.wait_ge(rexp, NB)
            e.preload_act_table_set("silu_and_others")
            e.wait_ge(plan_ready, 1)
            pipeline(e, DT // DU, DU, 3, step)

        def d_dve(e):
            e.wait_ge(plan_ready, 1)

            def step(i, k):
                if t := dtile(i, k, 0):
                    ti, tk, s = t
                    after(e, y_ready, s - DU + 1)
                    e.tensor_copy(idr[:, tk:tk + 1], idi[:, ds(s, 1)]).then_inc(idr_ready, 1)
                if t := dtile(i, k, 1):
                    ti, tk, s = t
                    e.wait_ge(egath[tk % 2], 16 * (DU // 2 * ti + tk // 2 + 1))
                    after(e, added, 16 * (s - DU + 1))
                    e.tensor_copy(toki[:, tk:tk + 1], eg[:, tk, 1:2]).then_inc(tok_ready, 1)
                if t := dtile(i, k, 2):
                    dst, src = choose_w1(e, 0, t[1], t[2])
                    e.tensor_copy(dst, src).then_inc(w1_ready[0], 1)
                if t := dtile(i, k, 4):
                    ti, tk, s = t
                    e.wait_ge(y_done, s + 1)
                    after(e, added, 16 * (s - 1))
                    e.tensor_scalar(Y[:, tk % 2, :], ps[:, 6 + tk % 2, 0:H], eg[:, tk, 0:1], None, ALU.mult).then_inc(y_ready, 1)
            pipeline(e, DT // DU, DU, 4, step)

        def d_pool(e):
            e.wait_ge(scat[0], 128 * (NB // 2))
            e.wait_ge(scat[1], 128 * (NB // 2))
            e.wait_ge(x_out[0], 16 * (NB // 2))
            e.wait_ge(x_out[1], 16 * (NB // 2))
            e.wait_ge(c_pad, 64)
            e.wait_ge(res_out, 16 * NB)

            def step(i, k):
                if t := dtile(i, k, 0):
                    ti, tk, s = t
                    e.wait_ge(idr_ready, s + 1)
                    gate(e)
                    after(e, y_ready, s - DU + 1)
                    gate(e)
                    e.indirect_dma_start(out=eg[:, tk, :], out_offset=None, in_=lists,
                                         in_offset=bass.IndirectOffsetOnAxis(ap=idr[:, tk:tk + 1], axis=0)).then_inc(egath[tk % 2], 16)
                if t := dtile(i, k, 1):
                    ti, tk, s = t
                    e.wait_ge(tok_ready, s + 1)
                    gate(e)
                    after(e, xd_done, s - DU + 1)
                    gate(e)
                    e.indirect_dma_start(out=XG[:, tk, :], out_offset=None, in_=xrows,
                                         in_offset=bass.IndirectOffsetOnAxis(ap=toki[:, tk:tk + 1], axis=0)).then_inc(gath[tk], 16)
                if t := dtile(i, k, 5):
                    ti, tk, s = t
                    e.wait_ge(y_ready, s + 1)
                    gate(e)
                    after(e, added, 16 * s)
                    gate(e)
                    e.indirect_dma_start(out=out_ext, out_offset=bass.IndirectOffsetOnAxis(ap=toki[:, tk:tk + 1], axis=0),
                                         in_=Y[:, tk % 2, :], in_offset=None, compute_op=ALU.add).then_inc(added, 16)
            pipeline(e, DT // DU, DU, 5, step)
            e.wait_ge(added, 16 * DT)

        block = ctx.enter_context(nc.Block())

        @block.sync
        def _(e):
            a_sync(e)
            b_sync(e)
            c_sync(e)

        @block.gpsimd
        def _(e):
            a_pool(e)
            b_pool(e)
            d_pool(e)

        @block.tensor
        def _(e):
            a_pe(e)
            b_pe(e)
            d_pe(e)

        @block.scalar
        def _(e):
            a_act(e)
            b_act(e)
            d_act(e)

        @block.vector
        def _(e):
            a_dve(e)
            b_dve(e)
            make_plan(e)
            d_dve(e)


def host_arrays(I):
    import numpy as np
    A = {k: np.asarray(v) for k, v in I.items()}
    names = ("promoter", "co_exp", "gene_family", "peca_grn")
    c = np.ascontiguousarray
    f = np.float32
    t = "L0_tok_"
    r = {}
    r["ids"] = c(A["x"].reshape(NT, P, 1))
    r["vals"] = c(A["fside_BS_values"].reshape(NT, P, 1))
    r["homo"] = c(A[t + "homologous_index"].reshape(-1, 1))
    r["word"] = c(A[t + "word_emb"])
    r["tabs"] = np.concatenate([A[t + n + "_k"] for n in names], axis=1)
    r["wkT"] = c(np.stack([A[t + n + "_W"].T.reshape(2, HC, DK) for n in names]).transpose(2, 1, 0, 3))
    r["bk"] = c(np.stack([A[t + n + "_b"].reshape(2, HC) for n in names]).transpose(2, 1, 0))
    r["fc_w"] = c(A[t + "cat_fc_W"])
    r["fc_b"] = c(A[t + "cat_fc_b"].reshape(1, H))
    r["pj"] = np.concatenate([A[t + "cat_proj_W"], A[t + "cat_proj_b"].reshape(1, H), A[t + "tok_type_emb"][0:1]], axis=0)
    r["pos"] = c(A[t + "pos_emb"])
    vec = np.stack([A[t + "cat_ln_g"], A[t + "cat_ln_b"], A[t + "ln_g"], A[t + "ln_b"], A["L0_ffn_ln_gamma"], A["L0_ffn_ln_beta"]])
    r["lnp"] = c(np.broadcast_to(vec[None], (P, 6, H)))
    r["qkv"] = np.concatenate([A["L0_attn_qkv_weight"].T, A["L0_attn_qkv_bias"].reshape(1, -1)], axis=0)
    wo = np.zeros((P, NG, H), f)
    pw = A["L0_attn_proj_weight"].T
    for h in range(NH):
        wo[32 * (h % HG):32 * (h % HG) + HD, h // HG] = pw[HD * h:HD * h + HD]
    wo[HD, 0] = A["L0_attn_proj_bias"]
    r["wo"] = wo
    r["router"] = c(A["L0_ffn_router_w"])
    r["w1"] = c(A["L0_ffn_w1"].reshape(E, 2, HC, FF).transpose(2, 0, 1, 3))
    r["w2"] = c(A["L0_ffn_w2"].reshape(E, FC, P, H).transpose(2, 0, 1, 3))
    k = np.zeros((P, C_END), f)
    k[:, C_ID:C_ID + P] = np.eye(P)
    k[:, C_TRI:C_TRI + P] = np.triu(np.ones((P, P)), 1)
    k[:, C_ONE:C_ONE + P] = 1
    k[:, C_LOW:C_LOW + E * E] = np.tril(np.ones((E, E)), -1).reshape(1, -1)
    k[:, C_CAP:C_CAP + E] = CAP * np.arange(E)
    k[:, C_F:C_F + DT] = P * np.arange(DT)[None] + np.arange(P)[:, None]
    k[:, C_PAD] = E * CAP + np.arange(P)
    k[:, C_TOK:C_TOK + NT] = P * np.arange(NT)[None] + np.arange(P)[:, None]
    k[:, C_PADTOK] = NB * S + np.arange(P)
    r["const"] = k
    return r


def kernel(**inputs):
    import numpy as np
    import concourse.bacc as bacc
    from concourse.bass_utils import run_bass_kernel_spmd

    nc = bacc.Bacc("TRN2", target_bir_lowering=False, num_devices=1)
    arrays = {f"in_{n}": v for n, v in host_arrays(inputs).items()}
    aps = {n[3:]: nc.dram_tensor(n, v.shape, mybir.dt.from_np(v.dtype), kind="ExternalInput").ap() for n, v in arrays.items()}
    out = nc.dram_tensor("out_0", [NB * S + P, H], F32, kind="ExternalOutput").ap()
    build_program(nc, aps, out)
    got = run_bass_kernel_spmd(nc, [arrays], core_ids=[0]).results[0]["out_0"]
    return np.asarray(got)[0:NB * S].reshape(NB, S, H)
```
